# Optimizing a Trainium2 kernel written in Bass

```python
import numpy as np
import jax
import jax.numpy as jnp

def _softmax(x, axis=-1):
    return jax.nn.softmax(x, axis=axis)

def _gelu(x):
    return jax.nn.gelu(x, approximate=True)

def _silu(x):
    return jax.nn.silu(x)

def _sigmoid(x):
    return jax.nn.sigmoid(x)

def _layernorm(x, axis=-1, eps=1e-05):
    m = jnp.mean(x, axis=axis, keepdims=True)
    v = jnp.var(x, axis=axis, keepdims=True)
    return (x - m) / jnp.sqrt(v + eps)

def _scatter_add(tgt, idx, src, axis=0):
    return tgt.at[idx].add(src)

def _segment_sum(src, seg, n):
    return jax.ops.segment_sum(src, seg, n)
kernel_name = 'mk_gnn_ffn_d2_gnn_r16_cf9c41'

def setup_inputs(seed: int=0):
    np.random.seed(seed)
    _w = jnp.asarray

    def _rec_inputs():
        import jax
        import jax.numpy as jnp
        _gk = jax.random.key(seed)
        x = -0.000364 + 1 * jax.random.normal(jax.random.fold_in(_gk, 1), (625, 768), jnp.float32)
        src = jax.random.randint(jax.random.fold_in(_gk, 2), (10000,), 0, 625, jnp.int32)
        dst = jax.random.randint(jax.random.fold_in(_gk, 3), (10000,), 0, 625, jnp.int32)
        _o = jnp.argsort(dst, stable=True)
        src = src[_o]
        dst = dst[_o]
        edge_type_34 = jax.random.randint(jax.random.fold_in(_gk, 12), (10000,), 0, 34, jnp.int32)
        return (x, src, dst, edge_type_34)
    x, src, dst, edge_type_34 = _rec_inputs()

    def _L0_gnn_setup():
        import jax, jax.numpy as jnp
        import numpy as np
        N = 1250
        E_RAND = 20000
        NEG_SLOPE = 0.2

        def gat_layer(x, W, a_src, a_dst, bias, src, dst, heads, out_c, concat):
            n = x.shape[0]
            h = (x @ W).reshape(n, heads, out_c)
            al_s = jnp.einsum('nhc,hc->nh', h, a_src)
            al_d = jnp.einsum('nhc,hc->nh', h, a_dst)
            e = jax.nn.leaky_relu(al_s[src] + al_d[dst], NEG_SLOPE)
            m = jax.ops.segment_max(e, dst, num_segments=n)
            ex = jnp.exp(e - m[dst])
            z = jax.ops.segment_sum(ex, dst, num_segments=n)
            alpha = ex / (z[dst] + 1e-16)
            msg = h[src] * alpha[:, :, None]
            out = jax.ops.segment_sum(msg, dst, num_segments=n)
            out = out.reshape(n, heads * out_c) if concat else out.mean(axis=1)
            return out + bias
        key = jax.random.key(seed)
        ks = jax.random.split(key, 10)
        x = jax.random.normal(ks[0], (N, 768), dtype=jnp.float32)
        src = jax.random.randint(ks[1], (E_RAND,), 0, N)
        dst = jax.random.randint(ks[2], (E_RAND,), 0, N)
        loop = jnp.arange(N)
        edge_index = jnp.stack([jnp.concatenate([src, loop]), jnp.concatenate([dst, loop])])
        s = 1.0 / np.sqrt(768.0)
        W1 = jax.random.normal(ks[3], (768, 768), dtype=jnp.float32) * s
        a_src1 = jax.random.normal(ks[4], (8, 96), dtype=jnp.float32) * 0.1
        a_dst1 = jax.random.normal(ks[5], (8, 96), dtype=jnp.float32) * 0.1
        b1 = jnp.zeros((768,), dtype=jnp.float32)
        W2 = jax.random.normal(ks[6], (768, 768), dtype=jnp.float32) * s
        a_src2 = jax.random.normal(ks[7], (1, 768), dtype=jnp.float32) * 0.1
        a_dst2 = jax.random.normal(ks[8], (1, 768), dtype=jnp.float32) * 0.1
        b2 = jnp.zeros((768,), dtype=jnp.float32)
        return {'x': x, 'edge_index': edge_index, 'W1': W1, 'a_src1': a_src1, 'a_dst1': a_dst1, 'b1': b1, 'W2': W2, 'a_src2': a_src2, 'a_dst2': a_dst2, 'b2': b2}
    _L0_gnn_all = _L0_gnn_setup()
    _L0_gnn_in = {k: v for k, v in _L0_gnn_all.items() if k in ('W1', 'a_src1', 'a_dst1', 'b1', 'W2', 'a_src2', 'a_dst2', 'b2')}
    del _L0_gnn_all

    def _L0_ffn_setup():
        import jax, jax.numpy as jnp
        import numpy as np
        B, N, D, E, F, K = (2, 128, 768, 8, 192, 2)
        V_MAX = 3.0
        FEAT_CLAMP = 10.0

        def bk_green_diag(a):
            aT = jnp.swapaxes(a, 0, 1)

            def step(c, ai):
                d = ai - 1.0 / c
                return (d, d)
            d0 = aT[0]
            _, d_rest = jax.lax.scan(step, d0, aT[1:])
            d = jnp.concatenate([d0[None], d_rest], axis=0)
            eN = aT[-1]
            _, e_rest = jax.lax.scan(step, eN, aT[:-1], reverse=True)
            e = jnp.concatenate([e_rest, eN[None]], axis=0)
            G = 1.0 / (d + e - aT)
            return jnp.swapaxes(G, 0, 1)
        key = jax.random.key(seed)
        ks = jax.random.split(key, 8)
        s = lambda k, shape, sc: jax.random.normal(k, shape, jnp.float32) * sc
        return {'x': s(ks[0], (B, N, D), 1.0), 'v_w': s(ks[1], (D,), 0.02), 'v_b': jnp.zeros((), jnp.float32), 'gate_w': s(ks[2], (D, E), 0.02), 'gate_b': jnp.zeros((E,), jnp.float32), 'w1': s(ks[3], (E, D, F), 0.02), 'b1': jnp.zeros((E, F), jnp.float32), 'w2': s(ks[4], (E, F, D), 0.02), 'b2': jnp.zeros((E, D), jnp.float32), 'out_w': s(ks[5], (2, D), 0.02), 'out_b': jnp.zeros((D,), jnp.float32), 'bk_scale': jnp.ones((D,), jnp.float32)}
    _L0_ffn_all = _L0_ffn_setup()
    _L0_ffn_in = {k: v for k, v in _L0_ffn_all.items() if k in ('v_w', 'v_b', 'gate_w', 'gate_b', 'w1', 'b1', 'w2', 'b2', 'out_w', 'out_b', 'bk_scale')}
    del _L0_ffn_all

    def _L1_gnn_setup():
        import jax, jax.numpy as jnp
        import numpy as np
        N_NODES = 625
        N_EDGES = 6250
        N_REL = 34
        DIM = 768

        def _graph_encoder(x, edge_index, edge_type, W_rel, W_root, b_rgcn, W_gcn, b_gcn):
            n = x.shape[0]
            src, dst = (edge_index[0], edge_index[1])
            ones = jnp.ones((src.shape[0],), dtype=x.dtype)
            seg = edge_type * n + dst
            agg = jax.ops.segment_sum(x[src], seg, num_segments=N_REL * n)
            cnt = jax.ops.segment_sum(ones, seg, num_segments=N_REL * n)
            mean = agg.reshape(N_REL, n, -1) / jnp.maximum(cnt, 1.0).reshape(N_REL, n, 1)
            h1 = jnp.einsum('rni,rio->no', mean, W_rel) + x @ W_root + b_rgcn
            xw = h1 @ W_gcn
            deg = jax.ops.segment_sum(ones, dst, num_segments=n) + 1.0
            dinv = jax.lax.rsqrt(deg)
            norm = dinv[src] * dinv[dst]
            out = jax.ops.segment_sum(xw[src] * norm[:, None], dst, num_segments=n)
            out = out + xw * (dinv * dinv)[:, None]
            return out + b_gcn
        key = jax.random.key(seed)
        ks = jax.random.split(key, 6)
        scale = 1.0 / np.sqrt(DIM)
        x = jax.random.normal(ks[0], (N_NODES, DIM), dtype=jnp.float32)
        edge_index = jax.random.randint(ks[1], (2, N_EDGES), 0, N_NODES, dtype=jnp.int32)
        edge_type = jax.random.randint(ks[2], (N_EDGES,), 0, N_REL, dtype=jnp.int32)
        W_rel = jax.random.normal(ks[3], (N_REL, DIM, DIM), dtype=jnp.float32) * scale
        W_root = jax.random.normal(ks[4], (DIM, DIM), dtype=jnp.float32) * scale
        b_rgcn = jnp.zeros((DIM,), dtype=jnp.float32)
        W_gcn = jax.random.normal(ks[5], (DIM, DIM), dtype=jnp.float32) * scale
        b_gcn = jnp.zeros((DIM,), dtype=jnp.float32)
        return {'x': x, 'edge_index': edge_index, 'edge_type': edge_type, 'W_rel': W_rel, 'W_root': W_root, 'b_rgcn': b_rgcn, 'W_gcn': W_gcn, 'b_gcn': b_gcn}
    _L1_gnn_all = _L1_gnn_setup()
    _L1_gnn_in = {k: v for k, v in _L1_gnn_all.items() if k in ('W_rel', 'W_root', 'b_rgcn', 'W_gcn', 'b_gcn')}
    del _L1_gnn_all

    def _L1_ffn_setup():
        import math
        import jax, jax.numpy as jnp
        import numpy as np
        NUM_EXPERTS = 8
        TOP_K = 2
        CAPACITY_FACTOR = 1.25
        H = 768
        INNER = 192
        B, S = (2, 128)
        key = jax.random.key(seed)
        ks = jax.random.split(key, 9)
        scale = 0.02
        x = jax.random.normal(ks[0], (B, S, H), dtype=jnp.float32)
        Wr = jax.random.normal(ks[1], (H, NUM_EXPERTS), dtype=jnp.float32) * scale
        w1 = jax.random.normal(ks[2], (NUM_EXPERTS, H, INNER), dtype=jnp.float32) * scale
        w3 = jax.random.normal(ks[3], (NUM_EXPERTS, H, INNER), dtype=jnp.float32) * scale
        w2 = jax.random.normal(ks[4], (NUM_EXPERTS, INNER, H), dtype=jnp.float32) * scale
        s1 = jax.random.normal(ks[5], (H, INNER), dtype=jnp.float32) * scale
        s3 = jax.random.normal(ks[6], (H, INNER), dtype=jnp.float32) * scale
        s2 = jax.random.normal(ks[7], (INNER, H), dtype=jnp.float32) * scale
        return {'x': x, 'Wr': Wr, 'w1': w1, 'w3': w3, 'w2': w2, 's1': s1, 's3': s3, 's2': s2}
    _L1_ffn_all = _L1_ffn_setup()
    _L1_ffn_in = {k: v for k, v in _L1_ffn_all.items() if k in ('Wr', 'w1', 'w3', 'w2', 's1', 's3', 's2')}
    del _L1_ffn_all
    return {'x': x, 'src': src, 'dst': dst, 'edge_type_34': edge_type_34, 'L0_gnn_W1': _L0_gnn_in['W1'], 'L0_gnn_a_src1': _L0_gnn_in['a_src1'], 'L0_gnn_a_dst1': _L0_gnn_in['a_dst1'], 'L0_gnn_b1': _L0_gnn_in['b1'], 'L0_gnn_W2': _L0_gnn_in['W2'], 'L0_gnn_a_src2': _L0_gnn_in['a_src2'], 'L0_gnn_a_dst2': _L0_gnn_in['a_dst2'], 'L0_gnn_b2': _L0_gnn_in['b2'], 'L0_ffn_v_w': _L0_ffn_in['v_w'], 'L0_ffn_v_b': _L0_ffn_in['v_b'], 'L0_ffn_gate_w': _L0_ffn_in['gate_w'], 'L0_ffn_gate_b': _L0_ffn_in['gate_b'], 'L0_ffn_w1': _L0_ffn_in['w1'], 'L0_ffn_b1': _L0_ffn_in['b1'], 'L0_ffn_w2': _L0_ffn_in['w2'], 'L0_ffn_b2': _L0_ffn_in['b2'], 'L0_ffn_out_w': _L0_ffn_in['out_w'], 'L0_ffn_out_b': _L0_ffn_in['out_b'], 'L0_ffn_bk_scale': _L0_ffn_in['bk_scale'], 'L1_gnn_W_rel': _L1_gnn_in['W_rel'], 'L1_gnn_W_root': _L1_gnn_in['W_root'], 'L1_gnn_b_rgcn': _L1_gnn_in['b_rgcn'], 'L1_gnn_W_gcn': _L1_gnn_in['W_gcn'], 'L1_gnn_b_gcn': _L1_gnn_in['b_gcn'], 'L1_ffn_Wr': _L1_ffn_in['Wr'], 'L1_ffn_w1': _L1_ffn_in['w1'], 'L1_ffn_w3': _L1_ffn_in['w3'], 'L1_ffn_w2': _L1_ffn_in['w2'], 'L1_ffn_s1': _L1_ffn_in['s1'], 'L1_ffn_s3': _L1_ffn_in['s3'], 'L1_ffn_s2': _L1_ffn_in['s2']}

def reference(x, src, dst, edge_type_34, L0_gnn_W1, L0_gnn_a_src1, L0_gnn_a_dst1, L0_gnn_b1, L0_gnn_W2, L0_gnn_a_src2, L0_gnn_a_dst2, L0_gnn_b2, L0_ffn_v_w, L0_ffn_v_b, L0_ffn_gate_w, L0_ffn_gate_b, L0_ffn_w1, L0_ffn_b1, L0_ffn_w2, L0_ffn_b2, L0_ffn_out_w, L0_ffn_out_b, L0_ffn_bk_scale, L1_gnn_W_rel, L1_gnn_W_root, L1_gnn_b_rgcn, L1_gnn_W_gcn, L1_gnn_b_gcn, L1_ffn_Wr, L1_ffn_w1, L1_ffn_w3, L1_ffn_w2, L1_ffn_s1, L1_ffn_s3, L1_ffn_s2):
    import jax
    import jax.numpy as jnp

    def _L0_gnn_ref(x, edge_index, W1, a_src1, a_dst1, b1, W2, a_src2, a_dst2, b2):
        import jax, jax.numpy as jnp
        import numpy as np
        N = 1250
        E_RAND = 20000
        NEG_SLOPE = 0.2

        def gat_layer(x, W, a_src, a_dst, bias, src, dst, heads, out_c, concat):
            n = x.shape[0]
            h = (x @ W).reshape(n, heads, out_c)
            al_s = jnp.einsum('nhc,hc->nh', h, a_src)
            al_d = jnp.einsum('nhc,hc->nh', h, a_dst)
            e = jax.nn.leaky_relu(al_s[src] + al_d[dst], NEG_SLOPE)
            m = jax.ops.segment_max(e, dst, num_segments=n)
            ex = jnp.exp(e - m[dst])
            z = jax.ops.segment_sum(ex, dst, num_segments=n)
            alpha = ex / (z[dst] + 1e-16)
            msg = h[src] * alpha[:, :, None]
            out = jax.ops.segment_sum(msg, dst, num_segments=n)
            out = out.reshape(n, heads * out_c) if concat else out.mean(axis=1)
            return out + bias
        src, dst = (edge_index[0], edge_index[1])
        h = gat_layer(x, W1, a_src1, a_dst1, b1, src, dst, heads=8, out_c=96, concat=True)
        h = jax.nn.elu(h)
        out = gat_layer(h, W2, a_src2, a_dst2, b2, src, dst, heads=1, out_c=768, concat=False)
        return out

    def _L0_ffn_ref(x, v_w, v_b, gate_w, gate_b, w1, b1, w2, b2, out_w, out_b, bk_scale):
        import jax, jax.numpy as jnp
        import numpy as np
        B, N, D, E, F, K = (2, 128, 768, 8, 192, 2)
        V_MAX = 3.0
        FEAT_CLAMP = 10.0

        def bk_green_diag(a):
            aT = jnp.swapaxes(a, 0, 1)

            def step(c, ai):
                d = ai - 1.0 / c
                return (d, d)
            d0 = aT[0]
            _, d_rest = jax.lax.scan(step, d0, aT[1:])
            d = jnp.concatenate([d0[None], d_rest], axis=0)
            eN = aT[-1]
            _, e_rest = jax.lax.scan(step, eN, aT[:-1], reverse=True)
            e = jnp.concatenate([e_rest, eN[None]], axis=0)
            G = 1.0 / (d + e - aT)
            return jnp.swapaxes(G, 0, 1)
        v = jnp.clip(x @ v_w + v_b, -V_MAX, V_MAX)
        a = (-2.0 + v).astype(jnp.complex64) - 1j
        G = bk_green_diag(a)
        feats = jnp.stack([G.real, G.imag], axis=-1)
        logits = x @ gate_w + gate_b
        probs = jax.nn.softmax(logits, axis=-1)
        topv, topi = jax.lax.top_k(probs, K)
        topv = topv / jnp.sum(topv, axis=-1, keepdims=True)
        comb = jnp.sum(topv[..., None] * jax.nn.one_hot(topi, E, dtype=x.dtype), axis=2)
        h = jax.nn.gelu(jnp.einsum('bnd,edf->bnef', x, w1) + b1)
        y = jnp.einsum('bnef,efd->bned', h, w2) + b2
        ffn_out = jnp.einsum('bne,bned->bnd', comb, y)
        feats_c = jnp.clip(feats, -FEAT_CLAMP, FEAT_CLAMP)
        spec_out = feats_c @ out_w + out_b
        return ffn_out + bk_scale * spec_out

    def _L1_gnn_ref(x, edge_index, edge_type, W_rel, W_root, b_rgcn, W_gcn, b_gcn):
        import jax, jax.numpy as jnp
        import numpy as np
        N_NODES = 625
        N_EDGES = 6250
        N_REL = 34
        DIM = 768

        def _graph_encoder(x, edge_index, edge_type, W_rel, W_root, b_rgcn, W_gcn, b_gcn):
            n = x.shape[0]
            src, dst = (edge_index[0], edge_index[1])
            ones = jnp.ones((src.shape[0],), dtype=x.dtype)
            seg = edge_type * n + dst
            agg = jax.ops.segment_sum(x[src], seg, num_segments=N_REL * n)
            cnt = jax.ops.segment_sum(ones, seg, num_segments=N_REL * n)
            mean = agg.reshape(N_REL, n, -1) / jnp.maximum(cnt, 1.0).reshape(N_REL, n, 1)
            h1 = jnp.einsum('rni,rio->no', mean, W_rel) + x @ W_root + b_rgcn
            xw = h1 @ W_gcn
            deg = jax.ops.segment_sum(ones, dst, num_segments=n) + 1.0
            dinv = jax.lax.rsqrt(deg)
            norm = dinv[src] * dinv[dst]
            out = jax.ops.segment_sum(xw[src] * norm[:, None], dst, num_segments=n)
            out = out + xw * (dinv * dinv)[:, None]
            return out + b_gcn
        return _graph_encoder(x, edge_index, edge_type, W_rel, W_root, b_rgcn, W_gcn, b_gcn)

    def _L1_ffn_ref(x, Wr, w1, w3, w2, s1, s3, s2):
        import math
        import jax, jax.numpy as jnp
        import numpy as np
        NUM_EXPERTS = 8
        TOP_K = 2
        CAPACITY_FACTOR = 1.25
        H = 768
        INNER = 192
        B, S = (2, 128)
        b, s, h = x.shape
        n = b * s
        flat = x.reshape(n, h)
        logits = flat @ Wr
        probs = jax.nn.softmax(logits, axis=-1)
        topk_p, topk_i = jax.lax.top_k(probs, TOP_K)
        topk_p = topk_p / jnp.clip(topk_p.sum(-1, keepdims=True), 1e-09)
        capacity = max(1, math.ceil(n * TOP_K / NUM_EXPERTS * CAPACITY_FACTOR))
        onehot = topk_i[None, :, :] == jnp.arange(NUM_EXPERTS)[:, None, None]
        w_tok = jnp.sum(topk_p[None] * onehot, axis=-1)
        assigned = jnp.any(onehot, axis=-1)
        score = jnp.where(assigned, w_tok, -jnp.inf)
        order = jnp.argsort(-score, axis=1)[:, :capacity]
        score_sel = jnp.take_along_axis(score, order, axis=1)
        valid = jnp.isfinite(score_sel)
        weight_sel = jnp.where(valid, score_sel, 0.0)
        dispatch = flat[order]
        gate = jax.nn.silu(jnp.einsum('ech,ehi->eci', dispatch, w1))
        up = jnp.einsum('ech,ehi->eci', dispatch, w3)
        expert_out = jnp.einsum('eci,eih->ech', gate * up, w2)
        expert_out = expert_out * weight_sel[..., None]
        routed = jnp.zeros((n, h), dtype=flat.dtype)
        routed = routed.at[order.reshape(-1)].add(expert_out.reshape(-1, h))
        shared = jax.nn.silu(flat @ s1) * (flat @ s3) @ s2
        out = routed + shared
        return out.reshape(b, s, h)
    edge_index = jnp.stack([src, dst])
    x = x + _L0_gnn_ref(_layernorm(x, axis=-1), edge_index, L0_gnn_W1, L0_gnn_a_src1, L0_gnn_a_dst1, L0_gnn_b1, L0_gnn_W2, L0_gnn_a_src2, L0_gnn_a_dst2, L0_gnn_b2)
    x = x + _L0_ffn_ref(_layernorm(x, axis=-1)[None], L0_ffn_v_w, L0_ffn_v_b, L0_ffn_gate_w, L0_ffn_gate_b, L0_ffn_w1, L0_ffn_b1, L0_ffn_w2, L0_ffn_b2, L0_ffn_out_w, L0_ffn_out_b, L0_ffn_bk_scale)[0]
    x = x + _L1_gnn_ref(_layernorm(x, axis=-1), edge_index, edge_type_34, L1_gnn_W_rel, L1_gnn_W_root, L1_gnn_b_rgcn, L1_gnn_W_gcn, L1_gnn_b_gcn)
    x = x + _L1_ffn_ref(_layernorm(x, axis=-1)[None], L1_ffn_Wr, L1_ffn_w1, L1_ffn_w3, L1_ffn_w2, L1_ffn_s1, L1_ffn_s3, L1_ffn_s2)[0]
    return x

_drawn_inputs = setup_inputs


def setup_inputs(seed=0):
    import zlib

    import numpy as np

    out = dict(_drawn_inputs(seed))
    spreads = {'L0_gnn_b1': (0.0, 0.1),
     'L0_gnn_b2': (0.0, 0.1),
     'L0_ffn_gate_b': (0.0, 0.1),
     'L0_ffn_b1': (0.0, 0.579),
     'L0_ffn_b2': (0.0, 0.1),
     'L0_ffn_out_b': (0.0, 0.1),
     'L0_ffn_bk_scale': (1.0, 0.2),
     'L1_gnn_b_rgcn': (0.0, 0.1),
     'L1_gnn_b_gcn': (0.0, 0.1)}
    factors = {'L0_gnn_a_dst2': 3.122, 'L0_ffn_v_w': 8.0, 'L0_ffn_out_w': 3.204, 'L1_ffn_Wr': 2.757}
    for name, (base, spread) in spreads.items():
        noise = np.random.default_rng([zlib.crc32(name.encode()), seed]).standard_normal(out[name].shape)
        drawn = base * np.exp(spread * noise) if base else spread * noise
        out[name] = jnp.asarray(drawn.astype(out[name].dtype))
    for name, factor in factors.items():
        out[name] = (out[name] * factor).astype(out[name].dtype)
    return out
```

```python
import concourse.bass as bass
from concourse import mybir
from contextlib import ExitStack, contextmanager

N, D = 625, 768
P = 125
T = N // P
K = D // 128
EDGES = 10000
EP = 125
ET = EDGES // EP
REL = 34
HEADS, HC = 8, D // 8
NE, F = 8, 192
FF = NE * F
FK = FF // 128
CAP = 196
BC = 25
HALF = D // 2
BANK = 512
EPS = 1e-5

STAGES = [
    ("edges", [1, 1, 1, 1]), ("mask", [2, 1, 1, 1]),
    ("turn1", [2, 2, 1, 1]), ("w1", [2, 1, 1, 1]), ("heads1", [HEADS] * 4),
    ("turn2", [2, 2, 1, 1]), ("w2", [2, 1, 1, 1]), ("heads2", [3, 1, 1, 3]),
    ("turn3", [2, 2, 1, 1]), ("route1", [1, 1, 1, 0]), ("inner1", [6, 6, 6, 6]), ("outer1", [2, 1, 1, 1]),
    ("turn4", [2, 2, 1, 1]), ("relations", [3 * REL // 2, 3 * REL // 2, 2 * REL // 2, 2 * REL // 2]),
    ("messages", [1, 1, 1, 1]), ("turn5", [2, 2, 1, 1]), ("wgcn", [2, 1, 1, 1]), ("gcn", [2, 1, 1, 1]),
    ("turn6", [2, 2, 1, 1]), ("route2", [1, 0, 0, 0]), ("ranks", [2, 2, 2, 2]),
    ("inner2", [12, 12, 12, 0]), ("shared", [2, 2, 0, 0]), ("outer2", [2, 1, 1, 1]),
]
BEFORE, _n = {}, [0, 0, 0, 0]
for _name, _jobs in STAGES:
    BEFORE[_name] = list(_n)
    _n = [a + b for a, b in zip(_n, _jobs)]


class Track:

    def __init__(self, eng, own):
        self.eng, self.own, self.n, self.extra = eng, own, 0, None

    def __call__(self, ins):
        ins.then_inc(self.own, 1)
        self.n += 1
        return ins

    def sync(self):
        self.eng.wait_ge(self.own, self.n if self.extra is None else self.n + self.extra)

    def do(self, ins):
        self(ins)
        self.sync()

    @contextmanager
    def turns(self, n, signals):
        start = self.n
        with self.eng.Fori(0, n) as i:
            self.extra = i * signals
            yield i
        assert self.n - start == signals, (self.n - start, signals)
        self.extra = None
        self.n = start + signals * n


def build(nc, x, src, dst, etype, w):
    f32, f32r, bf16 = mybir.dt.float32, mybir.dt.float32r, mybir.dt.bfloat16
    i32, u32, i16 = mybir.dt.int32, mybir.dt.uint32, mybir.dt.int16
    ALU, ACT, AX = mybir.AluOpType, mybir.ActivationFunctionType, mybir.AxisListType

    out = w["out"]
    z_dram = nc.dram_tensor("z_dram", [REL * N, D], f32).ap()
    inv_dram = nc.dram_tensor("inv_dram", [REL * N, 1], f32).ap()
    v_dram = nc.dram_tensor("v_dram", [N], f32).ap()
    mat_dram = nc.dram_tensor("mat_dram", [BC, 16], f32).ap()
    rho_dram = nc.dram_tensor("rho_dram", [BC, 4], f32).ap()
    green_dram = nc.dram_tensor("green_dram", [2, N], f32).ap()

    ctx = ExitStack()
    with ctx:
        def sb(name, shape, dt=f32, where=ctx):
            return where.enter_context(nc.sbuf_tensor(name, shape, dt))

        def sem(name):
            return ctx.enter_context(nc.semaphore(name))

        x_res = sb("x_res", [P, T, D])
        xn = sb("xn", [P, T, D])
        xT = sb("xT", [128, K, N])
        cnt = sb("cnt", [P, T, N])
        ident = sb("ident", [128, 128])
        ones = sb("ones", [128, 128])
        stats = sb("stats", [P, T, 2, 6])
        mv = sb("mv", [P, T, 2])
        rstd = sb("rstd", [P, T])
        small = sb("small", [P, 12, T, NE])
        rev = sb("rev", [P, NE])
        asg = sb("asg", [P, T, NE])
        comb1 = sb("comb1", [P, T, NE])
        t5 = sb("t5", [P, 8, T])
        dinv = sb("dinv", [P, T])
        evw = sb("evw", [EP, ET])
        dstf = sb("dstf", [EP, ET])
        zidx = sb("zidx", [EP, ET], u32)
        iota16 = sb("iota16", [P, N], i16)
        gate_sb = sb("gate_sb", [128, K, NE + 1])
        wr_sb = sb("wr_sb", [128, K, NE])
        gate_b = sb("gate_b", [P, NE])
        scol = [sb(f"scol{b}", [P, T]) for b in range(2)]
        v_b = sb("v_b", [P, 1])
        PS = ctx.enter_context(nc.psum_tensor("PS", [128, 8 * BANK], f32))

        def slot(q):
            return PS[:, q * 2 * BANK:(q + 1) * 2 * BANK]

        full = [sem(f"slot{q}_full") for q in range(4)]
        free = [sem(f"slot{q}_free") for q in range(4)]
        act_step, dve_step, pool_step = sem("act_step"), sem("dve_step"), sem("pool_step")
        consts_ready = sem("consts_ready")
        ld_edges, ld_x, ld_gate, ld_rows = sem("ld_edges"), sem("ld_x"), sem("ld_gate"), sem("ld_rows")
        ld_w1, ld_w2 = sem("ld_w1"), sem("ld_w2")
        onehots_ready, onehots_used = sem("onehots_ready"), sem("onehots_used")
        cnt_ready, inv_ready, inv_stored = sem("cnt_ready"), sem("inv_ready"), sem("inv_stored")
        cidx_ready, evw_loaded, evw_ready = sem("cidx_ready"), sem("evw_loaded"), sem("evw_ready")
        idx_used = sem("idx_used")
        var_ready, std_ready, xn_ready, xT_ready = sem("var_ready"), sem("std_ready"), sem("xn_ready"), sem("xT_ready")
        h_ready, cols_ready, r_ready = sem("h_ready"), sem("cols_ready"), sem("r_ready")
        exps_ready, probs_ready, probs_free = sem("exps_ready"), sem("probs_ready"), sem("probs_free")
        elu_in, elu_exp = sem("elu_in"), sem("elu_exp")
        logits_in, logits_exp = sem("logits_in"), sem("logits_exp")
        deg_ready, deg_sqrt = sem("deg_ready"), sem("deg_sqrt")
        comb_ready, combw_ready = sem("comb_ready"), sem("combw_ready")
        act_done, inner_done = sem("act_done"), sem("inner_done")
        ld_f1, ld_f2 = [sem("ld_f1a"), sem("ld_f1b")], sem("ld_f2")
        ld_small = sem("ld_small")
        v_out, v_in, mat_out, mat_in = sem("v_out"), sem("v_in"), sem("mat_out"), sem("mat_in")
        rho_out, rho_in, green_out, green_in = sem("rho_out"), sem("rho_in"), sem("green_out"), sem("green_in")
        v_ready, mat_ready, rho_ready, green_ready = sem("v_ready"), sem("mat_ready"), sem("rho_ready"), sem("green_ready")
        specw_ready, layer_done = sem("specw_ready"), sem("layer_done")
        split_hi, split_lo = sem("split_hi"), sem("split_lo")
        raw_loaded = [sem("raw_loaded0"), sem("raw_loaded1")]
        xsplit_ready = sem("xsplit_ready")
        z_stored = [sem(f"z_stored{t}") for t in range(T)]
        gathered = [sem(f"gathered{b}") for b in range(4)]
        msg_hi, msg_ready, msg_used, hot_ready = sem("msg_hi"), sem("msg_ready"), sem("msg_used"), sem("hot_ready")
        ld_root, ld_gcn = sem("ld_root"), sem("ld_gcn")
        h1_ready, xw_ready, xws_ready = sem("h1_ready"), sem("xw_ready"), sem("xws_ready")
        earlier_ready = sem("earlier_ready")
        gathers_begun, maxima_begun = sem("gathers_begun"), sem("maxima_begun")
        out_stored = sem("out_stored")

        g = ExitStack()
        with g:
            negm = sb("negm", [P, T, N], f32, g)
            hx = sb("hx", [P, T, D + HEADS], f32, g)
            e1 = [sb(f"e1_{b}", [P, T, N], f32, g) for b in range(2)]
            e2 = sb("e2", [P, T, N], f32, g)
            gw = [sb(f"gw{b}", [128, K, D], f32, g) for b in range(2)]
            arow = sb("arow", [P, 4, D], f32, g)
            brow = sb("brow", [P, 2, D], f32, g)
            tmp = sb("tmp", [P, D], f32, g)
            al = sb("al", [P, T, 2, HEADS], f32, g)
            hcol = sb("hcol", [P, T, 2], f32, g)
            rcol = sb("rcol", [P, T, 2], f32, g)
            smax = sb("smax", [P, 4, T], f32, g)
            iota34 = sb("iota34", [EP, REL], i16, g)
            eint = sb("eint", [EP, 3, ET], i32, g)
            ef = sb("ef", [EP, 3, ET], f32, g)
            cidx = sb("cidx", [EP, ET], u32, g)
            idxb = sb("idxb", [EP, 1], u32, g)
            evwb = sb("evwb", [EP, 1], f32, g)
            hot_s = [sb(f"hot_s{b}", [EP, N], bf16, g) for b in range(2)]
            hot_d = [sb(f"hot_d{b}", [EP, N], bf16, g) for b in range(2)]
            hot_r = [sb(f"hot_r{b}", [EP, REL], bf16, g) for b in range(2)]
            inv = sb("inv", [REL, N], f32, g)
        g = ExitStack()
        with g:
            hT = sb("hT", [128, FK + 2, N], f32, g)
            fw1 = [sb(f"fw1_{b}", [128, K, 2 * F], f32, g) for b in range(2)]
            fw3 = [sb(f"fw3_{b}", [128, K, 2 * F], f32, g) for b in range(2)]
            fw2 = sb("fw2", [128, FK + 2, D], f32, g)
            combw = [sb(f"combw{b}", [P, T, 2 * F], f32, g) for b in range(2)]
            b1r = sb("b1r", [FK, 128], f32, g)
            b1T = sb("b1T", [128, FK], f32, g)
            b2r = sb("b2r", [NE, D], f32, g)
            combT = sb("combT", [NE, N], f32, g)
            specw = sb("specw", [3, D], f32, g)
            bkrow = sb("bkrow", [3, D], f32, g)
            feats = sb("feats", [3, N], f32, g)
        g = ExitStack()
        with g:
            pad = sb("pad", [128, FK + 2, N], f32, g)
            pad2 = sb("pad2", [128, 2, K, 2 * F], f32, g)
            vch = sb("vch", [BC, BC], f32, g)
            ar = sb("ar", [BC, 2, BC], f32, g)
            ar2 = sb("ar2", [BC, BC, 2, 2], f32, g)
            S = sb("S", [BC, BC + 2, 8], f32, g)
            SW = sb("SW", [BC, 2, 8], f32, g)
            ml = sb("ml", [1, BC, 16], f32, g)
            mo = sb("mo", [1, BC, 2, 12], f32, g)
            rho = sb("rho", [1, BC + 1, 2, 2], f32, g)
            rhoo = sb("rhoo", [1, BC, 4], f32, g)
            mt = sb("mt", [1, 5, 2, 4], f32, g)
            rin = sb("rin", [BC, 2, 2], f32, g)
            nrin = sb("nrin", [BC, 2, 2], f32, g)
            sol = sb("sol", [BC, 2, BC + 1, 2], f32, g)
            dq = sb("dq", [BC, 6, 2, BC, 2], f32, g)
            green = sb("green", [BC, 2, BC], f32, g)
            v_col = sb("v_col", [P, T], f32, g)
        g = ExitStack()
        with g:
            raw = sb("raw", [128, K, D], f32, g)
            whi = [sb(f"whi{b}", [128, K, D], f32r, g) for b in range(2)]
            wlo = [sb(f"wlo{b}", [128, K, D], f32r, g) for b in range(2)]
            xhi = sb("xhi", [128, K, N], f32r, g)
            xlo = sb("xlo", [128, K, N], f32r, g)
        zbuf = xn
        g = ExitStack()
        with g:
            wroot = sb("wroot", [128, K, D], f32, g)
            wgcn = sb("wgcn", [128, K, D], f32, g)
            rbrow = sb("rbrow", [1, D], f32, g)
            gbrow = sb("gbrow", [P, D], f32, g)
            hotf = [sb(f"hotf{b}", [EP, N], f32r, g) for b in range(2)]
            zg = [sb(f"zg{b}", [EP, D], f32, g) for b in range(4)]
            mhi = [sb(f"mhi{b}", [EP, D], f32r, g) for b in range(2)]
            mlo = [sb(f"mlo{b}", [EP, D], f32r, g) for b in range(2)]
            zib = [sb(f"zib{b}", [EP, 1], u32, g) for b in range(4)]
            h1 = sb("h1", [P, T, D], f32, g)
            xws = sb("xws", [P, T, D], f32, g)
            gtmp = sb("gtmp", [P, D], f32, g)

        psT = lambda q: slot(q)[:, 0:T * 128].rearrange("p (t c) -> p t c", c=128)

        block = ctx.enter_context(nc.Block())

        @block.sync
        def _(sp):
            sp.dma_start(eint[:, 0, :], src.rearrange("(p j) -> p j", j=ET)).then_inc(ld_edges, 16)
            sp.dma_start(eint[:, 1, :], dst.rearrange("(p j) -> p j", j=ET)).then_inc(ld_edges, 16)
            sp.dma_start(eint[:, 2, :], etype.rearrange("(p j) -> p j", j=ET)).then_inc(ld_edges, 16)
            sp.dma_start(x_res[:, :, :], x.rearrange("(t p) d -> p t d", p=P)).then_inc(ld_x, 16)
            sp.dma_start(gw[0][:, :, :], w["L0_gnn_W1"].rearrange("(k p) n -> p k n", p=128)).then_inc(ld_w1, 16)
            for n, name in enumerate(("L0_gnn_a_src1", "L0_gnn_a_dst1", "L0_gnn_a_src2", "L0_gnn_a_dst2")):
                sp.dma_start(arow[:, n, :], w[name].rearrange("h c -> (h c)").partition_broadcast(P)).then_inc(ld_rows, 16)
            for n, name in enumerate(("L0_gnn_b1", "L0_gnn_b2")):
                sp.dma_start(brow[:, n, :], w[name].partition_broadcast(P)).then_inc(ld_rows, 16)
            sp.dma_start(gw[1][:, :, :], w["L0_gnn_W2"].rearrange("(k p) n -> p k n", p=128)).then_inc(ld_w2, 16)
            sp.dma_start(gate_sb[:, :, 0:NE], w["L0_ffn_gate_w"].rearrange("(k p) n -> p k n", p=128)).then_inc(ld_gate, 16)
            sp.dma_start(gate_sb[:, :, NE:NE + 1], w["L0_ffn_v_w"].rearrange("(k p n) -> p k n", p=128, n=1), allow_slow_non_contiguous=True).then_inc(ld_gate, 16)
            sp.dma_start(wr_sb[:, :, :], w["L1_ffn_Wr"].rearrange("(k p) n -> p k n", p=128)).then_inc(ld_gate, 16)
            sp.dma_start(gate_b[:, :], w["L0_ffn_gate_b"].partition_broadcast(P)).then_inc(ld_gate, 16)
            sp.dma_start(v_b[:, :], w["L0_ffn_v_b"].partition_broadcast(P)).then_inc(ld_gate, 16)
            sp.wait_ge(inv_ready, 1)
            sp.dma_start(inv_dram.rearrange("(r n) o -> r (n o)", n=N), inv[:, :]).then_inc(inv_stored, 16)

            sp.wait_ge(inv_stored, 16)
            sp.wait_ge(evw_ready, 1)
            sp.wait_ge(layer_done, 1)
            sp.dma_start(b1r[:, :], w["L0_ffn_b1"].rearrange("e f -> (e f)").rearrange("(c p) -> c p", p=128)).then_inc(ld_small, 16)
            sp.dma_start(b2r[:, :], w["L0_ffn_b2"]).then_inc(ld_small, 16)
            sp.dma_start(specw[0:2, :], w["L0_ffn_out_w"]).then_inc(ld_small, 16)
            sp.dma_start(specw[2:3, :], w["L0_ffn_out_b"].rearrange("(a d) -> a d", a=1)).then_inc(ld_small, 16)
            sp.dma_start(bkrow[:, :], w["L0_ffn_bk_scale"].partition_broadcast(3)).then_inc(ld_small, 16)
            w1v = w["L0_ffn_w1"].rearrange("e (k p) f -> e p k f", p=128)

            def load_pair(buf, view, i, signal):
                for e in range(2):
                    sp.dma_start(buf[:, :, e * F:(e + 1) * F], view[2 * i + e, :, :, :]).then_inc(signal, 16)

            load_pair(fw1[0], w1v, 0, ld_f1[0])
            load_pair(fw1[1], w1v, 1, ld_f1[1])
            sp.dma_start(fw2[:, 0:FK, :], w["L0_ffn_w2"].rearrange("e f d -> (e f) d").rearrange("(c p) d -> p c d", p=128)).then_inc(ld_f2, 16)
            for i in (2, 3):
                sp.wait_ge(act_done, 1 + 3 * (i - 1))
                load_pair(fw1[i % 2], w1v, i, ld_f1[i % 2])
            sp.wait_ge(v_ready, 1)
            sp.dma_start(v_dram.rearrange("(t p) -> p t", p=P), v_col[:, :], allow_slow_non_contiguous=True).then_inc(v_out, 16)
            sp.wait_ge(v_out, 16)
            sp.dma_start(vch[:, :], v_dram.rearrange("(c t) -> c t", t=BC)).then_inc(v_in, 16)
            sp.wait_ge(mat_ready, 1)
            sp.dma_start(mat_dram, S[:, BC:BC + 2, :].rearrange("p a b -> p (a b)")).then_inc(mat_out, 16)
            sp.wait_ge(mat_out, 16)
            sp.dma_start(ml[:, :, :], mat_dram.rearrange("(a c) m -> a c m", a=1)).then_inc(mat_in, 16)
            sp.wait_ge(rho_ready, 1)
            sp.dma_start(rho_dram.rearrange("(a c) m -> a c m", a=1), rhoo[:, :, :]).then_inc(rho_out, 16)
            sp.wait_ge(rho_out, 16)
            sp.dma_start(rin[:, :, :].rearrange("p a b -> p (a b)"), rho_dram).then_inc(rho_in, 16)
            sp.wait_ge(green_ready, 1)
            sp.dma_start(green_dram.rearrange("r (c t) -> c r t", t=BC), green[:, :, :]).then_inc(green_out, 16)
            sp.wait_ge(green_out, 16)
            sp.dma_start(feats[0:2, :], green_dram).then_inc(green_in, 16)

            sp.wait_ge(layer_done, 2)
            wv = w["L1_gnn_W_rel"].rearrange("r (k p) n -> r p k n", p=128)
            KH = K // 2

            def load_raw(r, first):
                for half in range(2):
                    if not first:
                        sp.wait_ge(split_lo, r * 2 + half - 1)
                    sp.dma_start(raw[:, half * KH:(half + 1) * KH, :],
                                 wv[r, :, half * KH:(half + 1) * KH, :]).then_inc(raw_loaded[half], 16)

            load_raw(0, True)
            with sp.Fori(1, REL) as r:
                load_raw(r, False)

            sp.wait_ge(layer_done, 3)
            sp.dma_start(wroot[:, :, :], w["L1_gnn_W_root"].rearrange("(k p) n -> p k n", p=128)).then_inc(ld_root, 16)
            sp.dma_start(rbrow[:, :], w["L1_gnn_b_rgcn"].rearrange("(a d) -> a d", a=1)).then_inc(ld_root, 16)
            sp.dma_start(wgcn[:, :, :], w["L1_gnn_W_gcn"].rearrange("(k p) n -> p k n", p=128)).then_inc(ld_gcn, 16)
            sp.dma_start(gbrow[:, :], w["L1_gnn_b_gcn"].partition_broadcast(P)).then_inc(ld_gcn, 16)

            sp.wait_ge(layer_done, 4)
            v1 = w["L1_ffn_w1"].rearrange("e (k p) f -> e p k f", p=128)
            v3 = w["L1_ffn_w3"].rearrange("e (k p) f -> e p k f", p=128)
            for i in range(NE // 2):
                if i >= 2:
                    sp.wait_ge(inner_done, FK + 3 * (i - 1))
                load_pair(fw1[i % 2], v1, i, ld_f1[i % 2])
                load_pair(fw3[i % 2], v3, i, ld_f1[i % 2])
                if i == 1:
                    sp.dma_start(fw2[:, 0:FK, :], w["L1_ffn_w2"].rearrange("e f d -> (e f) d").rearrange("(c p) d -> p c d", p=128)).then_inc(ld_f2, 16)
                    sp.dma_start(fw2[0:F // 2, FK:FK + 2, :], w["L1_ffn_s2"].rearrange("(c p) d -> p c d", c=2)).then_inc(ld_f2, 16)
            sp.wait_ge(inner_done, FK + 9)
            sp.dma_start(fw1[0][:, :, 0:F], w["L1_ffn_s1"].rearrange("(k p) f -> p k f", p=128)).then_inc(ld_f1[0], 16)
            sp.dma_start(fw3[0][:, :, 0:F], w["L1_ffn_s3"].rearrange("(k p) f -> p k f", p=128)).then_inc(ld_f1[0], 16)

            sp.wait_ge(layer_done, 5)
            sp.dma_start(out.rearrange("(t p) d -> p t d", p=P), x_res[:, :, :]).then_inc(out_stored, 16)
            sp.wait_ge(out_stored, 16)

        @block.gpsimd
        def _(pool):
            step = Track(pool, pool_step)
            step(pool.iota(iota16[:, :], [[1, N]], base=0, channel_multiplier=0, allow_small_or_imprecise_dtypes=True))
            step(pool.iota(iota34[:, :], [[1, REL]], base=0, channel_multiplier=0, allow_small_or_imprecise_dtypes=True))
            step(pool.iota(rev[:, :], [[-1, NE]], base=NE, channel_multiplier=0, allow_small_or_imprecise_dtypes=True))
            step(pool.memset(ones[:, :], 1.0))
            step.do(pool.memset(ident[:, :], 0.0))
            step.do(pool.affine_select(out=ident[:, :], in_=ident[:, :], compare_op=ALU.not_equal, fill=1.0,
                                       base=0, pattern=[[-1, 128]], channel_multiplier=1))
            pool.sem_inc(consts_ready, 1)
            pool.wait_ge(inv_stored, 16)
            pool.wait_ge(cidx_ready, 1)
            with step.turns(ET, 2) as j:
                step.do(pool.tensor_copy(idxb[:, :], cidx[:, bass.ds(j, 1)]))
                pool.sem_inc(gathers_begun, 1)
                pool.indirect_dma_start(evwb[:, :], None, inv_dram,
                                        bass.IndirectOffsetOnAxis(ap=idxb[:, :], axis=0)).then_inc(evw_loaded, 16)
                pool.wait_ge(evw_loaded, j * 16 + 16)
                step.do(pool.tensor_copy(evw[:, bass.ds(j, 1)], evwb[:, :]))
            pool.sem_inc(evw_ready, 1)
            pool.wait_ge(layer_done, 3)
            with pool.Fori(0, ET // 4) as j:
                for b in range(4):
                    pool.wait_ge(idx_used, j * 4 + b + 1)
                    pool.sem_inc(gathers_begun, 1)
                    pool.indirect_dma_start(zg[b][:, :], None, z_dram,
                                            bass.IndirectOffsetOnAxis(ap=zib[b][:, :], axis=0)).then_inc(gathered[b], 16)
            pool.wait_ge(layer_done, 4)
            step.do(pool.memset(hT[0:P, 2:2 + T, :], 1.0))
            for i in range(T):
                step(pool.affine_select(out=hT[0:P, 2 + i, :], in_=hT[0:P, 2 + i, :], compare_op=ALU.is_gt, fill=0.0,
                                        base=i * P, pattern=[[-1, N]], channel_multiplier=1))
            step.sync()
            pool.sem_inc(earlier_ready, 1)

        @block.scalar
        def _(act):
            step = Track(act, act_step)

            def evict(stage, q, k, dst_ap, src_ap, signal=None):
                act.wait_ge(full[q], BEFORE[stage][q] + k + 1)
                ins = act.activation(dst_ap, src_ap, ACT.Copy)
                step.do(ins)
                act.sem_inc(free[q], 1)
                if signal is not None:
                    act.sem_inc(signal, 1)

            def turn(stage):
                for k in range(K):
                    evict(stage, k % 4, k // 4, xT[:, k, :].rearrange("p (t c) -> p t c", c=P), psT(k % 4)[:, :, 0:P], xT_ready)

            def root(ready, k, ap_out, ap_in):
                act.wait_ge(ready, k)
                step.do(act.activation(ap_out, ap_in, ACT.Sqrt))
                act.sem_inc(std_ready, 1)

            def sides(q):
                return slot(q).rearrange("p (b c) -> p b c", c=BANK)[0:P, :, 0:HALF]

            def product(stage, dst_of, signal):
                for t in range(T):
                    to = dst_of(t)
                    of = sides(t % 4)
                    evict(stage, t % 4, t // 4, to, of.rearrange("p b (h c) -> p b h c", c=HC) if stage == "w1" else of, signal)

            flat = cnt[:, :, :].rearrange("p t n -> p (t n)")
            for q in range(3):
                evict("edges", q, 0, flat[:, q * 2 * BANK:(q + 1) * 2 * BANK], slot(q)[0:P, :])
            act.sem_inc(cnt_ready, 1)
            act.wait_ge(deg_ready, 1)
            step.do(act.activation(dinv[:, :], t5[:, 7, :], ACT.Sqrt))
            act.sem_inc(deg_sqrt, 1)

            root(var_ready, 1, rstd[:, :], t5[:, 0, :])
            turn("turn1")
            hv = hx[:, :, :].rearrange("p t (h c) -> p t h c", c=HC + 1)
            product("w1", lambda t: hv[:, t, :, 0:HC].rearrange("p (b h) c -> p b h c", b=2), h_ready)

            def exps(stage, turn_no, k1, k2):
                act.wait_ge(full[1], k1)
                act.wait_ge(full[2], k2)
                for q, dest in ((1, e1[0]), (2, e2)):
                    for t in range(T):
                        step(act.activation(dest[:, t, :].rearrange("p (t c) -> p t c", c=P), psT(q)[0:P, :, 0:P],
                                            ACT.Exp, bias=(hcol if q == 1 else rcol)[:, t, 0:1]))
                    step.sync()
                    act.sem_inc(free[q], 1)
                act.sem_inc(exps_ready, 1)

            with step.turns(HEADS, 2 * T) as h:
                act.wait_ge(probs_free, h + 1)
                exps("heads1", h, h + BEFORE["heads1"][1] + 1, h + BEFORE["heads1"][2] + 1)
            act.wait_ge(elu_in, 1)
            for t in range(T):
                step(act.activation(hx[:, t, 0:D], xn[:, t, :], ACT.Exp))
            step.sync()
            act.sem_inc(elu_exp, 1)
            turn("turn2")
            product("w2", lambda t: hx[:, t, 0:D].rearrange("p (b c) -> p b c", b=2), h_ready)
            act.wait_ge(probs_free, HEADS + 1)
            exps("heads2", 0, BEFORE["heads2"][1] + 1, BEFORE["heads2"][2] + 1)

            def router(n):
                act.wait_ge(logits_in, n)
                step.do(act.activation(small[:, 1, :, :], small[:, 0, :, :], ACT.Exp))
                act.sem_inc(logits_exp, 1)

            root(var_ready, 2, rstd[:, :], t5[:, 0, :])
            turn("turn3")
            router(1)
            act.wait_ge(full[1], BEFORE["route1"][1] + 1)
            step.do(act.activation(combT[:, :].rearrange("p (t c) -> p t c", c=P), psT(1)[0:NE, :, 0:P], ACT.Copy))
            act.sem_inc(free[1], 1)
            act.wait_ge(full[2], BEFORE["route1"][2] + 1)
            step.do(act.activation(b1T[:, :], slot(2)[:, 0:FK], ACT.Copy))
            act.sem_inc(free[2], 1)
            act.sem_inc(act_done, 1)

            def gelus(c, b, k):
                act.wait_ge(full[b], BEFORE["inner1"][b] + 1 + k)
                step.do(act.activation(hT[:, c, :], slot(b)[:, 0:N], ACT.Gelu_apprx_tanh, bias=b1T[:, c:c + 1]))
                act.sem_inc(free[b], 1)
                act.sem_inc(act_done, 1)

            for c in range(FK):
                gelus(c, c % 2, c // 2)

            root(var_ready, 3, rstd[:, :], t5[:, 0, :])
            turn("turn4")
            for k in range(K):
                step(act.activation(xhi[:, k, :], xT[:, k, :], ACT.Copy))
            step.sync()
            act.sem_inc(xsplit_ready, 1)
            KH = K // 2
            SLOTS = [0, 1, 2, 3, 0, 1, 2, 3, 0, 1]
            SEEN = [0, 0, 0, 0, 1, 1, 1, 1, 2, 2]
            PER = [3, 3, 2, 2]

            def hi_halves(r, b):
                for half in range(2):
                    act.wait_ge(raw_loaded[half], r * 16 + 16)
                    step.do(act.activation(whi[b][:, half * KH:(half + 1) * KH, :],
                                           raw[:, half * KH:(half + 1) * KH, :], ACT.Copy))
                    act.sem_inc(split_hi, 1)

            def z_out(r, b, turn_no, first):
                for t in range(T):
                    n = T * b + t
                    q = SLOTS[n]
                    act.wait_ge(full[q], BEFORE["relations"][q] + SEEN[n] + 1 + turn_no * PER[q])
                    if not first:
                        act.wait_ge(z_stored[t], r * 16)
                    step.do(act.activation(zbuf[:, t, :].rearrange("p (b c) -> p b c", b=2), sides(q), ACT.Copy))
                    act.sem_inc(free[q], 1)
                    act.dma_start(z_dram.rearrange("(r t p) d -> r t p d", p=P, t=T)[r, t, :, :], zbuf[:, t, :]).then_inc(z_stored[t], 16)

            hi_halves(0, 0)
            hi_halves(1, 1)
            z_out(0, 0, 0, True)
            with step.turns(REL // 2 - 1, 4 + 2 * T) as i:
                hi_halves(i * 2 + 2, 0)
                z_out(i * 2 + 1, 1, i, False)
                hi_halves(i * 2 + 3, 1)
                z_out(i * 2 + 2, 0, i + 1, False)
            z_out(REL - 1, 1, REL // 2 - 1, False)
            for t in range(T):
                act.wait_ge(z_stored[t], REL * 16)
            act.sem_inc(layer_done, 1)

            def high(i, b, z):
                act.wait_ge(gathered[z], i * 16 + 16)
                act.wait_ge(hot_ready, i * 4 + z + 1)
                step.do(act.activation(mhi[b][:, :], zg[z][:, :], ACT.Copy, scale=gtmp[:, z:z + 1]))
                act.sem_inc(msg_hi, 1)

            with step.turns(ET // 4, 4) as i:
                for z in range(4):
                    high(i, z % 2, z)

            turn("turn5")
            product("wgcn", lambda t: xws[:, t, :].rearrange("p (b c) -> p b c", b=2), xw_ready)

            root(var_ready, 4, rstd[:, :], t5[:, 0, :])
            turn("turn6")
            router(2)
            for c in range(FK):
                act.wait_ge(full[0], BEFORE["inner2"][0] + 1 + c)
                step.do(act.activation(hT[:, c, :], slot(0)[:, 0:N], ACT.Silu))
                act.sem_inc(free[0], 1)
                act.sem_inc(act_done, 1)
            for c in range(2):
                act.wait_ge(full[0], BEFORE["shared"][0] + 1 + c)
                step.do(act.activation(hT[0:F // 2, FK + c, :], slot(0)[0:F // 2, 0:N], ACT.Silu))
                act.sem_inc(free[0], 1)
                act.sem_inc(act_done, 1)

        @block.vector
        def _(dve):
            step = Track(dve, dve_step)
            do = step.do

            def tt(o, a, b, op):
                return dve.tensor_tensor(o, a, b, op)

            def ts(o, a, s1, s2, op0, op1=None):
                return dve.tensor_scalar(o, a, s1, s2, op0) if op1 is None else dve.tensor_scalar(o, a, s1, s2, op0, op1)

            def free_slot(q):
                dve.sem_inc(free[q], 1)

            dve.wait_ge(ld_edges, 48)
            dve.wait_ge(consts_ready, 1)
            do(dve.tensor_copy(ef[:, :, :], eint[:, :, :]))
            step(dve.tensor_copy(dstf[:, :], ef[:, 1, :]))
            step(dve.scalar_tensor_tensor(zidx[:, :], ef[:, 2, :], float(N), ef[:, 0, :], ALU.mult, ALU.add))
            do(dve.scalar_tensor_tensor(cidx[:, :], ef[:, 2, :], float(N), ef[:, 1, :], ALU.mult, ALU.add))
            dve.sem_inc(cidx_ready, 1)

            def onehots(j, b, first):
                if not first:
                    dve.wait_ge(onehots_used, j + b - 1)
                dve.tensor_scalar(hot_s[b][:, :], iota16[:, :], ef[:, 0, bass.ds(j + b, 1)], None, ALU.is_equal)
                dve.tensor_scalar(hot_d[b][:, :], iota16[:, :], ef[:, 1, bass.ds(j + b, 1)], None, ALU.is_equal)
                dve.tensor_scalar(hot_r[b][:, :], iota34[:, :], ef[:, 2, bass.ds(j + b, 1)], None,
                                  ALU.is_equal).then_inc(onehots_ready, 1)

            for b in range(2):
                onehots(0, b, True)
            with dve.Fori(1, ET // 2) as i:
                for b in range(2):
                    onehots(i * 2, b, False)
            dve.wait_ge(full[3], BEFORE["edges"][3] + 1)
            flat = cnt[:, :, :].rearrange("p t n -> p (t n)")
            step(dve.tensor_copy(flat[:, 6 * BANK:T * N], slot(3)[0:P, 0:T * N - 6 * BANK]))
            do(ts(inv[:, :], slot(3)[0:REL, T * N - 6 * BANK:(T + 1) * N - 6 * BANK], 1.0, None, ALU.max))
            dve.sem_inc(cnt_ready, 1)
            free_slot(3)
            do(dve.reciprocal(inv[:, :], inv[:, :]))
            dve.sem_inc(inv_ready, 1)
            for t in range(T):
                dve.wait_ge(full[t % 4], BEFORE["mask"][t % 4] + t // 4 + 1)
                if t == 0:
                    do(ts(t5[:, 7, :], slot(0)[0:P, 700:700 + T], 1.0, None, ALU.add))
                    dve.sem_inc(deg_ready, 1)
                do(ts(negm[:, t, :].rearrange("p (t c) -> p t c", c=P), psT(t % 4)[0:P, :, 0:P], 0.0, -1e30, ALU.is_equal, ALU.mult))
                free_slot(t % 4)
            dve.wait_ge(deg_sqrt, 1)
            do(dve.reciprocal(dinv[:, :], dinv[:, :]))

            def norm(n, source):
                for t in range(T):
                    for s in range(2):
                        step(dve.bn_stats(stats[:, t, s, :], source[:, t, s * HALF:(s + 1) * HALF]))
                step.sync()
                for t in range(T):
                    step(dve.bn_aggr(mv[:, t, :], stats[:, t, :, :].rearrange("p a b -> p (a b)")))
                step.sync()
                do(ts(t5[:, 0, :], mv[:, :, 1], EPS, None, ALU.add))
                dve.sem_inc(var_ready, 1)
                dve.wait_ge(std_ready, n)
                do(dve.reciprocal(rstd[:, :], rstd[:, :]))
                for t in range(T):
                    do(ts(xn[:, t, :], source[:, t, :], mv[:, t, 0:1], rstd[:, t:t + 1], ALU.subtract, ALU.mult))
                    dve.sem_inc(xn_ready, 1)

            dve.wait_ge(ld_x, 16)
            norm(1, x_res)

            hv = hx[:, :, :].rearrange("p t (h c) -> p t h c", c=HC + 1)
            dve.wait_ge(ld_rows, 96)
            do(dve.memset(hv[:, :, :, HC:HC + 1], 1.0))
            for t in range(T):
                dve.wait_ge(h_ready, t + 1)
                for s in range(2):
                    do(tt(tmp[:, :].rearrange("p (h c) -> p h c", c=HC), hv[:, t, :, 0:HC],
                          arow[:, s, :].rearrange("p (h c) -> p h c", c=HC), ALU.mult))
                    do(dve.tensor_reduce(al[:, t, s, :], tmp[:, :].rearrange("p (h c) -> p h c", c=HC), AX.X, ALU.add))

            def head(h, turn_no, agg):
                do(dve.tensor_copy(hcol[:, :, :], al[:, :, :, bass.ds(h, 1)].rearrange("p t s o -> p t (s o)")))
                do(ts(rcol[:, :, 0], hcol[:, :, 0], 0.2, None, ALU.mult))
                dve.sem_inc(cols_ready, 1)
                dve.wait_ge(full[0], turn_no[0] + 1)
                dve.sem_inc(maxima_begun, 1)
                for i in range(T):
                    step(dve.tensor_tensor_reduce(e2[:, i, :].rearrange("p (t c) -> p t c", c=P),
                                                  negm[:, i, :].rearrange("p (t c) -> p t c", c=P), psT(0)[0:P, :, 0:P],
                                                  1.0, -3e38, ALU.add, ALU.max, smax[:, 0, i:i + 1]))
                step.sync()
                free_slot(0)
                do(tt(smax[:, 1, :], smax[:, 0, :], hcol[:, :, 1], ALU.add))
                do(dve.scalar_tensor_tensor(smax[:, 2, :], smax[:, 1, :], 0.2, smax[:, 1, :], ALU.mult, ALU.max))
                step(tt(rcol[:, :, 1], hcol[:, :, 1], smax[:, 2, :], ALU.subtract))
                do(dve.scalar_tensor_tensor(smax[:, 3, :], hcol[:, :, 1], 0.2, smax[:, 2, :], ALU.mult, ALU.subtract))
                dve.sem_inc(r_ready, 1)
                dve.sem_inc(probs_free, 1)
                dve.wait_ge(exps_ready, turn_no[1] + 1)
                for t in range(T):
                    step(tt(e2[:, t, :], e1[0][:, t, :], e2[:, t, :], ALU.max))
                step.sync()
                for t in range(T):
                    do(dve.scalar_tensor_tensor(e1[1][:, t, :], e2[:, t, :], 1.0, cnt[:, t, :], ALU.min, ALU.mult))
                    dve.sem_inc(probs_ready, 1)
                agg(h)

            def agg1(h, k):
                dve.wait_ge(full[3], k)
                o = slot(3)[0:P, 0:T * (HC + 1)].rearrange("p (t c) -> p t c", c=HC + 1)
                do(ts(smax[:, 1, :], o[:, :, HC], 1e-16, None, ALU.add))
                do(dve.reciprocal(smax[:, 1, :], smax[:, 1, :]))
                do(tt(xn[:, :, bass.ds(h * HC, HC)], o[:, :, 0:HC], smax[:, 1, :].unsqueeze(2).broadcast_to([P, T, HC]), ALU.mult))
                free_slot(3)

            HEAD_STEPS = 1 + 1 + T + 1 + 1 + 2 + T + T + 3
            dve.wait_ge(xT_ready, K)
            head(0, (BEFORE["heads1"][0], 0), lambda h: agg1(h, BEFORE["heads1"][3] + 1))
            with step.turns(HEADS - 1, HEAD_STEPS) as i:
                head(i + 1, (i + 1 + BEFORE["heads1"][0], i + 1), lambda h: agg1(h, i + 1 + BEFORE["heads1"][3] + 1))

            for t in range(T):
                do(tt(xn[:, t, :], xn[:, t, :], brow[:, 0, :], ALU.add))
            dve.sem_inc(elu_in, 1)
            dve.wait_ge(elu_exp, 1)
            for t in range(T):
                do(ts(hx[:, t, 0:D], hx[:, t, 0:D], 1.0, -1.0, ALU.min, ALU.add))
                do(dve.scalar_tensor_tensor(xn[:, t, :], xn[:, t, :], 0.0, hx[:, t, 0:D], ALU.max, ALU.add))
                dve.sem_inc(xn_ready, 1)
            do(dve.memset(hx[:, :, D:D + 1], 1.0))
            for t in range(T):
                dve.wait_ge(h_ready, T + t + 1)
                for s in range(2):
                    do(tt(tmp[:, :], hx[:, t, 0:D], arow[:, 2 + s, :], ALU.mult))
                    do(dve.tensor_reduce(al[:, t, s, 0:1], tmp[:, :], AX.X, ALU.add))

            def agg2(h):
                for i in range(T):
                    q = (3, 0)[i % 2]
                    base = BEFORE["heads2"][q] + (1 if q == 0 else 0)
                    dve.wait_ge(full[q], base + i // 2 + 1)
                    do(ts(smax[:, 1, 0:1], slot(q)[0:P, BANK + HALF:BANK + HALF + 1], 1e-16, None, ALU.add))
                    do(dve.reciprocal(smax[:, 1, 0:1], smax[:, 1, 0:1]))
                    do(dve.scalar_tensor_tensor(xn[:, i, :].rearrange("p (b c) -> p b c", b=2),
                                                slot(q).rearrange("p (b c) -> p b c", c=BANK)[0:P, :, 0:HALF],
                                                smax[:, 1, 0:1],
                                                x_res[:, i, :].rearrange("p (b c) -> p b c", b=2), ALU.mult, ALU.add))
                    free_slot(q)
                    do(tt(x_res[:, i, :], xn[:, i, :], brow[:, 1, :], ALU.add))

            head(0, (BEFORE["heads2"][0], HEADS), agg2)
            dve.wait_ge(evw_ready, 1)
            dve.sem_inc(layer_done, 1)

            norm(2, x_res)

            def route(n, stage, bias):
                dve.wait_ge(full[0], BEFORE[stage][0] + 1)
                lg = slot(0)[0:P, 0:T * 16].rearrange("p (t c) -> p t c", c=16)
                L, E1, pr, k1, oh1, p2, oh2 = (small[:, i, :, :] for i in range(7))
                wide = lambda a: a.unsqueeze(2).broadcast_to([P, T, NE])
                if bias:
                    do(tt(pr, lg[:, :, 0:NE], gate_b[:, :].unsqueeze(1).broadcast_to([P, T, NE]), ALU.add))
                    do(ts(v_col[:, :], lg[:, :, NE], v_b[:, 0:1], -3.0, ALU.add, ALU.max))
                    do(ts(v_col[:, :], v_col[:, :], 3.0, -2.0, ALU.min, ALU.add))
                    dve.sem_inc(v_ready, 1)
                else:
                    do(dve.tensor_copy(pr, lg[:, :, 0:NE]))
                free_slot(0)
                do(dve.tensor_reduce(t5[:, 1, :], pr, AX.X, ALU.max))
                do(tt(L, pr, wide(t5[:, 1, :]), ALU.subtract))
                dve.sem_inc(logits_in, 1)
                dve.wait_ge(logits_exp, n)
                do(dve.tensor_reduce(t5[:, 1, :], E1, AX.X, ALU.add))
                do(dve.reciprocal(t5[:, 1, :], t5[:, 1, :]))
                do(tt(pr, E1, wide(t5[:, 1, :]), ALU.mult))
                for m, source, hot in ((2, pr, oh1), (3, p2, oh2)):
                    do(dve.tensor_reduce(t5[:, m, :], source, AX.X, ALU.max))
                    do(tt(k1, source, wide(t5[:, m, :]), ALU.is_equal))
                    do(tt(k1, k1, rev[:, :].unsqueeze(1).broadcast_to([P, T, NE]), ALU.mult))
                    do(dve.tensor_reduce(t5[:, 4, :], k1, AX.X, ALU.max))
                    do(tt(hot, k1, wide(t5[:, 4, :]), ALU.is_equal))
                    if m == 2:
                        do(dve.scalar_tensor_tensor(p2, hot, -2.0, pr, ALU.mult, ALU.add))
                do(tt(t5[:, 4, :], t5[:, 2, :], t5[:, 3, :], ALU.add))
                if not bias:
                    do(ts(t5[:, 4, :], t5[:, 4, :], 1e-9, None, ALU.max))
                do(dve.reciprocal(t5[:, 4, :], t5[:, 4, :]))
                do(tt(asg[:, :, :], oh1, oh2, ALU.add))
                do(tt(comb1[:, :, :], pr, asg[:, :, :], ALU.mult))
                do(tt(comb1[:, :, :], comb1[:, :, :], wide(t5[:, 4, :]), ALU.mult))

            dve.wait_ge(ld_gate, 80)
            route(1, "route1", True)
            dve.sem_inc(comb_ready, 1)

            def widen(i, b):
                do(dve.tensor_copy(combw[b][:, :, :].rearrange("p t (e f) -> p t e f", e=2),
                                   comb1[:, :, 2 * i:2 * i + 2].unsqueeze(3).broadcast_to([P, T, 2, F])))
                dve.sem_inc(combw_ready, 1)

            widen(0, 0)
            widen(1, 1)
            for c in range(FK):
                dve.wait_ge(act_done, c + 2)
                dve.wait_ge(full[2 + c % 2], BEFORE["inner1"][2 + c % 2] + c // 2 + 1)
                do(tt(hT[:, c, :], hT[:, c, :], slot(2 + c % 2)[:, 0:N], ALU.mult))
                free_slot(2 + c % 2)
                dve.sem_inc(inner_done, 1)
                if c % 3 == 2 and c // 3 + 2 < NE // 2:
                    widen(c // 3 + 2, c // 3 % 2)

            dve.wait_ge(v_in, 16)
            step(dve.tensor_copy(ar[:, 0, :], vch[:, :]))
            do(dve.tensor_copy(ar[:, 1, :], vch[:, ::-1]))
            step(ts(ar2[:, :, :, 0], ar[:, :, :].rearrange("p d t -> p t d"), -1.0, None, ALU.mult))
            step(dve.tensor_copy(ar2[:, :, :, 1], ar[:, :, :].rearrange("p d t -> p t d")))
            do(dve.memset(S[:, 0:2, :], 0.0))
            S5 = S[:, :, :].rearrange("p t (d k c) -> p t d k c", d=2, k=2)
            step(dve.memset(S5[:, 0, :, 1, 0:1], 1.0))
            do(dve.memset(S5[:, 1, :, 0, 0:1], 1.0))
            SW4 = SW[:, :, :].rearrange("p a (d k c) -> p a d k c", d=2, k=2)
            for t in range(BC):
                step(tt(SW[:, 0, :], S[:, t + 1, :], S[:, t, :], ALU.add))
                do(tt(SW4[:, 1, :, :, :], S5[:, t + 1, :, :, ::-1],
                      ar2[:, t, :, :].unsqueeze(2).broadcast_to([BC, 2, 2, 2]), ALU.mult))
                do(tt(S[:, t + 2, :], SW[:, 0, :], SW[:, 1, :], ALU.add))
            dve.sem_inc(mat_ready, 1)
            dve.wait_ge(mat_in, 16)
            m6 = ml[:, :, :].rearrange("o c (m d k r) -> o c m d k r", m=2, d=2, k=2)
            mo6 = mo[:, :, :, :].rearrange("o c d (k m r) -> o c d k m r", k=3, m=2)
            for d in range(2):
                s = slice(None, None, -1) if d else slice(None)
                for m in range(2):
                    step(dve.tensor_copy(mo6[:, :, d, 0, m, :], m6[:, s, m, d, 0, :]))
                    step(dve.tensor_copy(mo6[:, :, d, 1, m, :], m6[:, s, m, d, 1, :]))
                    step(ts(mo6[:, :, d, 2, m, 0], m6[:, s, m, d, 1, 1], -1.0, None, ALU.mult))
                    step(dve.tensor_copy(mo6[:, :, d, 2, m, 1], m6[:, s, m, d, 1, 0]))
            do(dve.memset(rho[:, 0:1, :, :], 0.0))
            for c in range(BC - 1):
                cur = rho[:, c, :, :]
                M4 = lambda k: mo[:, c, :, 4 * k:4 * k + 4]
                step(tt(mt[:, 0, :, :], M4(1), cur[:, :, 0:1].broadcast_to([1, 2, 4]), ALU.mult))
                do(tt(mt[:, 1, :, :], M4(2), cur[:, :, 1:2].broadcast_to([1, 2, 4]), ALU.mult))
                do(tt(mt[:, 0, :, :], mt[:, 0, :, :], M4(0), ALU.add))
                do(tt(mt[:, 0, :, :], mt[:, 0, :, :], mt[:, 1, :, :], ALU.add))
                num, den = mt[:, 0, :, 0:2], mt[:, 0, :, 2:4]
                nd = mt[:, 0, :, :].rearrange("o d (m r) -> o d m r", m=2)
                step(tt(mt[:, 2, :, :].rearrange("o d (m r) -> o d m r", m=2), nd,
                        den.unsqueeze(2).broadcast_to([1, 2, 2, 2]), ALU.mult))
                do(tt(mt[:, 3, :, 0:2], num, den[:, :, ::-1], ALU.mult))
                step(dve.tensor_reduce(mt[:, 4, :, 0:3:2], mt[:, 2, :, :].rearrange("o d (m r) -> o d m r", m=2), AX.X, ALU.add))
                do(tt(mt[:, 4, :, 1:2], mt[:, 3, :, 1:2], mt[:, 3, :, 0:1], ALU.subtract))
                do(dve.reciprocal(mt[:, 4, :, 3:4], mt[:, 4, :, 2:3]))
                do(tt(rho[:, c + 1, :, :], mt[:, 4, :, 0:2], mt[:, 4, :, 3:4].broadcast_to([1, 2, 2]), ALU.mult))
            step(dve.tensor_copy(rhoo[:, :, 0:2], rho[:, 0:BC, 0, :]))
            do(dve.tensor_copy(rhoo[:, :, 2:4], rho[:, 0:BC, 1, :][:, ::-1, :]))
            dve.sem_inc(rho_ready, 1)
            dve.wait_ge(rho_in, 16)
            do(ts(nrin[:, :, :], rin[:, :, :], -1.0, None, ALU.mult))
            for d in range(2):
                al_, be = S5[:, 1:, d, 0, :], S5[:, 1:, d, 1, :]
                do(dve.scalar_tensor_tensor(sol[:, d, :, :], be, rin[:, d, 0:1], al_, ALU.mult, ALU.add))
                step(dve.scalar_tensor_tensor(sol[:, d, :, 0], be[:, :, 1], nrin[:, d, 1:2], sol[:, d, :, 0], ALU.mult, ALU.add))
                do(dve.scalar_tensor_tensor(sol[:, d, :, 1], be[:, :, 0], rin[:, d, 1:2], sol[:, d, :, 1], ALU.mult, ALU.add))
            for d in range(2):
                X, Y = sol[:, d, 1:, :], sol[:, d, 0:BC, :]
                q = lambda i: dq[:, i, d, :, :]
                step(tt(q(0), X, Y, ALU.mult))
                step(tt(q(1), X, Y[:, :, ::-1], ALU.mult))
                do(tt(q(2), Y, Y, ALU.mult))
                step(tt(q(3)[:, :, 0], q(1)[:, :, 1], q(1)[:, :, 0], ALU.subtract))
                step(dve.scalar_tensor_tensor(q(3)[:, :, 1], q(0)[:, :, 0], -1.0, q(0)[:, :, 1], ALU.mult, ALU.subtract))
                do(dve.tensor_reduce(q(4)[:, :, 0], q(2), AX.X, ALU.add))
                do(dve.reciprocal(q(4)[:, :, 1], q(4)[:, :, 0]))
                do(tt(q(5), q(3), q(4)[:, :, 1:2].broadcast_to([BC, BC, 2]), ALU.mult))
            do(tt(dq[:, 0, 0, :, :], dq[:, 5, 0, :, :], dq[:, 5, 1, ::-1, :], ALU.add))
            step(tt(dq[:, 0, 0, :, 0], dq[:, 0, 0, :, 0], ar[:, 0, :], ALU.subtract))
            do(ts(dq[:, 0, 0, :, 1], dq[:, 0, 0, :, 1], 1.0, None, ALU.add))
            do(tt(dq[:, 1, 0, :, :], dq[:, 0, 0, :, :], dq[:, 0, 0, :, :], ALU.mult))
            do(dve.tensor_reduce(dq[:, 2, 0, :, 0], dq[:, 1, 0, :, :], AX.X, ALU.add))
            do(dve.reciprocal(dq[:, 2, 0, :, 1], dq[:, 2, 0, :, 0]))
            step(tt(green[:, 0, :], dq[:, 0, 0, :, 0], dq[:, 2, 0, :, 1], ALU.mult))
            do(dve.scalar_tensor_tensor(green[:, 1, :], dq[:, 0, 0, :, 1], -1.0, dq[:, 2, 0, :, 1], ALU.mult, ALU.mult))
            do(ts(green[:, :, :], green[:, :, :], 10.0, -10.0, ALU.min, ALU.max))
            do(dve.memset(feats[:, :], 1.0))
            dve.sem_inc(green_ready, 1)
            dve.wait_ge(ld_small, 80)
            do(tt(specw[:, :], specw[:, :], bkrow[:, :], ALU.mult))
            dve.sem_inc(specw_ready, 1)

            def add_result(stage):
                for t in range(T):
                    q = t % 4
                    dve.wait_ge(full[q], BEFORE[stage][q] + t // 4 + 1)
                    xr = x_res[:, t, :].rearrange("p (b c) -> p b c", b=2)
                    do(tt(xr, slot(q).rearrange("p (b c) -> p b c", c=BANK)[0:P, :, 0:HALF], xr, ALU.add))
                    free_slot(q)

            add_result("outer1")
            dve.sem_inc(layer_done, 1)

            norm(3, x_res)
            for k in range(K):
                dve.wait_ge(xsplit_ready, 1)
                step(tt(xlo[:, k, :], xT[:, k, :], xhi[:, k, :].bitcast(f32), ALU.subtract))
            step.sync()
            dve.sem_inc(xsplit_ready, 1)
            KH = K // 2

            def low(r, b):
                for half in range(2):
                    dve.wait_ge(split_hi, r * 2 + half + 1)
                    s = slice(half * KH, (half + 1) * KH)
                    do(tt(wlo[b][:, s, :], raw[:, s, :], whi[b][:, s, :].bitcast(f32), ALU.subtract))
                    dve.sem_inc(split_lo, 1)

            with step.turns(REL // 2, 4) as i:
                low(i * 2, 0)
                low(i * 2 + 1, 1)

            dve.wait_ge(layer_done, 3)

            def message(j, z, first, more=True):
                b = z % 2
                if not first:
                    dve.wait_ge(msg_used, j + z - 1)
                step(dve.tensor_copy(gtmp[:, z:z + 1], evw[:, bass.ds(j + z, 1)]))
                do(dve.tensor_scalar(hotf[b][:, :], iota16[:, :], dstf[:, bass.ds(j + z, 1)], None, ALU.is_equal))
                dve.sem_inc(hot_ready, 1)
                dve.wait_ge(msg_hi, j + z + 1)
                do(dve.scalar_tensor_tensor(mlo[b][:, :], zg[z][:, :], gtmp[:, z:z + 1], mhi[b][:, :].bitcast(f32),
                                            ALU.mult, ALU.subtract))
                dve.sem_inc(msg_ready, 1)
                if more:
                    do(dve.tensor_copy(zib[z][:, :], zidx[:, bass.ds(j + z + 4, 1)]))
                    dve.sem_inc(idx_used, 1)

            for z in range(4):
                step(dve.tensor_copy(zib[z][:, :], zidx[:, z:z + 1]))
            step.sync()
            dve.sem_inc(idx_used, 4)
            for z in range(4):
                message(0, z, z < 2)
            with step.turns(ET // 4 - 2, 16) as i:
                for z in range(4):
                    message(i * 4 + 4, z, False)
            for z in range(4):
                message(ET - 4, z, False, False)
            for q in range(4):
                dve.wait_ge(full[q], BEFORE["messages"][q] + 1)
            do(dve.tensor_copy(h1[:, :, :], PS[0:P, 0:T * D].rearrange("p (t d) -> p t d", d=D)))
            for q in range(4):
                free_slot(q)
            dve.sem_inc(h1_ready, 1)
            for t in range(T):
                do(tt(cnt[:, t, t * P:(t + 1) * P], cnt[:, t, t * P:(t + 1) * P], ident[0:P, 0:P], ALU.add))
                dve.wait_ge(xw_ready, t + 1)
                do(ts(xws[:, t, :], xws[:, t, :], dinv[:, t:t + 1], None, ALU.mult))
                dve.sem_inc(xws_ready, 1)
            dve.wait_ge(ld_gcn, 32)
            for t in range(T):
                q = t % 4
                dve.wait_ge(full[q], BEFORE["gcn"][q] + t // 4 + 1)
                xr = x_res[:, t, :].rearrange("p (b c) -> p b c", b=2)
                do(dve.scalar_tensor_tensor(xr, slot(q).rearrange("p (b c) -> p b c", c=BANK)[0:P, :, 0:HALF],
                                            dinv[:, t:t + 1], xr, ALU.mult, ALU.add))
                free_slot(q)
                do(tt(x_res[:, t, :], x_res[:, t, :], gbrow[:, :], ALU.add))
            dve.sem_inc(layer_done, 1)

            norm(4, x_res)
            route(2, "route2", False)
            score = small[:, 7, :, :]
            do(dve.scalar_tensor_tensor(score, asg[:, :, :], -1.0, comb1[:, :, :], ALU.add, ALU.add))
            dve.wait_ge(earlier_ready, 1)
            for e in range(NE):
                b = e % 2
                do(dve.tensor_copy(scol[b][:, :], score[:, :, e]))
                dve.sem_inc(cols_ready, 1)
                dve.wait_ge(full[e % 4], BEFORE["ranks"][e % 4] + e // 4 + 1)
                for i in range(T):
                    ps = psT(e % 4)[0:P, :, 0:P]
                    s = scol[b][:, i:i + 1]
                    junk = hT[0:P, 1, :].rearrange("p (t c) -> p t c", c=P)
                    step(dve.tensor_scalar(junk, ps, s, None, ALU.is_gt, ALU.add, accum_out=small[:, 8, i, e:e + 1]))
                    tri = hT[0:P, 2 + i, :].rearrange("p (t c) -> p t c", c=P)
                    step(dve.scalar_tensor_tensor(hT[0:P, 7 + i, :].rearrange("p (t c) -> p t c", c=P), ps, s, tri,
                                                  ALU.is_equal, ALU.mult, accum_out=small[:, 9, i, e:e + 1]))
                    step.sync()
                step.sync()
                free_slot(e % 4)
            do(tt(small[:, 8, :, :], small[:, 8, :, :], small[:, 9, :, :], ALU.add))
            do(ts(small[:, 8, :, :], small[:, 8, :, :], float(CAP), None, ALU.is_lt))
            do(tt(comb1[:, :, :], comb1[:, :, :], small[:, 8, :, :], ALU.mult))
            dve.sem_inc(comb_ready, 1)
            widen(0, 0)
            widen(1, 1)
            for c in range(FK):
                dve.wait_ge(act_done, 1 + FK + c + 1)
                dve.wait_ge(full[1], BEFORE["inner2"][1] + c + 1)
                do(tt(hT[:, c, :], hT[:, c, :], slot(1)[:, 0:N], ALU.mult))
                free_slot(1)
                dve.wait_ge(full[2], BEFORE["inner2"][2] + c + 1)
                do(tt(hT[:, c, :], hT[:, c, :], slot(2)[:, 0:N], ALU.mult))
                free_slot(2)
                dve.sem_inc(inner_done, 1)
                if c % 3 == 2 and c // 3 + 2 < NE // 2:
                    widen(c // 3 + 2, c // 3 % 2)
            for c in range(2):
                dve.wait_ge(act_done, 1 + 2 * FK + c + 1)
                dve.wait_ge(full[1], BEFORE["shared"][1] + c + 1)
                do(tt(hT[0:F // 2, FK + c, :], hT[0:F // 2, FK + c, :], slot(1)[0:F // 2, 0:N], ALU.mult))
                free_slot(1)
                dve.sem_inc(inner_done, 1)
            add_result("outer2")
            dve.sem_inc(layer_done, 1)

        @block.tensor
        def _(pe):
            def take(stage, q, k):
                n = k + BEFORE[stage][q]
                if not isinstance(n, int) or n > 0:
                    pe.wait_ge(free[q], n)

            def piece(o, c0, n):
                while n:
                    m = min(n, BANK - c0 % BANK)
                    yield o, c0, m
                    c0, o, n = c0 + m, o + m, n - m

            pe.wait_ge(consts_ready, 1)

            def count(b, start):
                last = None
                for i in range(T + 1):
                    lhs = hot_s[b][:, i * P:(i + 1) * P] if i < T else hot_r[b][:, :]
                    for o, c, m in piece(0, i * N, N):
                        rows = P if i < T else REL
                        last = pe.matmul(PS[0:rows, c:c + m], lhs, hot_d[b][:, o:o + m],
                                         start=start and c % BANK == 0, stop=False, skip_group_check=True)
                return last

            for b in range(2):
                pe.wait_ge(onehots_ready, b + 1)
                count(b, b == 0).then_inc(onehots_used, 1)
            with pe.Fori(1, ET // 2) as i:
                for b in range(2):
                    pe.wait_ge(onehots_ready, i * 2 + b + 1)
                    count(b, False).then_inc(onehots_used, 1)
            pe.wait_ge(onehots_used, ET)
            for q in range(4):
                pe.sem_inc(full[q], 1)

            pe.wait_ge(cnt_ready, 2)
            for i in range(T):
                take("mask", i % 4, i // 4)
                for t in range(T):
                    mm = pe.transpose(psT(i % 4)[0:P, t, 0:P], cnt[:, t, i * P:(i + 1) * P], ident[0:P, 0:P])
                if i == 0:
                    for j in range(T):
                        for t in range(T):
                            mm = pe.matmul(slot(0)[0:P, 700 + j:701 + j], cnt[:, t, j * P:(j + 1) * P], ones[0:P, 0:1],
                                           start=(t == 0), stop=(t == T - 1))
                mm.then_inc(full[i % 4], 1)

            def turn(stage, source, ready):
                ready()
                for k in range(K):
                    take(stage, k % 4, k // 4)
                    for t in range(T):
                        mm = pe.transpose(psT(k % 4)[:, t, 0:P], source[:, t, k * 128:(k + 1) * 128], ident[0:P, 0:P])
                    mm.then_inc(full[k % 4], 1)

            def product(stage, weights, turns_done):
                pe.wait_ge(xT_ready, turns_done * K)
                for t in range(T):
                    take(stage, t % 4, t // 4)
                    for k in range(K):
                        for s in range(2):
                            mm = pe.matmul(slot(t % 4)[0:P, s * BANK:s * BANK + HALF], xT[:, k, t * P:(t + 1) * P],
                                           weights[:, k, s * HALF:(s + 1) * HALF], start=(k == 0), stop=(k == K - 1))
                    mm.then_inc(full[t % 4], 1)

            def spread(q, column):
                for t in range(T):
                    mm = pe.matmul(psT(q)[0:P, t, 0:P], column(t).broadcast_to([P, P]), ident[0:P, 0:P],
                                   start=True, stop=True)
                mm.then_inc(full[q], 1)

            turn("turn1", xn, lambda: pe.wait_ge(xn_ready, T))
            pe.wait_ge(ld_w1, 16)
            product("w1", gw[0], 1)

            def head_rows(stage, h):
                pe.wait_ge(cols_ready, h + 1)
                take(stage, 0, h if stage == "heads1" else 0)
                spread(0, lambda t: hcol[:, t, 0:1])
                pe.wait_ge(r_ready, h + 1)
                take(stage, 1, h if stage == "heads1" else 0)
                spread(1, lambda t: rcol[:, t, 1:2])
                take(stage, 2, h if stage == "heads1" else 0)
                spread(2, lambda t: smax[:, 3, t:t + 1])

            with pe.Fori(0, HEADS) as h:
                head_rows("heads1", h)
                take("heads1", 3, h)
                pe.wait_ge(probs_ready, (h + 1) * T)
                for i in range(T):
                    for t in range(T):
                        mm = pe.matmul(slot(3)[0:P, i * (HC + 1):(i + 1) * (HC + 1)], e1[1][:, t, i * P:(i + 1) * P],
                                       hx[:, t, bass.ds(h * (HC + 1), HC + 1)], start=(t == 0), stop=(t == T - 1))
                mm.then_inc(full[3], 1)

            turn("turn2", xn, lambda: pe.wait_ge(xn_ready, 2 * T))
            pe.wait_ge(ld_w2, 16)
            product("w2", gw[1], 2)
            head_rows("heads2", HEADS)
            pe.wait_ge(probs_ready, (HEADS + 1) * T)
            for i in range(T):
                q = (3, 0)[i % 2]
                take("heads2", q, i // 2 + (1 if q == 0 else 0))
                for t in range(T):
                    for s in range(2):
                        n = HALF + s
                        mm = pe.matmul(slot(q)[0:P, s * BANK:s * BANK + n], e1[1][:, t, i * P:(i + 1) * P],
                                       hx[:, t, s * HALF:s * HALF + n], start=(t == 0), stop=(t == T - 1))
                mm.then_inc(full[q], 1)

            turn("turn3", xn, lambda: pe.wait_ge(xn_ready, 3 * T))

            def logits(stage, weights, n, turns_done):
                pe.wait_ge(xT_ready, turns_done * K)
                take(stage, 0, 0)
                for t in range(T):
                    for k in range(K):
                        mm = pe.matmul(slot(0)[0:P, 16 * t:16 * t + n], xT[:, k, t * P:(t + 1) * P], weights[:, k, :],
                                       start=(k == 0), stop=(k == K - 1))
                mm.then_inc(full[0], 1)

            pe.wait_ge(ld_gate, 80)
            logits("route1", gate_sb, NE + 1, 3)
            pe.wait_ge(comb_ready, 1)
            take("route1", 1, 0)
            for t in range(T):
                mm = pe.transpose(psT(1)[0:NE, t, 0:P], comb1[:, t, :], ident[0:P, 0:P])
            mm.then_inc(full[1], 1)
            pe.wait_ge(ld_small, 80)
            take("route1", 2, 0)
            pe.transpose(slot(2)[:, 0:FK], b1r[:, :], ident[0:FK, 0:FK]).then_inc(full[2], 1)

            def inner(dst_ps, weights, c, rows=128):
                for k in range(K):
                    for o, n in ((0, BANK), (BANK, N - BANK)):
                        mm = pe.matmul(dst_ps[0:rows, o:o + n], weights[:, k, c * rows:(c + 1) * rows],
                                       xT[:, k, o:o + n], start=(k == 0), stop=(k == K - 1))
                return mm

            def weights_row(q, b, c):
                for t in range(T):
                    for o, p0, n in piece(0, t * P, P):
                        mm = pe.matmul(slot(q)[:, p0:p0 + n], combw[b][:, t, c * 128:(c + 1) * 128],
                                       ident[0:P, o:o + n], start=True, stop=True)
                mm.then_inc(full[q], 1)

            for c in range(FK):
                i, b = c // 3, c // 3 % 2
                pe.wait_ge(ld_f1[b], 32 * (i // 2 + 1))
                take("inner1", c % 2, c // 2)
                inner(slot(c % 2), fw1[b], c % 3).then_inc(full[c % 2], 1)
                take("inner1", 2 + c % 2, c // 2)
                pe.wait_ge(combw_ready, i + 1)
                weights_row(2 + c % 2, b, c % 3)

            def outer(stage, chunks, after):
                pe.wait_ge(ld_f2, 16 if stage == "outer1" else 48)
                for first, end in ((0, 4), (4, 5)):
                    for t in range(first, end):
                        take(stage, t % 4, t // 4)
                        for c, rows in chunks:
                            for s in range(2):
                                mm = pe.matmul(slot(t % 4)[0:P, s * BANK:s * BANK + HALF], hT[0:rows, c, t * P:(t + 1) * P],
                                               fw2[0:rows, c, s * HALF:(s + 1) * HALF], start=(c == 0),
                                               stop=(after is None and c == chunks[-1][0]))
                        if after is None:
                            mm.then_inc(full[t % 4], 1)
                    if after is not None:
                        for t in range(first, end):
                            after(t)

            def spectral(t):
                if t == 0:
                    pe.wait_ge(green_in, 16)
                    pe.wait_ge(specw_ready, 1)
                for s in range(2):
                    o = slot(t % 4)[0:P, s * BANK:s * BANK + HALF]
                    pe.matmul(o, combT[:, t * P:(t + 1) * P], b2r[:, s * HALF:(s + 1) * HALF], start=False, stop=False)
                    mm = pe.matmul(o, feats[:, t * P:(t + 1) * P], specw[:, s * HALF:(s + 1) * HALF],
                                   start=False, stop=True)
                mm.then_inc(full[t % 4], 1)

            pe.wait_ge(act_done, 1)
            pe.wait_ge(inner_done, FK)
            outer("outer1", [(c, 128) for c in range(FK)], spectral)

            turn("turn4", xn, lambda: pe.wait_ge(xn_ready, 4 * T))
            pe.wait_ge(xsplit_ready, 2)
            SLOTS = [0, 1, 2, 3, 0, 1, 2, 3, 0, 1]
            SEEN = [0, 0, 0, 0, 1, 1, 1, 1, 2, 2]
            PER = [3, 3, 2, 2]
            with pe.Fori(0, REL // 2) as r:
                for b in range(2):
                    pe.wait_ge(split_lo, r * 4 + 2 * b + 2)
                    for t in range(T):
                        n = T * b + t
                        q = SLOTS[n]
                        pe.wait_ge(free[q], BEFORE["relations"][q] + SEEN[n] + r * PER[q])
                        for k in range(K):
                            for part, (a, wt) in enumerate(((xhi, whi[b]), (xhi, wlo[b]), (xlo, whi[b]))):
                                for s in range(2):
                                    mm = pe.matmul(slot(q)[0:P, s * BANK:s * BANK + HALF], a[:, k, t * P:(t + 1) * P],
                                                   wt[:, k, s * HALF:(s + 1) * HALF],
                                                   start=(k == 0 and part == 0), stop=(k == K - 1 and part == 2))
                        mm.then_inc(full[q], 1)

            for q in range(4):
                take("messages", q, 0)

            def scatter(b, start):
                for part in (mhi[b], mlo[b]):
                    for i in range(T):
                        for o, c, m in piece(0, i * D, D):
                            mm = pe.matmul(PS[0:P, c:c + m], hotf[b][:, i * P:(i + 1) * P], part[:, o:o + m],
                                           start=start and part is mhi[b] and c % BANK == 0, stop=False, skip_group_check=True)
                mm.then_inc(msg_used, 1)

            for b in range(2):
                pe.wait_ge(msg_ready, b + 1)
                scatter(b, b == 0)
            with pe.Fori(1, ET // 2) as i:
                for b in range(2):
                    pe.wait_ge(msg_ready, i * 2 + b + 1)
                    scatter(b, False)
            pe.wait_ge(ld_root, 32)
            for i in range(T):
                for o, c, m in piece(0, i * D, D):
                    for k in range(K):
                        pe.matmul(PS[0:P, c:c + m], xT[:, k, i * P:(i + 1) * P], wroot[:, k, o:o + m],
                                  start=False, stop=False, skip_group_check=True)
                    mm = pe.matmul(PS[0:P, c:c + m], ones[0:1, 0:P], rbrow[:, o:o + m],
                                   start=False, stop=True, skip_group_check=True)
            mm.then_inc(full[0], 1)
            pe.wait_ge(full[0], BEFORE["messages"][0] + 1)
            for q in range(1, 4):
                pe.sem_inc(full[q], 1)

            turn("turn5", h1, lambda: pe.wait_ge(h1_ready, 1))
            pe.wait_ge(ld_gcn, 32)
            product("wgcn", wgcn, 5)
            pe.wait_ge(xws_ready, T)
            for i in range(T):
                take("gcn", i % 4, i // 4)
                for t in range(T):
                    for s in range(2):
                        mm = pe.matmul(slot(i % 4)[0:P, s * BANK:s * BANK + HALF], cnt[:, t, i * P:(i + 1) * P],
                                       xws[:, t, s * HALF:(s + 1) * HALF], start=(t == 0), stop=(t == T - 1))
                mm.then_inc(full[i % 4], 1)

            turn("turn6", xn, lambda: pe.wait_ge(xn_ready, 5 * T))
            logits("route2", wr_sb, NE, 6)
            for e in range(NE):
                pe.wait_ge(cols_ready, HEADS + 1 + e + 1)
                take("ranks", e % 4, e // 4)
                spread(e % 4, lambda t: scol[e % 2][:, t:t + 1])
            pe.wait_ge(comb_ready, 2)
            for c in range(FK):
                i, b = c // 3, c // 3 % 2
                pe.wait_ge(ld_f1[b], 64 + 64 * (i // 2 + 1))
                take("inner2", 0, c)
                inner(slot(0), fw1[b], c % 3).then_inc(full[0], 1)
                take("inner2", 1, c)
                inner(slot(1), fw3[b], c % 3).then_inc(full[1], 1)
                take("inner2", 2, c)
                pe.wait_ge(combw_ready, 4 + i + 1)
                weights_row(2, b, c % 3)
            pe.wait_ge(ld_f1[0], 64 + 128 + 32)
            for c in range(2):
                take("shared", 0, c)
                inner(slot(0), fw1[0], c, F // 2).then_inc(full[0], 1)
                take("shared", 1, c)
                inner(slot(1), fw3[0], c, F // 2).then_inc(full[1], 1)
            pe.wait_ge(inner_done, 2 * FK + 2)
            outer("outer2", [(c, 128) for c in range(FK)] + [(FK, F // 2), (FK + 1, F // 2)], None)


_WEIGHTS = [
    "L0_gnn_W1",
    "L0_gnn_a_src1",
    "L0_gnn_a_dst1",
    "L0_gnn_b1",
    "L0_gnn_W2",
    "L0_gnn_a_src2",
    "L0_gnn_a_dst2",
    "L0_gnn_b2",
    "L0_ffn_v_w",
    "L0_ffn_v_b",
    "L0_ffn_gate_w",
    "L0_ffn_gate_b",
    "L0_ffn_w1",
    "L0_ffn_b1",
    "L0_ffn_w2",
    "L0_ffn_b2",
    "L0_ffn_out_w",
    "L0_ffn_out_b",
    "L0_ffn_bk_scale",
    "L1_gnn_W_rel",
    "L1_gnn_W_root",
    "L1_gnn_b_rgcn",
    "L1_gnn_W_gcn",
    "L1_gnn_b_gcn",
    "L1_ffn_Wr",
    "L1_ffn_w1",
    "L1_ffn_w3",
    "L1_ffn_w2",
    "L1_ffn_s1",
    "L1_ffn_s3",
    "L1_ffn_s2",
]


def kernel(**inputs):
    import numpy as _np
    import concourse.bacc as _bacc
    from concourse.bass_utils import run_bass_kernel_spmd as _run

    nc = _bacc.Bacc("TRN2", target_bir_lowering=False, num_devices=1)
    arrays, aps = {}, {}
    for name in ["x", "src", "dst", "edge_type_34"] + _WEIGHTS:
        a = _np.ascontiguousarray(inputs[name])
        if name == "L0_ffn_v_b":
            a = a.reshape(1)
        arrays[f"in_{name}"] = a
        aps[name] = nc.dram_tensor(f"in_{name}", a.shape, mybir.dt.from_np(a.dtype), kind="ExternalInput").ap()
    aps["out"] = nc.dram_tensor("out_0", (N, D), mybir.dt.float32, kind="ExternalOutput").ap()
    build(nc, aps["x"], aps["src"], aps["dst"], aps["edge_type_34"], aps)
    r = _run(nc, [arrays], core_ids=[0])
    return r.results[0]["out_0"]
```

```python
import concourse.bass as bass
from concourse import mybir
from contextlib import ExitStack, contextmanager

N, D = 625, 768
P = 125
T = N // P
K = D // 128
EDGES = 10000
EP = 125
ET = EDGES // EP
REL = 34
HEADS, HC = 8, D // 8
NE, F = 8, 192
FF = NE * F
FK = FF // 128
CAP = 196
BC = 25
AHEAD = 8
RT = 2
MORE = -(-N // 128) - RT
LIST = 1000
FIRST = REL * RT * 128
FEW = 4
MANY = -(-EDGES * MORE // ((RT + 1) * 128 + 1))
HALF = D // 2
BANK = 512
EPS = 1e-5

STAGES = [
    ("edges", [1, 1, 1, 1]), ("turn1", [2, 2, 1, 1]), ("mask", [2, 1, 1, 1]), ("ranks", [0, 1, 0, 0]),
    ("w1", [2, 1, 1, 1]), ("heads1", [HEADS] * 4),
    ("turn2", [2, 2, 1, 1]), ("w2", [2, 1, 1, 1]), ("heads2", [3, 1, 1, 3]),
    ("turn3", [2, 2, 1, 1]), ("route1", [1, 1, 1, 0]), ("inner1", [6, 6, 6, 6]),
    ("lists", [1, 1, 0, 0]), ("outer1", [2, 1, 1, 1]),
    ("turn4", [2, 2, 1, 1]), ("relations", [REL + 2 * MORE * REL, REL, REL + MORE * REL, REL]),
    ("messages", [1, 1, 1, 1]), ("turn5", [2, 2, 1, 1]), ("wgcn", [2, 1, 1, 1]), ("gcn", [2, 1, 1, 1]),
    ("turn6", [2, 2, 1, 1]), ("route2", [1, 0, 0, 0]),
    ("inner2", [12, 12, 12, 8]), ("shared", [2, 2, 0, 0]), ("outer2", [2, 1, 1, 1]),
]
BEFORE, _n = {}, [0, 0, 0, 0]
for _name, _jobs in STAGES:
    BEFORE[_name] = list(_n)
    _n = [a + b for a, b in zip(_n, _jobs)]


class Track:

    def __init__(self, eng, own):
        self.eng, self.own, self.n, self.extra = eng, own, 0, None

    def __call__(self, ins):
        ins.then_inc(self.own, 1)
        self.n += 1
        return ins

    def sync(self):
        self.eng.wait_ge(self.own, self.n if self.extra is None else self.n + self.extra)

    def do(self, ins):
        self(ins)
        self.sync()

    @contextmanager
    def turns(self, n, signals):
        start = self.n
        with self.eng.Fori(0, n) as i:
            self.extra = i * signals
            yield i
        assert self.n - start == signals, (self.n - start, signals)
        self.extra = None
        self.n = start + signals * n


def build(nc, x, src, dst, etype, w):
    f32, f32r, bf16 = mybir.dt.float32, mybir.dt.float32r, mybir.dt.bfloat16
    i32, u32, i16 = mybir.dt.int32, mybir.dt.uint32, mybir.dt.int16
    ALU, ACT, AX = mybir.AluOpType, mybir.ActivationFunctionType, mybir.AxisListType

    out = w["out"]
    z_dram = nc.dram_tensor("z_dram", [FIRST + MANY * 128, D], f32).ap()
    inv_dram = nc.dram_tensor("inv_dram", [REL * N, 1], f32).ap()
    zrow_dram = nc.dram_tensor("zrow_dram", [REL * N, 1], u32).ap()
    xn_dram = nc.dram_tensor("xn_dram", [N, D], f32).ap()
    v_dram = nc.dram_tensor("v_dram", [N], f32).ap()
    mat_dram = nc.dram_tensor("mat_dram", [BC, 16], f32).ap()
    rho_dram = nc.dram_tensor("rho_dram", [BC, 4], f32).ap()
    green_dram = nc.dram_tensor("green_dram", [2, N], f32).ap()

    ctx = ExitStack()
    with ctx:
        def sb(name, shape, dt=f32, where=ctx):
            return where.enter_context(nc.sbuf_tensor(name, shape, dt))

        def sem(name):
            return ctx.enter_context(nc.semaphore(name))

        x_res = sb("x_res", [P, T, D])
        xn_all = sb("xn", [128, T, D])
        xn = xn_all[0:P, :, :]
        xT = sb("xT", [128, K, N])
        counts = sb("counts", [P, T, N + REL])
        cnt = counts[:, :, 0:N]
        ident = sb("ident", [128, 128])
        ones = sb("ones", [128, 128])
        stats = sb("stats", [P, T, 2, 6])
        mv = sb("mv", [P, T, 2])
        rstd = sb("rstd", [P, T])
        small = sb("small", [P, 12, T, NE])
        rev = sb("rev", [P, NE])
        asg = sb("asg", [P, T, NE])
        comb1 = sb("comb1", [P, T, NE])
        t5 = sb("t5", [P, 8, T])
        dinv = sb("dinv", [P, T])
        evw = sb("evw", [EP, ET])
        dstf = sb("dstf", [EP, ET])
        zidx = sb("zidx", [EP, ET], u32)
        iota16 = sb("iota16", [P, T * 128], i16)
        pos = sb("pos", [P, T, REL])
        poscol = sb("poscol", [P, T])
        rel_n = sb("rel_n", [1, REL], i32)
        ran_before = sb("ran_before", [1, REL + 1], i32)
        node_of = sb("node_of", [P, T, 2], bf16)
        inlist = [sb(f"inlist{b}", [P, T, RT * 128], bf16) for b in range(2)]
        xrow = sb("xrow", [128, 2, RT], u32)
        node = sb("node", [128, RT])
        gate_sb = sb("gate_sb", [128, K, NE + 1])
        wr_sb = sb("wr_sb", [128, K, NE])
        gate_b = sb("gate_b", [P, NE])
        scol = [sb(f"scol{b}", [P, T]) for b in range(2)]
        v_b = sb("v_b", [P, 1])
        PS = ctx.enter_context(nc.psum_tensor("PS", [128, 8 * BANK], f32))

        def slot(q):
            return PS[:, q * 2 * BANK:(q + 1) * 2 * BANK]

        full = [sem(f"slot{q}_full") for q in range(4)]
        free = [sem(f"slot{q}_free") for q in range(4)]
        act_step, dve_step, pool_step = sem("act_step"), sem("dve_step"), sem("pool_step")
        consts_ready = sem("consts_ready")
        ld_edges, ld_x, ld_gate, ld_rows = sem("ld_edges"), sem("ld_x"), sem("ld_gate"), sem("ld_rows")
        ld_w1, ld_w2 = sem("ld_w1"), sem("ld_w2")
        onehots_ready, onehots_used = sem("onehots_ready"), sem("onehots_used")
        cnt_ready, inv_ready, inv_stored = sem("cnt_ready"), sem("inv_ready"), sem("inv_stored")
        cidx_ready, evw_loaded, evw_ready = sem("cidx_ready"), sem("evw_loaded"), sem("evw_ready")
        idx_used = sem("idx_used")
        var_ready, std_ready, xn_ready, xT_ready = sem("var_ready"), sem("std_ready"), sem("xn_ready"), sem("xT_ready")
        h_ready, cols_ready, r_ready = sem("h_ready"), sem("cols_ready"), sem("r_ready")
        exps_ready, probs_ready, agg_taken = sem("exps_ready"), sem("probs_ready"), sem("agg_taken")
        elu_in, elu_exp = sem("elu_in"), sem("elu_exp")
        logits_in, logits_exp = sem("logits_in"), sem("logits_exp")
        deg_ready, deg_sqrt = sem("deg_ready"), sem("deg_sqrt")
        comb_ready, combw_ready = sem("comb_ready"), sem("combw_ready")
        act_done, inner_done = sem("act_done"), sem("inner_done")
        ld_f1, ld_f2 = [sem("ld_f1a"), sem("ld_f1b")], sem("ld_f2")
        ld_small = sem("ld_small")
        v_out, v_in, mat_out, mat_in = sem("v_out"), sem("v_in"), sem("mat_out"), sem("mat_in")
        rho_out, rho_in, green_out, green_in = sem("rho_out"), sem("rho_in"), sem("green_out"), sem("green_in")
        v_ready, mat_ready, rho_ready, green_ready = sem("v_ready"), sem("mat_ready"), sem("rho_ready"), sem("green_ready")
        specw_ready, layer_done = sem("specw_ready"), sem("layer_done")
        split_hi, split_lo = sem("split_hi"), sem("split_lo")
        raw_loaded = [sem("raw_loaded0"), sem("raw_loaded1")]
        folded, fold_used, folds_begun = sem("folded"), sem("fold_used"), sem("folds_begun")
        pres_ready, pos_ready = sem("pres_ready"), sem("pos_ready")
        xn_stored, inlist_ready, rows_ready = sem("xn_stored"), sem("inlist_ready"), sem("rows_ready")
        x_gathered = [[sem(f"x_gathered{b}_{j}") for j in range(RT)] for b in range(2)]
        z_stored = [[sem(f"z_stored{b}_{j}") for j in range(RT)] for b in range(2)]
        xhi_ready, xlo_ready = sem("xhi_ready"), sem("xlo_ready")
        zrow_ready, zrow_stored, z_begun, z_filled = sem("zrow_ready"), sem("zrow_stored"), sem("z_begun"), sem("z_filled")
        inlist_m_ready, rows_m_ready, x_m_gathered = sem("inlist_m_ready"), sem("rows_m_ready"), sem("x_m_gathered")
        xhi_m_ready, xlo_m_ready = sem("xhi_m_ready"), sem("xlo_m_ready")
        x_m_ready, z_m_stored, stores_begun = sem("x_m_ready"), sem("z_m_stored"), sem("stores_begun")
        rows_loaded = sem("rows_loaded")
        gathered = [sem(f"gathered{b}") for b in range(4)]
        msg_hi, msg_ready, msg_used, hot_ready = sem("msg_hi"), sem("msg_ready"), sem("msg_used"), sem("hot_ready")
        ld_root, ld_gcn = sem("ld_root"), sem("ld_gcn")
        h1_ready, xw_ready, xws_ready = sem("h1_ready"), sem("xw_ready"), sem("xws_ready")
        wa_ready, al_taken, weighted = sem("wa_ready"), sem("al_taken"), sem("weighted")
        earlier_ready = sem("earlier_ready")
        gathers_begun, maxima_begun = sem("gathers_begun"), sem("maxima_begun")
        out_stored = sem("out_stored")

        g = ExitStack()
        with g:
            negm = sb("negm", [P, T, N], f32, g)
            hx = sb("hx", [P, T, D + HEADS], f32, g)
            gw = [sb(f"gw{b}", [128, K, D], f32, g) for b in range(2)]
            arow = sb("arow", [128, 4, D], f32, g)
            brow = sb("brow", [P, 2, D], f32, g)
            al = sb("al", [P, T, 2, HEADS], f32, g)
            wa1 = sb("wa1", [128, K, 2, HEADS], f32, g)
            wa2 = sb("wa2", [128, K, 2, 1], f32, g)
            hcol = [sb(f"hcol{b}", [P, T, 2], f32, g) for b in range(2)]
            rcol = [sb(f"rcol{b}", [P, T, 3], f32, g) for b in range(2)]
            smax = sb("smax", [P, 4, T], f32, g)
            cidx = sb("cidx", [EP, 2, ET], u32, g)
            idxb = sb("idxb", [EP, 2, AHEAD], u32, g)
            evwb = sb("evwb", [EP, AHEAD], f32, g)
            zidxb = sb("zidxb", [EP, AHEAD], u32, g)
            zrow = sb("zrow", [P, T, REL], u32, g)
            further = sb("further", [P, T, REL], f32, g)
            ran = sb("ran", [P, 3, REL], f32, g)
            rel_row = sb("rel_row", [P, 3, REL], f32, g)
            inv = sb("inv", [P, T, REL], f32, g)
            with ExitStack() as edges:
                tmp = [sb(f"tmp{b}", [128, D], f32, edges) for b in range(2)]
                iota34 = sb("iota34", [EP, REL], i16, edges)
                eint = sb("eint", [EP, 3, ET], i32, edges)
                ef = sb("ef", [EP, 3, ET], f32, edges)
                hot_s = [sb(f"hot_s{b}", [EP, N], bf16, edges) for b in range(AHEAD)]
                hot_dr = [sb(f"hot_dr{b}", [EP, N + REL], bf16, edges) for b in range(AHEAD)]
                pres = sb("pres", [P, T, REL], f32, edges)
                before = sb("before", [P, P], f32, edges)
            e1 = [sb(f"e1_{b}", [P, T, N], f32, g) for b in range(2)]
            e2 = [sb(f"e2_{b}", [P, T, N], f32, g) for b in range(2)]
        g = ExitStack()
        with g:
            hT = sb("hT", [128, FK + 2, N], f32, g)
            fw1 = [sb(f"fw1_{b}", [128, K, 2 * F], f32, g) for b in range(2)]
            fw3 = [sb(f"fw3_{b}", [128, K, 2 * F], f32, g) for b in range(2)]
            fw2 = sb("fw2", [128, FK + 2, D], f32, g)
            combw = [sb(f"combw{b}", [P, T, 2 * F], f32, g) for b in range(2)]
            b1r = sb("b1r", [FK, 128], f32, g)
            b1T = sb("b1T", [128, FK], f32, g)
            b2r = sb("b2r", [NE, D], f32, g)
            combT = sb("combT", [NE, N], f32, g)
        g = ExitStack()
        with g:
            pad = sb("pad", [128, FK + 2, N], f32, g)
            pad2 = sb("pad2", [128, 2, K, 2 * F], f32, g)
            vch = sb("vch", [BC, BC], f32, g)
            ar = sb("ar", [BC, 2, BC], f32, g)
            ar2 = sb("ar2", [BC, BC, 2, 2], f32, g)
            S = sb("S", [BC, BC + 2, 8], f32, g)
            SW = sb("SW", [BC, 2, 8], f32, g)
            ml = sb("ml", [1, BC, 16], f32, g)
            mo = sb("mo", [1, BC, 2, 12], f32, g)
            rho = sb("rho", [1, BC + 1, 2, 2], f32, g)
            rhoo = sb("rhoo", [1, BC, 4], f32, g)
            mt = sb("mt", [1, 5, 2, 4], f32, g)
            rin = sb("rin", [BC, 2, 2], f32, g)
            nrin = sb("nrin", [BC, 2, 2], f32, g)
            sol = sb("sol", [BC, 2, BC + 1, 2], f32, g)
            dq = sb("dq", [BC, 6, 2, BC, 2], f32, g)
            green = sb("green", [BC, 2, BC], f32, g)
            v_col = sb("v_col", [P, T], f32, g)
        feats, bkrow, specw = hT[0:3, FK, :], fw2[0:3, FK, :], fw2[0:3, FK + 1, :]
        g = ExitStack()
        with g:
            raw = sb("raw", [128, K, D], f32, g)
            whi = [sb(f"whi{b}", [128, K, D], f32r, g) for b in range(2)]
            wlo = [sb(f"wlo{b}", [128, K, D], f32r, g) for b in range(2)]
            xg = [[sb(f"xg{b}_{j}", [128, D], f32, g) for j in range(RT)] for b in range(2)]
            xhi = [[sb(f"xhi{b}_{j}", [128, K, 128], f32r, g) for j in range(RT)] for b in range(2)]
            xlo = [[sb(f"xlo{b}_{j}", [128, K, 128], f32r, g) for j in range(RT)] for b in range(2)]
            xg_m = sb("xg_m", [128, D], f32, g)
            xhi_m = sb("xhi_m", [128, K, 128], f32r, g)
            xlo_m = sb("xlo_m", [128, K, 128], f32r, g)
            inlist_m = sb("inlist_m", [P, T, 128], bf16, g)
            row_m = sb("row_m", [128, 2], f32, g)
            xrow_m = sb("xrow_m", [128, 1], u32, g)
        zb = [[xn_all[:, 2 * b + j, :] for j in range(RT)] for b in range(2)]
        zb_m = xn_all[:, 4, :]
        g = ExitStack()
        with g:
            wroot = sb("wroot", [128, K, D], f32, g)
            wgcn = sb("wgcn", [128, K, D], f32, g)
            rbrow = sb("rbrow", [1, D], f32, g)
            gbrow = sb("gbrow", [P, D], f32, g)
            hotf = [sb(f"hotf{b}", [EP, N], f32r, g) for b in range(2)]
            zg = [sb(f"zg{b}", [EP, D], f32, g) for b in range(4)]
            mhi = [sb(f"mhi{b}", [EP, D], f32r, g) for b in range(2)]
            mlo = [sb(f"mlo{b}", [EP, D], f32r, g) for b in range(2)]
            zib = [sb(f"zib{b}", [EP, 1], u32, g) for b in range(4)]
            h1 = sb("h1", [P, T, D], f32, g)
            xws = sb("xws", [P, T, D], f32, g)
            gtmp = sb("gtmp", [P, D], f32, g)

        def beyond(eng, r, tile, skip):
            n = eng.value_load(rel_n[0:1, bass.ds(r, 1)], min_val=0, max_val=N)
            with eng.If(n > RT * 128):
                tile(RT)
                with eng.If(n > (RT + 1) * 128):
                    for j in range(RT + 1, RT + MORE):
                        tile(j)
                with eng.Else():
                    skip(MORE - 1)
            with eng.Else():
                skip(MORE)

        psT = lambda q: slot(q)[:, 0:T * 128].rearrange("p (t c) -> p t c", c=128)

        block = ctx.enter_context(nc.Block())

        @block.sync
        def _(sp):
            sp.dma_start(eint[:, 0, :], src.rearrange("(p j) -> p j", j=ET)).then_inc(ld_edges, 16)
            sp.dma_start(eint[:, 1, :], dst.rearrange("(p j) -> p j", j=ET)).then_inc(ld_edges, 16)
            sp.dma_start(eint[:, 2, :], etype.rearrange("(p j) -> p j", j=ET)).then_inc(ld_edges, 16)
            sp.dma_start(x_res[:, :, :], x.rearrange("(t p) d -> p t d", p=P)).then_inc(ld_x, 16)
            sp.dma_start(gw[0][:, :, :], w["L0_gnn_W1"].rearrange("(k p) n -> p k n", p=128)).then_inc(ld_w1, 16)
            for n, name in enumerate(("L0_gnn_a_src1", "L0_gnn_a_dst1", "L0_gnn_a_src2", "L0_gnn_a_dst2")):
                sp.dma_start(arow[:, n, :], w[name].rearrange("h c -> (h c)").partition_broadcast(128)).then_inc(ld_rows, 16)
            for n, name in enumerate(("L0_gnn_b1", "L0_gnn_b2")):
                sp.dma_start(brow[:, n, :], w[name].partition_broadcast(P)).then_inc(ld_rows, 16)
            sp.dma_start(gw[1][:, :, :], w["L0_gnn_W2"].rearrange("(k p) n -> p k n", p=128)).then_inc(ld_w2, 16)
            sp.dma_start(gate_sb[:, :, 0:NE], w["L0_ffn_gate_w"].rearrange("(k p) n -> p k n", p=128)).then_inc(ld_gate, 16)
            sp.dma_start(gate_sb[:, :, NE:NE + 1], w["L0_ffn_v_w"].rearrange("(k p n) -> p k n", p=128, n=1), allow_slow_non_contiguous=True).then_inc(ld_gate, 16)
            sp.dma_start(wr_sb[:, :, :], w["L1_ffn_Wr"].rearrange("(k p) n -> p k n", p=128)).then_inc(ld_gate, 16)
            sp.dma_start(gate_b[:, :], w["L0_ffn_gate_b"].partition_broadcast(P)).then_inc(ld_gate, 16)
            sp.dma_start(v_b[:, :], w["L0_ffn_v_b"].partition_broadcast(P)).then_inc(ld_gate, 16)
            sp.wait_ge(inv_ready, 1)
            sp.dma_start(inv_dram.rearrange("(t p r) o -> p t (r o)", p=P, r=REL), inv[:, :, :]).then_inc(inv_stored, 16)
            sp.dma_start(z_dram[FIRST:FIRST + FEW * 128, :], x[0:FEW * 128, :]).then_inc(z_begun, 16)
            sp.wait_ge(z_begun, 16)
            sp.wait_ge(zrow_ready, 1)
            sp.dma_start(zrow_dram.rearrange("(t p r) o -> p t (r o)", p=P, r=REL), zrow[:, :, :]).then_inc(zrow_stored, 16)
            total = sp.value_load(ran_before[0:1, REL:REL + 1], min_val=0, max_val=REL * MORE)
            with sp.If(total > FEW):
                for n in range(FEW, MANY, FEW):
                    rows = min(FEW, MANY - n) * 128
                    sp.dma_start(z_dram[FIRST + n * 128:FIRST + n * 128 + rows, :], x[0:rows, :]).then_inc(z_begun, 16)
                sp.wait_ge(z_begun, 16 * -(-MANY // FEW))
                sp.sem_inc(z_filled, 1)
            with sp.Else():
                sp.sem_inc(z_filled, 1)

            sp.wait_ge(inv_stored, 16)
            sp.wait_ge(evw_ready, 1)
            sp.wait_ge(layer_done, 1)
            sp.dma_start(b1r[:, :], w["L0_ffn_b1"].rearrange("e f -> (e f)").rearrange("(c p) -> c p", p=128)).then_inc(ld_small, 16)
            sp.dma_start(b2r[:, :], w["L0_ffn_b2"]).then_inc(ld_small, 16)
            sp.dma_start(specw[0:2], w["L0_ffn_out_w"]).then_inc(ld_small, 16)
            sp.dma_start(specw[2:3], w["L0_ffn_out_b"].rearrange("(a d) -> a d", a=1)).then_inc(ld_small, 16)
            sp.dma_start(bkrow, w["L0_ffn_bk_scale"].partition_broadcast(3)).then_inc(ld_small, 16)
            w1v = w["L0_ffn_w1"].rearrange("e (k p) f -> e p k f", p=128)

            def load_pair(buf, view, i, signal):
                for e in range(2):
                    sp.dma_start(buf[:, :, e * F:(e + 1) * F], view[2 * i + e, :, :, :]).then_inc(signal, 16)

            load_pair(fw1[0], w1v, 0, ld_f1[0])
            load_pair(fw1[1], w1v, 1, ld_f1[1])
            sp.dma_start(fw2[:, 0:FK, :], w["L0_ffn_w2"].rearrange("e f d -> (e f) d").rearrange("(c p) d -> p c d", p=128)).then_inc(ld_f2, 16)
            for i in (2, 3):
                sp.wait_ge(act_done, 1 + 3 * (i - 1))
                load_pair(fw1[i % 2], w1v, i, ld_f1[i % 2])
            sp.wait_ge(layer_done, 2)
            wv = w["L1_gnn_W_rel"].rearrange("r (k p) n -> r p k n", p=128)
            KH = K // 2

            def load_raw(r, first):
                for half in range(2):
                    if not first:
                        sp.wait_ge(split_lo, r * 2 + half - 1)
                    sp.dma_start(raw[:, half * KH:(half + 1) * KH, :],
                                 wv[r, :, half * KH:(half + 1) * KH, :]).then_inc(raw_loaded[half], 16)

            load_raw(0, True)
            sp.wait_ge(xn_ready, 4 * T)
            sp.dma_start(xn_dram.rearrange("(t p) d -> p t d", p=P), xn).then_inc(xn_stored, 16)
            with sp.Fori(1, REL) as r:
                load_raw(r, False)

            sp.wait_ge(layer_done, 3)
            sp.dma_start(wroot[:, :, :], w["L1_gnn_W_root"].rearrange("(k p) n -> p k n", p=128)).then_inc(ld_root, 16)
            sp.dma_start(rbrow[:, :], w["L1_gnn_b_rgcn"].rearrange("(a d) -> a d", a=1)).then_inc(ld_root, 16)
            sp.dma_start(wgcn[:, :, :], w["L1_gnn_W_gcn"].rearrange("(k p) n -> p k n", p=128)).then_inc(ld_gcn, 16)
            sp.dma_start(gbrow[:, :], w["L1_gnn_b_gcn"].partition_broadcast(P)).then_inc(ld_gcn, 16)

            sp.wait_ge(layer_done, 4)
            v1 = w["L1_ffn_w1"].rearrange("e (k p) f -> e p k f", p=128)
            v3 = w["L1_ffn_w3"].rearrange("e (k p) f -> e p k f", p=128)
            for i in range(NE // 2):
                if i >= 2:
                    sp.wait_ge(inner_done, FK + 3 * (i - 1))
                load_pair(fw1[i % 2], v1, i, ld_f1[i % 2])
                load_pair(fw3[i % 2], v3, i, ld_f1[i % 2])
                if i == 1:
                    sp.dma_start(fw2[:, 0:FK, :], w["L1_ffn_w2"].rearrange("e f d -> (e f) d").rearrange("(c p) d -> p c d", p=128)).then_inc(ld_f2, 16)
                    sp.dma_start(fw2[0:F // 2, FK:FK + 2, :], w["L1_ffn_s2"].rearrange("(c p) d -> p c d", c=2)).then_inc(ld_f2, 16)
            sp.wait_ge(inner_done, FK + 9)
            sp.dma_start(fw1[0][:, :, 0:F], w["L1_ffn_s1"].rearrange("(k p) f -> p k f", p=128)).then_inc(ld_f1[0], 16)
            sp.dma_start(fw3[0][:, :, 0:F], w["L1_ffn_s3"].rearrange("(k p) f -> p k f", p=128)).then_inc(ld_f1[0], 16)

            sp.wait_ge(layer_done, 5)
            sp.dma_start(out.rearrange("(t p) d -> p t d", p=P), x_res[:, :, :]).then_inc(out_stored, 16)
            sp.wait_ge(out_stored, 16)

        @block.gpsimd
        def _(pool):
            step = Track(pool, pool_step)
            step(pool.iota(iota16[:, :], [[1, T * 128]], base=0, channel_multiplier=0, allow_small_or_imprecise_dtypes=True))
            step(pool.iota(iota34[:, :], [[1, REL]], base=0, channel_multiplier=0, allow_small_or_imprecise_dtypes=True))
            step(pool.iota(rev[:, :], [[-1, NE]], base=NE, channel_multiplier=0, allow_small_or_imprecise_dtypes=True))
            step(pool.memset(ones[:, :], 1.0))
            step.do(pool.memset(ident[:, :], 0.0))
            step.do(pool.affine_select(out=ident[:, :], in_=ident[:, :], compare_op=ALU.not_equal, fill=1.0,
                                       base=0, pattern=[[-1, 128]], channel_multiplier=1))
            pool.sem_inc(consts_ready, 1)
            step(pool.iota(node_of[:, :, 0], [[0, T]], base=0, channel_multiplier=1, allow_small_or_imprecise_dtypes=True))
            step(pool.iota(node_of[:, :, 1], [[1, T]], base=0, channel_multiplier=0, allow_small_or_imprecise_dtypes=True))
            step(pool.iota(rel_row[:, 0, :], [[RT * 128, REL]], base=0, channel_multiplier=0, allow_small_or_imprecise_dtypes=True))
            step.do(pool.memset(before[:, :], 1.0))
            step.do(pool.affine_select(out=before[:, :], in_=before[:, :], compare_op=ALU.is_gt, fill=0.0,
                                       base=0, pattern=[[1, P]], channel_multiplier=-1))
            pool.sem_inc(consts_ready, 1)
            pool.wait_ge(ld_rows, 96)
            pool.sem_inc(fold_used, 2)
            for layer, ready in enumerate((ld_w1, ld_w2)):
                pool.wait_ge(ready, 16)
                with pool.Fori(0, K) as k:
                    for s in range(2):
                        pool.wait_ge(fold_used, k * 2 + s + 2 * K * layer + 1)
                        pool.sem_inc(folds_begun, 1)
                        pool.tensor_tensor(tmp[s][:, :], gw[layer][:, bass.ds(k, 1), :].rearrange("p o n -> p (o n)"),
                                           arow[:, 2 * layer + s, :], ALU.mult).then_inc(folded, 1)
            pool.wait_ge(inv_stored, 16)
            pool.wait_ge(zrow_stored, 16)
            pool.wait_ge(cidx_ready, 1)
            with step.turns(ET // AHEAD, 3) as j:
                step.do(pool.tensor_copy(idxb[:, :, :], cidx[:, :, bass.ds(j * AHEAD, AHEAD)]))
                pool.sem_inc(gathers_begun, 1)
                for n in range(AHEAD):
                    pool.indirect_dma_start(evwb[:, n:n + 1], None, inv_dram,
                                            bass.IndirectOffsetOnAxis(ap=idxb[:, 0, n:n + 1], axis=0)).then_inc(evw_loaded, 16)
                    pool.indirect_dma_start(zidxb[:, n:n + 1], None, zrow_dram,
                                            bass.IndirectOffsetOnAxis(ap=idxb[:, 1, n:n + 1], axis=0)).then_inc(rows_loaded, 16)
                pool.wait_ge(evw_loaded, j * (16 * AHEAD) + 16 * AHEAD)
                step(pool.tensor_copy(evw[:, bass.ds(j * AHEAD, AHEAD)], evwb[:, :]))
                pool.wait_ge(rows_loaded, j * (16 * AHEAD) + 16 * AHEAD)
                step.do(pool.tensor_copy(zidx[:, bass.ds(j * AHEAD, AHEAD)], zidxb[:, :]))
            pool.sem_inc(evw_ready, 1)
            pool.wait_ge(v_ready, 1)
            pool.dma_start(v_dram.rearrange("(t p) -> p t", p=P), v_col[:, :], allow_slow_non_contiguous=True).then_inc(v_out, 16)
            pool.wait_ge(v_out, 16)
            pool.dma_start(vch[:, :], v_dram.rearrange("(c t) -> c t", t=BC)).then_inc(v_in, 16)
            pool.wait_ge(mat_ready, 1)
            pool.dma_start(mat_dram, S[:, BC:BC + 2, :].rearrange("p a b -> p (a b)")).then_inc(mat_out, 16)
            pool.wait_ge(mat_out, 16)
            pool.dma_start(ml[:, :, :], mat_dram.rearrange("(a c) m -> a c m", a=1)).then_inc(mat_in, 16)
            pool.wait_ge(rho_ready, 1)
            pool.dma_start(rho_dram.rearrange("(a c) m -> a c m", a=1), rhoo[:, :, :]).then_inc(rho_out, 16)
            pool.wait_ge(rho_out, 16)
            pool.dma_start(rin[:, :, :].rearrange("p a b -> p (a b)"), rho_dram).then_inc(rho_in, 16)
            pool.wait_ge(green_ready, 1)
            pool.dma_start(green_dram.rearrange("r (c t) -> c r t", t=BC), green[:, :, :]).then_inc(green_out, 16)
            pool.wait_ge(green_out, 16)
            pool.dma_start(feats[0:2], green_dram).then_inc(green_in, 16)

            def gather_x(b, k):
                pool.wait_ge(rows_ready, 2 * k + b + 1)
                pool.sem_inc(gathers_begun, 1)
                for j in range(RT):
                    pool.indirect_dma_start(xg[b][j][:, :], None, xn_dram,
                                            bass.IndirectOffsetOnAxis(ap=xrow[:, b, j:j + 1], axis=0)).then_inc(x_gathered[b][j], 16)

            def tile_m(r, j):
                n = r * MORE + (j - RT) + 1
                pool.wait_ge(rows_m_ready, n)
                pool.sem_inc(gathers_begun, 1)
                pool.indirect_dma_start(xg_m[:, :], None, xn_dram,
                                        bass.IndirectOffsetOnAxis(ap=xrow_m[:, :], axis=0)).then_inc(x_m_gathered, 16)
                ran = pool.value_load(ran_before[0:1, bass.ds(r, 1)], min_val=0, max_val=REL * MORE)
                pool.wait_ge(x_m_gathered, ran * 16 + 16 * (j - RT + 1))
                pool.sem_inc(x_m_ready, 1)

            def skip_m(n):
                pool.sem_inc(x_m_ready, n)

            pool.wait_ge(layer_done, 2)
            pool.wait_ge(xn_stored, 16)
            pool.wait_ge(pos_ready, 1)
            gather_x(0, 0)
            gather_x(1, 0)

            def relation(i, b, more):
                if more:
                    gather_x(b, i + 1)
                beyond(pool, i * 2 + b, lambda j: tile_m(i * 2 + b, j), skip_m)

            with pool.Fori(0, REL // 2 - 1) as i:
                for b in range(2):
                    relation(i, b, True)
            for b in range(2):
                relation(REL // 2 - 1, b, False)

            pool.wait_ge(layer_done, 3)

            def gather_z(z_rows):
                with pool.Fori(0, ET // 4) as j:
                    for b in range(4):
                        pool.wait_ge(idx_used, j * 4 + b + 1)
                        pool.sem_inc(gathers_begun, 1)
                        pool.indirect_dma_start(zg[b][:, :], None, z_rows,
                                                bass.IndirectOffsetOnAxis(ap=zib[b][:, :], axis=0)).then_inc(gathered[b], 16)

            total = pool.value_load(ran_before[0:1, REL:REL + 1], min_val=0, max_val=REL * MORE)
            with pool.If(total > FEW):
                gather_z(z_dram)
            with pool.Else():
                gather_z(z_dram[0:FIRST + FEW * 128, :])
            pool.wait_ge(layer_done, 4)
            for b in range(2):
                step(pool.memset(combw[b][:, :, :], 1.0))
            step.sync()
            for i in range(T):
                m = combw[i // 3][:, :, :].rearrange("p t f -> p (t f)")[:, i % 3 * N:(i % 3 + 1) * N]
                step(pool.affine_select(out=m, in_=m, compare_op=ALU.is_gt, fill=0.0,
                                        base=i * P, pattern=[[-1, N]], channel_multiplier=1))
            step.sync()
            pool.sem_inc(earlier_ready, 1)

        @block.scalar
        def _(act):
            step = Track(act, act_step)

            def evict(stage, q, k, dst_ap, src_ap, signal=None):
                act.wait_ge(full[q], BEFORE[stage][q] + k + 1)
                ins = act.activation(dst_ap, src_ap, ACT.Copy)
                step.do(ins)
                act.sem_inc(free[q], 1)
                if signal is not None:
                    act.sem_inc(signal, 1)

            def turn(stage):
                for k in range(K):
                    evict(stage, k % 4, k // 4, xT[:, k, :].rearrange("p (t c) -> p t c", c=P), psT(k % 4)[:, :, 0:P], xT_ready)

            def root(ready, k, ap_out, ap_in):
                act.wait_ge(ready, k)
                step.do(act.activation(ap_out, ap_in, ACT.Sqrt))
                act.sem_inc(std_ready, 1)

            def sides(q):
                return slot(q).rearrange("p (b c) -> p b c", c=BANK)[0:P, :, 0:HALF]

            def product(stage, dst_of, signal):
                for t in range(T):
                    to = dst_of(t)
                    of = sides(t % 4)
                    if stage in ("w1", "w2"):
                        act.wait_ge(al_taken, t + 1 + T * (stage == "w2"))
                    evict(stage, t % 4, t // 4, to, of.rearrange("p b (h c) -> p b h c", c=HC) if stage == "w1" else of, signal)

            for layer, (wa, heads) in enumerate(((wa1, HEADS), (wa2, 1))):
                with act.Fori(0, K) as k:
                    for s in range(2):
                        act.wait_ge(folded, k * 2 + s + 1 + 2 * K * layer)
                        for h in range(heads):
                            o = tmp[s][:, h * (D // heads):(h + 1) * (D // heads)]
                            ins = act.activation(o, o, ACT.Copy, accum_out=wa[:, bass.ds(k, 1), s, h:h + 1].rearrange("p o h -> p (o h)"))
                        ins.then_inc(fold_used, 1)
                if layer == 0:
                    root(var_ready, 1, rstd[:, :], t5[:, 0, :])
            act.wait_ge(fold_used, 4 * K + 2)
            act.sem_inc(wa_ready, 1)
            flat = counts[:, :, :].rearrange("p t n -> p (t n)")
            for q in range(3):
                evict("edges", q, 0, flat[:, q * 2 * BANK:(q + 1) * 2 * BANK], slot(q)[0:P, :])
            act.sem_inc(cnt_ready, 1)
            turn("turn1")
            act.wait_ge(deg_ready, 1)
            step.do(act.activation(dinv[:, :], t5[:, 7, :], ACT.Sqrt))
            act.sem_inc(deg_sqrt, 1)
            hv = hx[:, :, :].rearrange("p t (h c) -> p t h c", c=HC + 1)
            product("w1", lambda t: hv[:, t, :, 0:HC].rearrange("p (b h) c -> p b h c", b=2), h_ready)

            def exps(b, h, k1, k2):
                if not isinstance(h, int) or h >= 2:
                    act.wait_ge(agg_taken, h - 1)
                act.wait_ge(full[1], k1)
                act.wait_ge(full[2], k2)
                for t in range(T):
                    for q, to, bias in ((1, e1[b], hcol[b][:, t, 0:1]), (2, e2[b], rcol[b][:, t, 0:1])):
                        ins = act.activation(to[:, t, :].rearrange("p (t c) -> p t c", c=P), psT(q)[0:P, :, 0:P],
                                             ACT.Exp, bias=bias)
                        if t == T - 1:
                            step.do(ins)
                            act.sem_inc(free[q], 1)
                    if t < T - 1:
                        ins.then_inc(exps_ready, 1)
                act.sem_inc(exps_ready, 1)

            def exps1(b, h):
                exps(b, h, h + BEFORE["heads1"][1] + 1, h + BEFORE["heads1"][2] + 1)

            for b in range(2):
                exps1(b, b)
            with step.turns(HEADS // 2 - 1, 4) as i:
                for b in range(2):
                    exps1(b, i * 2 + 2 + b)
            act.wait_ge(elu_in, 1)
            for t in range(T):
                step(act.activation(hx[:, t, 0:D], xn[:, t, :], ACT.Exp))
            step.sync()
            act.sem_inc(elu_exp, 1)
            turn("turn2")
            product("w2", lambda t: hx[:, t, 0:D].rearrange("p (b c) -> p b c", b=2), h_ready)
            exps(0, HEADS, BEFORE["heads2"][1] + 1, BEFORE["heads2"][2] + 1)

            def router(n):
                act.wait_ge(logits_in, n)
                step.do(act.activation(small[:, 1, :, :], small[:, 0, :, :], ACT.Exp))
                act.sem_inc(logits_exp, 1)

            root(var_ready, 2, rstd[:, :], t5[:, 0, :])
            turn("turn3")
            router(1)
            act.wait_ge(full[1], BEFORE["route1"][1] + 1)
            step.do(act.activation(combT[:, :].rearrange("p (t c) -> p t c", c=P), psT(1)[0:NE, :, 0:P], ACT.Copy))
            act.sem_inc(free[1], 1)
            act.wait_ge(full[2], BEFORE["route1"][2] + 1)
            step.do(act.activation(b1T[:, :], slot(2)[:, 0:FK], ACT.Copy))
            act.sem_inc(free[2], 1)
            act.sem_inc(act_done, 1)

            def gelus(c, b, k):
                act.wait_ge(full[b], BEFORE["inner1"][b] + 1 + k)
                step.do(act.activation(hT[:, c, :], slot(b)[:, 0:N], ACT.Gelu_apprx_tanh, bias=b1T[:, c:c + 1]))
                act.sem_inc(free[b], 1)
                act.sem_inc(act_done, 1)

            for c in range(FK):
                gelus(c, c % 2, c // 2)

            root(var_ready, 3, rstd[:, :], t5[:, 0, :])
            turn("turn4")
            KH = K // 2

            def w_high(i, b):
                for half in range(2):
                    act.wait_ge(raw_loaded[half], (i * 2 + b) * 16 + 16)
                    step.do(act.activation(whi[b][:, half * KH:(half + 1) * KH, :],
                                           raw[:, half * KH:(half + 1) * KH, :], ACT.Copy))
                    act.sem_inc(split_hi, 1)

            def columns_of(q):
                return slot(q)[:, 0:K * 128].rearrange("p (k c) -> p k c", k=K)

            def x_high(i, b, j):
                r = i * 2 + b
                if j == 1 or isinstance(r, int) and r == 0:
                    act.wait_ge(full[j], BEFORE["relations"][j] + 1 + r)
                else:
                    act.wait_ge(full[0], BEFORE["relations"][0] + 1 - 2 * MORE + r * (1 + 2 * MORE))
                step.do(act.activation(xhi[b][j][:, :, :], columns_of(j), ACT.Copy))
                act.sem_inc(xhi_ready, 1)

            def z_out(i, b, j, first):
                r = i * 2 + b
                act.wait_ge(full[2 + j], BEFORE["relations"][2 + j] + 1 + (r * (1 + MORE) if j == 0 else r))
                if not first:
                    act.wait_ge(z_stored[b][j], i * 16)
                step.do(act.activation(zb[b][j].rearrange("p (b c) -> p b c", b=2),
                                       slot(2 + j).rearrange("p (b c) -> p b c", c=BANK)[:, :, 0:HALF], ACT.Copy))
                act.sem_inc(free[2 + j], 1)
                act.sem_inc(stores_begun, 1)
                act.dma_start(z_dram[bass.ds(r * (RT * 128) + j * 128, 128), :], zb[b][j]).then_inc(z_stored[b][j], 16)

            def tile_m(r, j, turned):
                n = r * MORE + (j - RT)
                act.wait_ge(full[0], BEFORE["relations"][0] + 1 + turned + r * (1 + 2 * MORE) + 2 * (j - RT) + 2)
                step.do(act.activation(xhi_m[:, :, :], columns_of(0), ACT.Copy))
                act.sem_inc(xhi_m_ready, 1)
                act.wait_ge(full[2], BEFORE["relations"][2] + r * (1 + MORE) + 1 + (j - RT) + 1)
                step.do(act.activation(zb_m.rearrange("p (b c) -> p b c", b=2),
                                       slot(2).rearrange("p (b c) -> p b c", c=BANK)[:, :, 0:HALF], ACT.Copy))
                act.sem_inc(free[2], 1)
                ran = act.value_load(ran_before[0:1, bass.ds(r, 1)], min_val=0, max_val=MANY - (j - RT + 1))
                act.dma_start(z_dram[bass.ds(ran * 128 + (FIRST + (j - RT) * 128), 128), :], zb_m).then_inc(z_m_stored, 16)
                act.wait_ge(z_m_stored, ran * 16 + 16 * (j - RT + 1))
                act.sem_inc(stores_begun, 1)

            def skip_m(n):
                act.sem_inc(act_step, 2 * n)
                act.sem_inc(xhi_m_ready, n)
                act.sem_inc(free[2], n)

            def relation(i, b, more, first):
                if more:
                    w_high(i + b, 1 - b)
                for j in range(RT):
                    if more:
                        x_high(i + b, 1 - b, j)
                    z_out(i, b, j, first)
                n = step.n
                beyond(act, i * 2 + b, lambda j: tile_m(i * 2 + b, j, int(more)), skip_m)
                assert step.n - n == 2 * MORE

            act.wait_ge(z_filled, 1)
            act.wait_ge(xn_stored, 16)
            act.wait_ge(pos_ready, 1)
            w_high(0, 0)
            for j in range(RT):
                x_high(0, 0, j)
            for b in range(2):
                relation(0, b, True, True)
            with act.Fori(1, REL // 2 - 1) as i:
                start = step.n
                A_STEPS = 2 * (2 + 2 * RT + 2 * MORE)
                step.extra = (i - 1) * A_STEPS
                for b in range(2):
                    relation(i, b, True, False)
                step.extra = None
            assert step.n - start == A_STEPS, step.n - start
            step.n = start + A_STEPS * (REL // 2 - 2)
            for b in range(2):
                relation(REL // 2 - 1, b, b == 0, False)
            for b in range(2):
                for j in range(RT):
                    act.wait_ge(z_stored[b][j], REL // 2 * 16)
            act.sem_inc(layer_done, 1)

            def high(i, b, z):
                act.wait_ge(gathered[z], i * 16 + 16)
                act.wait_ge(hot_ready, i * 4 + z + 1)
                step.do(act.activation(mhi[b][:, :], zg[z][:, :], ACT.Copy, scale=gtmp[:, z:z + 1]))
                act.sem_inc(msg_hi, 1)

            with step.turns(ET // 4, 4) as i:
                for z in range(4):
                    high(i, z % 2, z)

            turn("turn5")
            product("wgcn", lambda t: xws[:, t, :].rearrange("p (b c) -> p b c", b=2), xw_ready)

            root(var_ready, 4, rstd[:, :], t5[:, 0, :])
            turn("turn6")
            router(2)
            for c in range(FK):
                act.wait_ge(full[0], BEFORE["inner2"][0] + 1 + c)
                step.do(act.activation(hT[:, c, :], slot(0)[:, 0:N], ACT.Silu))
                act.sem_inc(free[0], 1)
                act.sem_inc(act_done, 1)
            for c in range(2):
                act.wait_ge(full[0], BEFORE["shared"][0] + 1 + c)
                step.do(act.activation(hT[0:F // 2, FK + c, :], slot(0)[0:F // 2, 0:N], ACT.Silu))
                act.sem_inc(free[0], 1)
                act.sem_inc(act_done, 1)

        @block.vector
        def _(dve):
            step = Track(dve, dve_step)
            do = step.do

            def tt(o, a, b, op):
                return dve.tensor_tensor(o, a, b, op)

            def ts(o, a, s1, s2, op0, op1=None):
                return dve.tensor_scalar(o, a, s1, s2, op0) if op1 is None else dve.tensor_scalar(o, a, s1, s2, op0, op1)

            def free_slot(q):
                dve.sem_inc(free[q], 1)

            def norm(n, source):
                for t in range(T):
                    for s in range(2):
                        step(dve.bn_stats(stats[:, t, s, :], source[:, t, s * HALF:(s + 1) * HALF]))
                step.sync()
                for t in range(T):
                    step(dve.bn_aggr(mv[:, t, :], stats[:, t, :, :].rearrange("p a b -> p (a b)")))
                step.sync()
                do(ts(t5[:, 0, :], mv[:, :, 1], EPS, None, ALU.add))
                dve.sem_inc(var_ready, 1)
                dve.wait_ge(std_ready, n)
                do(dve.reciprocal(rstd[:, :], rstd[:, :]))
                for t in range(T):
                    do(ts(xn[:, t, :], source[:, t, :], mv[:, t, 0:1], rstd[:, t:t + 1], ALU.subtract, ALU.mult))
                    dve.sem_inc(xn_ready, 1)

            dve.wait_ge(ld_edges, 48)
            dve.wait_ge(consts_ready, 1)
            do(dve.tensor_copy(ef[:, :, :], eint[:, :, :]))
            step(dve.tensor_copy(dstf[:, :], ef[:, 1, :]))
            step(dve.scalar_tensor_tensor(cidx[:, 1, :], ef[:, 0, :], float(REL), ef[:, 2, :], ALU.mult, ALU.add))
            do(dve.scalar_tensor_tensor(cidx[:, 0, :], ef[:, 1, :], float(REL), ef[:, 2, :], ALU.mult, ALU.add))
            dve.sem_inc(cidx_ready, 1)

            def onehots(j, b, first):
                if not first:
                    dve.wait_ge(onehots_used, j + b - AHEAD + 1)
                dve.tensor_scalar(hot_s[b][:, :], iota16[:, 0:N], ef[:, 0, bass.ds(j + b, 1)], None, ALU.is_equal)
                dve.tensor_scalar(hot_dr[b][:, 0:N], iota16[:, 0:N], ef[:, 1, bass.ds(j + b, 1)], None, ALU.is_equal)
                dve.tensor_scalar(hot_dr[b][:, N:N + REL], iota34[:, :], ef[:, 2, bass.ds(j + b, 1)], None,
                                  ALU.is_equal).then_inc(onehots_ready, 1)

            for b in range(AHEAD):
                onehots(0, b, True)
            with dve.Fori(1, ET // AHEAD // 2) as i:
                for b in range(AHEAD):
                    onehots(i * AHEAD, b, False)
            dve.wait_ge(ld_x, 16)
            norm(1, x_res)
            with dve.Fori(ET // AHEAD // 2, ET // AHEAD) as i:
                for b in range(AHEAD):
                    onehots(i * AHEAD, b, False)
            dve.wait_ge(full[3], BEFORE["edges"][3] + 1)
            flat = counts[:, :, :].rearrange("p t n -> p (t n)")
            rest = T * (N + REL) - 6 * BANK
            do(dve.tensor_copy(flat[:, 6 * BANK:T * (N + REL)], slot(3)[0:P, 0:rest]))
            dve.sem_inc(cnt_ready, 1)
            step(ts(inv[:, :, :].rearrange("p t r -> p (t r)"), slot(3)[0:P, rest:rest + T * REL], 1.0, None, ALU.max))
            step.sync()
            free_slot(3)
            dve.wait_ge(cnt_ready, 2)
            do(ts(pres[:, :, :], counts[:, :, N:N + REL], 1.0, None, ALU.min))
            dve.sem_inc(pres_ready, 1)
            do(dve.reciprocal(inv[:, :, :], inv[:, :, :]))
            dve.sem_inc(inv_ready, 1)
            for t in range(T):
                dve.wait_ge(full[t % 4], BEFORE["mask"][t % 4] + t // 4 + 1)
                if t == 0:
                    do(ts(t5[:, 7, :], slot(0)[0:P, 700:700 + T], 1.0, None, ALU.add))
                    dve.sem_inc(deg_ready, 1)
                    do(ts(t5[:, 6, :], t5[:, 7, :], 1.0, -2e30, ALU.is_gt, ALU.mult))
                    do(ts(t5[:, 6, :], t5[:, 6, :], 1e30, None, ALU.add))
                do(ts(negm[:, t, :].rearrange("p (t c) -> p t c", c=P), psT(t % 4)[0:P, :, 0:P], 0.0, t5[:, 6, t:t + 1],
                      ALU.is_equal, ALU.mult))
                free_slot(t % 4)
            dve.wait_ge(full[1], BEFORE["ranks"][1] + 1)
            do(dve.scalar_tensor_tensor(pos[:, :, :].rearrange("p t r -> p (t r)"), slot(1)[0:P, 0:T * REL], 1.0,
                                        pres[:, :, :].rearrange("p t r -> p (t r)"), ALU.add, ALU.mult))
            step(ts(pos[:, :, :], pos[:, :, :], -1.0, None, ALU.add))
            do(dve.tensor_copy(rel_n[:, :], slot(1)[0:1, BANK:BANK + REL]))
            do(dve.tensor_copy(ran[:, 0, :], slot(1)[0:P, BANK:BANK + REL]))
            free_slot(1)
            do(ts(ran[:, 1, :], ran[:, 0, :], float((RT + 1) * 128), float(MORE - 1), ALU.is_gt, ALU.mult))
            do(dve.scalar_tensor_tensor(ran[:, 2, :], ran[:, 0, :], float(RT * 128), ran[:, 1, :], ALU.is_gt, ALU.add))
            do(dve.tensor_copy(ran[:, 0, :], ran[:, 2, :]))
            n, a, b = 1, 0, 1
            while n < REL:
                step(dve.tensor_copy(ran[:, b, 0:n], ran[:, a, 0:n]))
                do(tt(ran[:, b, n:REL], ran[:, a, n:REL], ran[:, a, 0:REL - n], ALU.add))
                n, a, b = 2 * n, b, a
            do(dve.tensor_copy(ran_before[:, REL:REL + 1], ran[0:1, a, REL - 1:REL]))
            do(tt(ran[:, a, :], ran[:, a, :], ran[:, 2, :], ALU.subtract))
            do(dve.tensor_copy(ran_before[:, 0:REL], ran[0:1, a, :]))
            dve.sem_inc(pos_ready, 1)
            dve.wait_ge(consts_ready, 2)
            do(dve.scalar_tensor_tensor(rel_row[:, 1, :], ran[:, a, :], 128.0, rel_row[:, 0, :], ALU.mult, ALU.subtract))
            do(ts(rel_row[:, 1, :], rel_row[:, 1, :], float(FIRST - RT * 128), None, ALU.add))
            do(ts(further[:, :, :], pos[:, :, :], float(RT * 128), None, ALU.is_ge))
            do(tt(further[:, :, :], further[:, :, :], rel_row[:, 1, :].unsqueeze(1).broadcast_to([P, T, REL]), ALU.mult))
            do(tt(further[:, :, :], further[:, :, :], rel_row[:, 0, :].unsqueeze(1).broadcast_to([P, T, REL]), ALU.add))
            do(tt(further[:, :, :], further[:, :, :], pos[:, :, :], ALU.add))
            do(ts(zrow[:, :, :], further[:, :, :], 0.0, None, ALU.max))
            dve.sem_inc(zrow_ready, 1)
            dve.wait_ge(deg_sqrt, 1)
            do(dve.reciprocal(dinv[:, :], dinv[:, :]))

            hv = hx[:, :, :].rearrange("p t (h c) -> p t h c", c=HC + 1)
            do(dve.memset(hv[:, :, :, HC:HC + 1], 1.0))
            for t in range(T):
                dve.wait_ge(full[t % 4], BEFORE["w1"][t % 4] + t // 4 + 1)
                do(dve.tensor_copy(al[:, t, :, :].rearrange("p s h -> p (s h)"),
                                   slot(t % 4)[0:P, BANK + HALF:BANK + HALF + 2 * HEADS]))
                dve.sem_inc(al_taken, 1)

            def columns(b, h):
                do(dve.tensor_copy(hcol[b][:, :, :], al[:, :, :, bass.ds(h, 1)].rearrange("p t s o -> p t (s o)")))
                do(ts(rcol[b][:, :, 0], hcol[b][:, :, 0], 0.2, None, ALU.mult))
                dve.sem_inc(cols_ready, 1)

            def maxima(b, k):
                dve.wait_ge(full[0], k)
                dve.sem_inc(maxima_begun, 1)
                for i in range(T):
                    step(dve.tensor_tensor_reduce(e1[b][:, i, :].rearrange("p (t c) -> p t c", c=P),
                                                  negm[:, i, :].rearrange("p (t c) -> p t c", c=P), psT(0)[0:P, :, 0:P],
                                                  1.0, -3e38, ALU.add, ALU.max, smax[:, 0, i:i + 1]))
                step.sync()
                free_slot(0)
                do(tt(smax[:, 1, :], smax[:, 0, :], hcol[b][:, :, 1], ALU.add))
                do(dve.scalar_tensor_tensor(smax[:, 2, :], smax[:, 1, :], 0.2, smax[:, 1, :], ALU.mult, ALU.max))
                step(tt(rcol[b][:, :, 1], hcol[b][:, :, 1], smax[:, 2, :], ALU.subtract))
                do(dve.scalar_tensor_tensor(rcol[b][:, :, 2], hcol[b][:, :, 1], 0.2, smax[:, 2, :], ALU.mult, ALU.subtract))
                dve.sem_inc(r_ready, 1)

            def weigh(b, h):
                for t in range(T):
                    if isinstance(h, int) and h == HEADS:
                        dve.wait_ge(exps_ready, h * T + t + 1)
                    do(tt(e2[b][:, t, :], e1[b][:, t, :], e2[b][:, t, :], ALU.max))
                    do(dve.scalar_tensor_tensor(e2[b][:, t, :], e2[b][:, t, :], 1.0, cnt[:, t, :], ALU.min, ALU.mult))
                dve.sem_inc(probs_ready, 1)

            def head_sums(h, k):
                dve.wait_ge(full[3], k)
                o = slot(3)[0:P, 0:T * (HC + 1)].rearrange("p (t c) -> p t c", c=HC + 1)
                do(ts(smax[:, 3, :], o[:, :, HC], 1e-16, None, ALU.add))
                do(dve.reciprocal(smax[:, 3, :], smax[:, 3, :]))
                do(tt(xn[:, :, bass.ds(h * HC, HC)], o[:, :, 0:HC], smax[:, 3, :].unsqueeze(2).broadcast_to([P, T, HC]), ALU.mult))
                free_slot(3)
                dve.sem_inc(agg_taken, 1)

            def head(b, h, more):
                dve.wait_ge(exps_ready, h * T + T)
                if more:
                    columns(b, h + 2)
                weigh(b, h)
                if more:
                    maxima(b, h + 2 + BEFORE["heads1"][0] + 1)
                head_sums(h, h + BEFORE["heads1"][3] + 1)

            HEAD_STEPS = 2 + 2 * T + T + 4 + 3
            dve.wait_ge(xT_ready, K)
            dve.wait_ge(inv_stored, 16)
            for b in range(2):
                columns(b, b)
                maxima(b, b + BEFORE["heads1"][0] + 1)
            with step.turns(HEADS // 2 - 1, 2 * HEAD_STEPS) as i:
                for b in range(2):
                    head(b, i * 2 + b, True)
            for b in range(2):
                head(b, HEADS - 2 + b, False)

            for t in range(T):
                do(tt(xn[:, t, :], xn[:, t, :], brow[:, 0, :], ALU.add))
            dve.sem_inc(elu_in, 1)
            dve.wait_ge(elu_exp, 1)
            for t in range(T):
                do(ts(hx[:, t, 0:D], hx[:, t, 0:D], 1.0, -1.0, ALU.min, ALU.add))
                do(dve.scalar_tensor_tensor(xn[:, t, :], xn[:, t, :], 0.0, hx[:, t, 0:D], ALU.max, ALU.add))
                dve.sem_inc(xn_ready, 1)
            do(dve.memset(hx[:, :, D:D + 1], 1.0))
            for t in range(T):
                dve.wait_ge(full[t % 4], BEFORE["w2"][t % 4] + t // 4 + 1)
                do(dve.tensor_copy(al[:, t, :, 0:1].rearrange("p s h -> p (s h)"),
                                   slot(t % 4)[0:P, BANK + HALF:BANK + HALF + 2]))
                dve.sem_inc(al_taken, 1)

            def agg2():
                for i in range(T):
                    q = (3, 0)[i % 2]
                    base = BEFORE["heads2"][q] + (1 if q == 0 else 0)
                    dve.wait_ge(full[q], base + i // 2 + 1)
                    do(ts(smax[:, 1, 0:1], slot(q)[0:P, BANK + HALF:BANK + HALF + 1], 1e-16, None, ALU.add))
                    do(dve.reciprocal(smax[:, 1, 0:1], smax[:, 1, 0:1]))
                    do(dve.scalar_tensor_tensor(xn[:, i, :].rearrange("p (b c) -> p b c", b=2),
                                                slot(q).rearrange("p (b c) -> p b c", c=BANK)[0:P, :, 0:HALF],
                                                smax[:, 1, 0:1],
                                                x_res[:, i, :].rearrange("p (b c) -> p b c", b=2), ALU.mult, ALU.add))
                    free_slot(q)
                    do(tt(x_res[:, i, :], xn[:, i, :], brow[:, 1, :], ALU.add))

            columns(0, 0)
            maxima(0, BEFORE["heads2"][0] + 1)
            weigh(0, HEADS)
            agg2()
            dve.wait_ge(evw_ready, 1)
            dve.sem_inc(layer_done, 1)

            norm(2, x_res)

            def route(n, stage, bias):
                dve.wait_ge(full[0], BEFORE[stage][0] + 1)
                lg = slot(0)[0:P, 0:T * 16].rearrange("p (t c) -> p t c", c=16)
                L, E1, pr, k1, oh1, p2, oh2 = (small[:, i, :, :] for i in range(7))
                wide = lambda a: a.unsqueeze(2).broadcast_to([P, T, NE])
                if bias:
                    do(tt(pr, lg[:, :, 0:NE], gate_b[:, :].unsqueeze(1).broadcast_to([P, T, NE]), ALU.add))
                    do(ts(v_col[:, :], lg[:, :, NE], v_b[:, 0:1], -3.0, ALU.add, ALU.max))
                    do(ts(v_col[:, :], v_col[:, :], 3.0, -2.0, ALU.min, ALU.add))
                    dve.sem_inc(v_ready, 1)
                else:
                    do(dve.tensor_copy(pr, lg[:, :, 0:NE]))
                free_slot(0)
                do(dve.tensor_reduce(t5[:, 1, :], pr, AX.X, ALU.max))
                do(tt(L, pr, wide(t5[:, 1, :]), ALU.subtract))
                dve.sem_inc(logits_in, 1)
                dve.wait_ge(logits_exp, n)
                do(dve.tensor_reduce(t5[:, 1, :], E1, AX.X, ALU.add))
                do(dve.reciprocal(t5[:, 1, :], t5[:, 1, :]))
                do(tt(pr, E1, wide(t5[:, 1, :]), ALU.mult))
                for m, source, hot in ((2, pr, oh1), (3, p2, oh2)):
                    do(dve.tensor_reduce(t5[:, m, :], source, AX.X, ALU.max))
                    do(tt(k1, source, wide(t5[:, m, :]), ALU.is_equal))
                    do(tt(k1, k1, rev[:, :].unsqueeze(1).broadcast_to([P, T, NE]), ALU.mult))
                    do(dve.tensor_reduce(t5[:, 4, :], k1, AX.X, ALU.max))
                    do(tt(hot, k1, wide(t5[:, 4, :]), ALU.is_equal))
                    if m == 2:
                        do(dve.scalar_tensor_tensor(p2, hot, -2.0, pr, ALU.mult, ALU.add))
                do(tt(t5[:, 4, :], t5[:, 2, :], t5[:, 3, :], ALU.add))
                if not bias:
                    do(ts(t5[:, 4, :], t5[:, 4, :], 1e-9, None, ALU.max))
                do(dve.reciprocal(t5[:, 4, :], t5[:, 4, :]))
                do(tt(asg[:, :, :], oh1, oh2, ALU.add))
                do(tt(comb1[:, :, :], pr, asg[:, :, :], ALU.mult))
                do(tt(comb1[:, :, :], comb1[:, :, :], wide(t5[:, 4, :]), ALU.mult))

            dve.wait_ge(ld_gate, 80)
            route(1, "route1", True)
            dve.sem_inc(comb_ready, 1)

            def widen(i, b):
                do(dve.tensor_copy(combw[b][:, :, :].rearrange("p t (e f) -> p t e f", e=2),
                                   comb1[:, :, 2 * i:2 * i + 2].unsqueeze(3).broadcast_to([P, T, 2, F])))
                dve.sem_inc(combw_ready, 1)

            def spectral_steps():
                dve.wait_ge(v_in, 16)
                step(dve.tensor_copy(ar[:, 0, :], vch[:, :]))
                do(dve.tensor_copy(ar[:, 1, :], vch[:, ::-1]))
                step(ts(ar2[:, :, :, 0], ar[:, :, :].rearrange("p d t -> p t d"), -1.0, None, ALU.mult))
                step(dve.tensor_copy(ar2[:, :, :, 1], ar[:, :, :].rearrange("p d t -> p t d")))
                do(dve.memset(S[:, 0:2, :], 0.0))
                S5 = S[:, :, :].rearrange("p t (d k c) -> p t d k c", d=2, k=2)
                step(dve.memset(S5[:, 0, :, 1, 0:1], 1.0))
                do(dve.memset(S5[:, 1, :, 0, 0:1], 1.0))
                SW4 = SW[:, :, :].rearrange("p a (d k c) -> p a d k c", d=2, k=2)
                for t in range(BC):
                    step(tt(SW[:, 0, :], S[:, t + 1, :], S[:, t, :], ALU.add))
                    do(tt(SW4[:, 1, :, :, :], S5[:, t + 1, :, :, ::-1],
                          ar2[:, t, :, :].unsqueeze(2).broadcast_to([BC, 2, 2, 2]), ALU.mult))
                    do(tt(S[:, t + 2, :], SW[:, 0, :], SW[:, 1, :], ALU.add))
                    yield
                dve.sem_inc(mat_ready, 1)
                dve.wait_ge(mat_in, 16)
                m6 = ml[:, :, :].rearrange("o c (m d k r) -> o c m d k r", m=2, d=2, k=2)
                mo6 = mo[:, :, :, :].rearrange("o c d (k m r) -> o c d k m r", k=3, m=2)
                for d in range(2):
                    s = slice(None, None, -1) if d else slice(None)
                    for m in range(2):
                        step(dve.tensor_copy(mo6[:, :, d, 0, m, :], m6[:, s, m, d, 0, :]))
                        step(dve.tensor_copy(mo6[:, :, d, 1, m, :], m6[:, s, m, d, 1, :]))
                        step(ts(mo6[:, :, d, 2, m, 0], m6[:, s, m, d, 1, 1], -1.0, None, ALU.mult))
                        step(dve.tensor_copy(mo6[:, :, d, 2, m, 1], m6[:, s, m, d, 1, 0]))
                do(dve.memset(rho[:, 0:1, :, :], 0.0))
                for c in range(BC - 1):
                    cur = rho[:, c, :, :]
                    M4 = lambda k: mo[:, c, :, 4 * k:4 * k + 4]
                    step(tt(mt[:, 0, :, :], M4(1), cur[:, :, 0:1].broadcast_to([1, 2, 4]), ALU.mult))
                    do(tt(mt[:, 1, :, :], M4(2), cur[:, :, 1:2].broadcast_to([1, 2, 4]), ALU.mult))
                    do(tt(mt[:, 0, :, :], mt[:, 0, :, :], M4(0), ALU.add))
                    do(tt(mt[:, 0, :, :], mt[:, 0, :, :], mt[:, 1, :, :], ALU.add))
                    num, den = mt[:, 0, :, 0:2], mt[:, 0, :, 2:4]
                    nd = mt[:, 0, :, :].rearrange("o d (m r) -> o d m r", m=2)
                    step(tt(mt[:, 2, :, :].rearrange("o d (m r) -> o d m r", m=2), nd,
                            den.unsqueeze(2).broadcast_to([1, 2, 2, 2]), ALU.mult))
                    do(tt(mt[:, 3, :, 0:2], num, den[:, :, ::-1], ALU.mult))
                    step(dve.tensor_reduce(mt[:, 4, :, 0:3:2], mt[:, 2, :, :].rearrange("o d (m r) -> o d m r", m=2), AX.X, ALU.add))
                    do(tt(mt[:, 4, :, 1:2], mt[:, 3, :, 1:2], mt[:, 3, :, 0:1], ALU.subtract))
                    do(dve.reciprocal(mt[:, 4, :, 3:4], mt[:, 4, :, 2:3]))
                    do(tt(rho[:, c + 1, :, :], mt[:, 4, :, 0:2], mt[:, 4, :, 3:4].broadcast_to([1, 2, 2]), ALU.mult))
                    yield
                step(dve.tensor_copy(rhoo[:, :, 0:2], rho[:, 0:BC, 0, :]))
                do(dve.tensor_copy(rhoo[:, :, 2:4], rho[:, 0:BC, 1, :][:, ::-1, :]))
                dve.sem_inc(rho_ready, 1)
                dve.wait_ge(rho_in, 16)
                do(ts(nrin[:, :, :], rin[:, :, :], -1.0, None, ALU.mult))
                for d in range(2):
                    al_, be = S5[:, 1:, d, 0, :], S5[:, 1:, d, 1, :]
                    do(dve.scalar_tensor_tensor(sol[:, d, :, :], be, rin[:, d, 0:1], al_, ALU.mult, ALU.add))
                    step(dve.scalar_tensor_tensor(sol[:, d, :, 0], be[:, :, 1], nrin[:, d, 1:2], sol[:, d, :, 0], ALU.mult, ALU.add))
                    do(dve.scalar_tensor_tensor(sol[:, d, :, 1], be[:, :, 0], rin[:, d, 1:2], sol[:, d, :, 1], ALU.mult, ALU.add))
                for d in range(2):
                    X, Y = sol[:, d, 1:, :], sol[:, d, 0:BC, :]
                    q = lambda i: dq[:, i, d, :, :]
                    step(tt(q(0), X, Y, ALU.mult))
                    step(tt(q(1), X, Y[:, :, ::-1], ALU.mult))
                    do(tt(q(2), Y, Y, ALU.mult))
                    step(tt(q(3)[:, :, 0], q(1)[:, :, 1], q(1)[:, :, 0], ALU.subtract))
                    step(dve.scalar_tensor_tensor(q(3)[:, :, 1], q(0)[:, :, 0], -1.0, q(0)[:, :, 1], ALU.mult, ALU.subtract))
                    do(dve.tensor_reduce(q(4)[:, :, 0], q(2), AX.X, ALU.add))
                    do(dve.reciprocal(q(4)[:, :, 1], q(4)[:, :, 0]))
                    do(tt(q(5), q(3), q(4)[:, :, 1:2].broadcast_to([BC, BC, 2]), ALU.mult))
                do(tt(dq[:, 0, 0, :, :], dq[:, 5, 0, :, :], dq[:, 5, 1, ::-1, :], ALU.add))
                step(tt(dq[:, 0, 0, :, 0], dq[:, 0, 0, :, 0], ar[:, 0, :], ALU.subtract))
                do(ts(dq[:, 0, 0, :, 1], dq[:, 0, 0, :, 1], 1.0, None, ALU.add))
                do(tt(dq[:, 1, 0, :, :], dq[:, 0, 0, :, :], dq[:, 0, 0, :, :], ALU.mult))
                do(dve.tensor_reduce(dq[:, 2, 0, :, 0], dq[:, 1, 0, :, :], AX.X, ALU.add))
                do(dve.reciprocal(dq[:, 2, 0, :, 1], dq[:, 2, 0, :, 0]))
                step(tt(green[:, 0, :], dq[:, 0, 0, :, 0], dq[:, 2, 0, :, 1], ALU.mult))
                do(dve.scalar_tensor_tensor(green[:, 1, :], dq[:, 0, 0, :, 1], -1.0, dq[:, 2, 0, :, 1], ALU.mult, ALU.mult))
                do(ts(green[:, :, :], green[:, :, :], 10.0, -10.0, ALU.min, ALU.max))
                do(dve.memset(feats, 1.0))
                dve.sem_inc(green_ready, 1)
                dve.wait_ge(ld_small, 80)
                do(tt(specw, specw, bkrow, ALU.mult))
                dve.sem_inc(specw_ready, 1)


            spectral = spectral_steps()
            widen(0, 0)
            widen(1, 1)
            for c in range(FK):
                dve.wait_ge(act_done, c + 2)
                dve.wait_ge(full[2 + c % 2], BEFORE["inner1"][2 + c % 2] + c // 2 + 1)
                do(tt(hT[:, c, :], hT[:, c, :], slot(2 + c % 2)[:, 0:N], ALU.mult))
                free_slot(2 + c % 2)
                dve.sem_inc(inner_done, 1)
                if c % 3 == 2 and c // 3 + 2 < NE // 2:
                    widen(c // 3 + 2, c // 3 % 2)
                for _ in range(3):
                    next(spectral, None)
            for _ in spectral:
                pass

            def add_result(stage):
                for t in range(T):
                    q = t % 4
                    dve.wait_ge(full[q], BEFORE[stage][q] + t // 4 + 1)
                    xr = x_res[:, t, :].rearrange("p (b c) -> p b c", b=2)
                    do(tt(xr, slot(q).rearrange("p (b c) -> p b c", c=BANK)[0:P, :, 0:HALF], xr, ALU.add))
                    free_slot(q)

            def in_list(r, b):
                do(dve.tensor_copy(poscol[:, :], pos[:, :, bass.ds(r, 1)].rearrange("p t o -> p (t o)")))
                for t in range(T):
                    step(dve.tensor_scalar(inlist[b][:, t, :], iota16[:, 0:RT * 128], poscol[:, t:t + 1], None, ALU.is_equal))
                step.sync()
                dve.sem_inc(inlist_ready, 1)

            def rows(q, b):
                L = slot(q)[:, LIST:LIST + 2 * RT].rearrange("p (j c) -> p j c", c=2)
                do(dve.tensor_copy(node[:, :], L[:, :, 0]))
                do(dve.scalar_tensor_tensor(xrow[:, b, :], L[:, :, 1], float(P), node[:, :], ALU.mult, ALU.add))
                dve.sem_inc(rows_ready, 1)

            dve.wait_ge(consts_ready, 2)
            for b in range(2):
                in_list(b, b)
            for b in range(2):
                dve.wait_ge(full[b], BEFORE["lists"][b] + 1)
                rows(b, b)
                free_slot(b)
            add_result("outer1")
            dve.sem_inc(layer_done, 1)

            norm(3, x_res)
            KH = K // 2

            def w_low(i, b):
                for half in range(2):
                    dve.wait_ge(split_hi, (i * 2 + b) * 2 + half + 1)
                    s = slice(half * KH, (half + 1) * KH)
                    do(tt(wlo[b][:, s, :], raw[:, s, :], whi[b][:, s, :].bitcast(f32), ALU.subtract))
                    dve.sem_inc(split_lo, 1)

            def columns_of(q):
                return slot(q)[:, 0:K * 128].rearrange("p (k c) -> p k c", k=K)

            def x_low(i, b, j):
                dve.wait_ge(xhi_ready, (i * 2 + b) * RT + j + 1)
                do(tt(xlo[b][j][:, :, :], columns_of(j), xhi[b][j][:, :, :].bitcast(f32), ALU.subtract))
                dve.sem_inc(xlo_ready, 1)

            def tile_m(r, j, turned):
                n = r * MORE + (j - RT)
                for t in range(T):
                    step(dve.tensor_scalar(inlist_m[:, t, :], iota16[:, j * 128:(j + 1) * 128], poscol[:, t:t + 1], None, ALU.is_equal))
                step.sync()
                dve.sem_inc(inlist_m_ready, 1)
                job = BEFORE["relations"][0] + 1 + turned + r * (1 + 2 * MORE) + 2 * (j - RT)
                dve.wait_ge(full[0], job + 1)
                do(dve.tensor_copy(row_m[:, :], slot(0)[:, LIST:LIST + 2]))
                do(dve.scalar_tensor_tensor(xrow_m[:, :], row_m[:, 1:2], float(P), row_m[:, 0:1], ALU.mult, ALU.add))
                free_slot(0)
                dve.sem_inc(rows_m_ready, 1)
                dve.wait_ge(xhi_m_ready, n + 1)
                do(tt(xlo_m[:, :, :], columns_of(0), xhi_m[:, :, :].bitcast(f32), ALU.subtract))
                free_slot(0)
                dve.sem_inc(xlo_m_ready, 1)

            M_STEPS = T + 3

            def skip_m(n):
                dve.sem_inc(dve_step, M_STEPS * n)
                dve.sem_inc(inlist_m_ready, n)
                dve.sem_inc(rows_m_ready, n)
                dve.sem_inc(xlo_m_ready, n)
                dve.sem_inc(free[0], 2 * n)

            def relation(i, b, listed, more):
                if listed:
                    in_list(i * 2 + b + 2, b)
                if more:
                    w_low(i + b, 1 - b)
                    x_low(i + b, 1 - b, 0)
                if listed:
                    rows(0, b)
                if more:
                    free_slot(0)
                    x_low(i + b, 1 - b, 1)
                    free_slot(1)

                def tile_first(j):
                    if j == RT:
                        step(dve.tensor_copy(poscol[:, :], pos[:, :, bass.ds(i * 2 + b, 1)].rearrange("p t o -> p (t o)")))
                        step.sync()
                    tile_m(i * 2 + b, j, int(more))

                n = step.n
                beyond(dve, i * 2 + b, tile_first, lambda n: (skip_m(n), dve.sem_inc(dve_step, 1) if n == MORE else None))
                assert step.n - n == M_STEPS * MORE + 1, step.n - n

            w_low(0, 0)
            for j in range(RT):
                x_low(0, 0, j)
                free_slot(j)
            for b in range(2):
                relation(0, b, True, True)
            with dve.Fori(1, REL // 2 - 1) as i:
                start = step.n
                V_STEPS = 2 * (6 + 2 + 2 + 2 + M_STEPS * MORE + 1)
                step.extra = (i - 1) * V_STEPS
                for b in range(2):
                    relation(i, b, True, True)
                step.extra = None
            assert step.n - start == V_STEPS, step.n - start
            step.n = start + V_STEPS * (REL // 2 - 2)
            for b in range(2):
                relation(REL // 2 - 1, b, False, b == 0)

            dve.wait_ge(layer_done, 3)

            def message(j, z, first, more=True):
                b = z % 2
                if not first:
                    dve.wait_ge(msg_used, j + z - 1)
                step(dve.tensor_copy(gtmp[:, z:z + 1], evw[:, bass.ds(j + z, 1)]))
                do(dve.tensor_scalar(hotf[b][:, :], iota16[:, 0:N], dstf[:, bass.ds(j + z, 1)], None, ALU.is_equal))
                dve.sem_inc(hot_ready, 1)
                dve.wait_ge(msg_hi, j + z + 1)
                do(dve.scalar_tensor_tensor(mlo[b][:, :], zg[z][:, :], gtmp[:, z:z + 1], mhi[b][:, :].bitcast(f32),
                                            ALU.mult, ALU.subtract))
                dve.sem_inc(msg_ready, 1)
                if more:
                    do(dve.tensor_copy(zib[z][:, :], zidx[:, bass.ds(j + z + 4, 1)]))
                    dve.sem_inc(idx_used, 1)

            for z in range(4):
                step(dve.tensor_copy(zib[z][:, :], zidx[:, z:z + 1]))
            step.sync()
            dve.sem_inc(idx_used, 4)
            for z in range(4):
                message(0, z, z < 2)
            with step.turns(ET // 4 - 2, 16) as i:
                for z in range(4):
                    message(i * 4 + 4, z, False)
            for z in range(4):
                message(ET - 4, z, False, False)
            for q in range(4):
                dve.wait_ge(full[q], BEFORE["messages"][q] + 1)
            do(dve.tensor_copy(h1[:, :, :], PS[0:P, 0:T * D].rearrange("p (t d) -> p t d", d=D)))
            for q in range(4):
                free_slot(q)
            dve.sem_inc(h1_ready, 1)
            for t in range(T):
                do(tt(cnt[:, t, t * P:(t + 1) * P], cnt[:, t, t * P:(t + 1) * P], ident[0:P, 0:P], ALU.add))
                dve.wait_ge(xw_ready, t + 1)
                do(ts(xws[:, t, :], xws[:, t, :], dinv[:, t:t + 1], None, ALU.mult))
                dve.sem_inc(xws_ready, 1)
            dve.wait_ge(ld_gcn, 32)
            for t in range(T):
                q = t % 4
                dve.wait_ge(full[q], BEFORE["gcn"][q] + t // 4 + 1)
                xr = x_res[:, t, :].rearrange("p (b c) -> p b c", b=2)
                do(dve.scalar_tensor_tensor(xr, slot(q).rearrange("p (b c) -> p b c", c=BANK)[0:P, :, 0:HALF],
                                            dinv[:, t:t + 1], xr, ALU.mult, ALU.add))
                free_slot(q)
                do(tt(x_res[:, t, :], x_res[:, t, :], gbrow[:, :], ALU.add))
            dve.sem_inc(layer_done, 1)

            norm(4, x_res)
            route(2, "route2", False)
            score = small[:, 7, :, :]
            do(dve.scalar_tensor_tensor(score, asg[:, :, :], -1.0, comb1[:, :, :], ALU.add, ALU.add))
            dve.wait_ge(earlier_ready, 1)
            def mask(i):
                return combw[i // 3][:, :, :].rearrange("p t f -> p (t f)")[:, i % 3 * N:(i % 3 + 1) * N]\
                    .rearrange("p (t c) -> p t c", c=P)

            compared = combw[1][:, :, :].rearrange("p t f -> p (t f)")[:, 2 * N:3 * N].rearrange("p (t c) -> p t c", c=P)

            def rank(e):
                do(dve.tensor_copy(scol[e % 2][:, :], score[:, :, e]))
                dve.sem_inc(cols_ready, 1)
                dve.wait_ge(full[3], BEFORE["inner2"][3] + e + 1)
                row = psT(3)[0:P, :, 0:P]
                for i in range(T):
                    own = scol[e % 2][:, i:i + 1]
                    do(dve.tensor_scalar(compared, row, own, None, ALU.is_gt, ALU.add, accum_out=small[:, 8, i, e:e + 1]))
                    do(dve.scalar_tensor_tensor(compared, row, own, mask(i), ALU.is_equal, ALU.mult,
                                                accum_out=small[:, 9, i, e:e + 1]))
                free_slot(3)

            def weight(c):
                dve.wait_ge(full[2], BEFORE["inner2"][2] + c + 1)
                do(tt(hT[:, c, :], hT[:, c, :], slot(2)[:, 0:N], ALU.mult))
                free_slot(2)
                dve.sem_inc(weighted, 1)
                if c % 3 == 2 and c // 3 + 2 < NE // 2:
                    widen(c // 3 + 2, c // 3 % 2)

            for c in range(FK):
                if c < NE:
                    rank(c)
                if c == NE:
                    do(tt(small[:, 8, :, :], small[:, 8, :, :], small[:, 9, :, :], ALU.add))
                    do(ts(small[:, 8, :, :], small[:, 8, :, :], float(CAP), None, ALU.is_lt))
                    do(tt(comb1[:, :, :], comb1[:, :, :], small[:, 8, :, :], ALU.mult))
                    widen(0, 0)
                    widen(1, 1)
                dve.wait_ge(act_done, 1 + FK + c + 1)
                dve.wait_ge(full[1], BEFORE["inner2"][1] + c + 1)
                do(tt(hT[:, c, :], hT[:, c, :], slot(1)[:, 0:N], ALU.mult))
                free_slot(1)
                dve.sem_inc(inner_done, 1)
                if c > NE:
                    weight(c - NE - 1)
            for c in range(FK - NE - 1, FK):
                weight(c)
            for c in range(2):
                dve.wait_ge(act_done, 1 + 2 * FK + c + 1)
                dve.wait_ge(full[1], BEFORE["shared"][1] + c + 1)
                do(tt(hT[0:F // 2, FK + c, :], hT[0:F // 2, FK + c, :], slot(1)[0:F // 2, 0:N], ALU.mult))
                free_slot(1)
                dve.sem_inc(inner_done, 1)
            add_result("outer2")
            dve.sem_inc(layer_done, 1)

        @block.tensor
        def _(pe):
            def take(stage, q, k):
                n = k + BEFORE[stage][q]
                if not isinstance(n, int) or n > 0:
                    pe.wait_ge(free[q], n)

            def piece(o, c0, n):
                while n:
                    m = min(n, BANK - c0 % BANK)
                    yield o, c0, m
                    c0, o, n = c0 + m, o + m, n - m

            pe.wait_ge(consts_ready, 1)

            def count(b, start):
                for i in range(T):
                    for o, c, m in piece(0, i * (N + REL), N + REL):
                        pe.matmul(PS[0:P, c:c + m], hot_s[b][:, i * P:(i + 1) * P], hot_dr[b][:, o:o + m],
                                  start=start and c % BANK == 0, stop=False, skip_group_check=True)
                for i in range(T):
                    c = T * (N + REL) + i * REL
                    last = pe.matmul(PS[0:P, c:c + REL], hot_dr[b][:, i * P:(i + 1) * P], hot_dr[b][:, N:N + REL],
                                     start=False, stop=False, skip_group_check=True)
                return last

            for b in range(AHEAD):
                pe.wait_ge(onehots_ready, b + 1)
                count(b, b == 0).then_inc(onehots_used, 1)
            with pe.Fori(1, ET // AHEAD) as i:
                for b in range(AHEAD):
                    pe.wait_ge(onehots_ready, i * AHEAD + b + 1)
                    count(b, False).then_inc(onehots_used, 1)
            pe.wait_ge(onehots_used, ET)
            for q in range(4):
                pe.sem_inc(full[q], 1)

            def turn(stage, source, ready):
                ready()
                for k in range(K):
                    take(stage, k % 4, k // 4)
                    for t in range(T):
                        mm = pe.transpose(psT(k % 4)[:, t, 0:P], source[:, t, k * 128:(k + 1) * 128], ident[0:P, 0:P])
                    mm.then_inc(full[k % 4], 1)

            def product(stage, weights, turns_done, extra=None):
                pe.wait_ge(xT_ready, turns_done * K)
                for t in range(T):
                    take(stage, t % 4, t // 4)
                    for k in range(K):
                        for s in range(2):
                            mm = pe.matmul(slot(t % 4)[0:P, s * BANK:s * BANK + HALF], xT[:, k, t * P:(t + 1) * P],
                                           weights[:, k, s * HALF:(s + 1) * HALF], start=(k == 0), stop=(k == K - 1))
                    if extra is not None:
                        n = extra.shape[2] * extra.shape[3]
                        for k in range(K):
                            mm = pe.matmul(slot(t % 4)[0:P, BANK + HALF:BANK + HALF + n], xT[:, k, t * P:(t + 1) * P],
                                           extra[:, k, :, :].rearrange("p s h -> p (s h)"), start=(k == 0), stop=(k == K - 1))
                    mm.then_inc(full[t % 4], 1)

            def spread(q, column):
                for t in range(T):
                    mm = pe.matmul(psT(q)[0:P, t, 0:P], column(t).broadcast_to([P, P]), ident[0:P, 0:P],
                                   start=True, stop=True)
                mm.then_inc(full[q], 1)

            turn("turn1", xn, lambda: pe.wait_ge(xn_ready, T))

            pe.wait_ge(cnt_ready, 2)
            for i in range(T):
                take("mask", i % 4, i // 4)
                for t in range(T):
                    mm = pe.transpose(psT(i % 4)[0:P, t, 0:P], cnt[:, t, i * P:(i + 1) * P], ident[0:P, 0:P])
                if i == 0:
                    for j in range(T):
                        for t in range(T):
                            mm = pe.matmul(slot(0)[0:P, 700 + j:701 + j], cnt[:, t, j * P:(j + 1) * P], ones[0:P, 0:1],
                                           start=(t == 0), stop=(t == T - 1))
                mm.then_inc(full[i % 4], 1)
            pe.wait_ge(pres_ready, 1)
            pe.wait_ge(consts_ready, 2)
            take("ranks", 1, 0)
            for i in range(T):
                for t in range(i + 1):
                    pe.matmul(slot(1)[0:P, i * REL:(i + 1) * REL], before[:, :] if t == i else ones[0:P, 0:P], pres[:, t, :],
                              start=(t == 0), stop=(t == i))
            for t in range(T):
                mm = pe.matmul(slot(1)[0:P, BANK:BANK + REL], ones[0:P, 0:P], pres[:, t, :], start=(t == 0), stop=(t == T - 1))
            mm.then_inc(full[1], 1)

            pe.wait_ge(ld_w1, 16)
            pe.wait_ge(wa_ready, 1)
            product("w1", gw[0], 1, wa1)

            def source_row(stage, b, h, k):
                pe.wait_ge(cols_ready, h + 1)
                take(stage, 0, k)
                spread(0, lambda t: hcol[b][:, t, 0:1])

            def target_rows(stage, b, h, k):
                pe.wait_ge(r_ready, h + 1)
                for q in (1, 2):
                    take(stage, q, k)
                    spread(q, lambda t: rcol[b][:, t, q:q + 1])

            def head_product(b, h):
                take("heads1", 3, h)
                pe.wait_ge(probs_ready, h + 1)
                for i in range(T):
                    for t in range(T):
                        mm = pe.matmul(slot(3)[0:P, i * (HC + 1):(i + 1) * (HC + 1)], e2[b][:, t, i * P:(i + 1) * P],
                                       hx[:, t, bass.ds(h * (HC + 1), HC + 1)], start=(t == 0), stop=(t == T - 1))
                mm.then_inc(full[3], 1)

            for b in range(2):
                source_row("heads1", b, b, b)
                target_rows("heads1", b, b, b)
            with pe.Fori(0, HEADS // 2 - 1) as i:
                for b in range(2):
                    source_row("heads1", b, i * 2 + 2 + b, i * 2 + 2 + b)
                    head_product(b, i * 2 + b)
                    target_rows("heads1", b, i * 2 + 2 + b, i * 2 + 2 + b)
            for b in range(2):
                head_product(b, HEADS - 2 + b)

            turn("turn2", xn, lambda: pe.wait_ge(xn_ready, 2 * T))
            pe.wait_ge(ld_w2, 16)
            product("w2", gw[1], 2, wa2)
            source_row("heads2", 0, HEADS, 0)
            target_rows("heads2", 0, HEADS, 0)
            pe.wait_ge(probs_ready, HEADS + 1)
            for i in range(T):
                q = (3, 0)[i % 2]
                take("heads2", q, i // 2 + (1 if q == 0 else 0))
                for t in range(T):
                    for s in range(2):
                        n = HALF + s
                        mm = pe.matmul(slot(q)[0:P, s * BANK:s * BANK + n], e2[0][:, t, i * P:(i + 1) * P],
                                       hx[:, t, s * HALF:s * HALF + n], start=(t == 0), stop=(t == T - 1))
                mm.then_inc(full[q], 1)

            turn("turn3", xn, lambda: pe.wait_ge(xn_ready, 3 * T))

            def logits(stage, weights, n, turns_done):
                pe.wait_ge(xT_ready, turns_done * K)
                take(stage, 0, 0)
                for t in range(T):
                    for k in range(K):
                        mm = pe.matmul(slot(0)[0:P, 16 * t:16 * t + n], xT[:, k, t * P:(t + 1) * P], weights[:, k, :],
                                       start=(k == 0), stop=(k == K - 1))
                mm.then_inc(full[0], 1)

            pe.wait_ge(ld_gate, 80)
            logits("route1", gate_sb, NE + 1, 3)
            pe.wait_ge(comb_ready, 1)
            take("route1", 1, 0)
            for t in range(T):
                mm = pe.transpose(psT(1)[0:NE, t, 0:P], comb1[:, t, :], ident[0:P, 0:P])
            mm.then_inc(full[1], 1)
            pe.wait_ge(ld_small, 80)
            take("route1", 2, 0)
            pe.transpose(slot(2)[:, 0:FK], b1r[:, :], ident[0:FK, 0:FK]).then_inc(full[2], 1)

            def inner(dst_ps, weights, c, rows=128):
                for k in range(K):
                    for o, n in ((0, BANK), (BANK, N - BANK)):
                        mm = pe.matmul(dst_ps[0:rows, o:o + n], weights[:, k, c * rows:(c + 1) * rows],
                                       xT[:, k, o:o + n], start=(k == 0), stop=(k == K - 1))
                return mm

            def weights_row(q, b, c):
                for t in range(T):
                    for o, p0, n in piece(0, t * P, P):
                        mm = pe.matmul(slot(q)[:, p0:p0 + n], combw[b][:, t, c * 128:(c + 1) * 128],
                                       ident[0:P, o:o + n], start=True, stop=True)
                mm.then_inc(full[q], 1)

            LAG = 1
            for n in range(FK + LAG):
                if n < FK:
                    c, i, b = n, n // 3, n // 3 % 2
                    pe.wait_ge(ld_f1[b], 32 * (i // 2 + 1))
                    take("inner1", c % 2, c // 2)
                    inner(slot(c % 2), fw1[b], c % 3).then_inc(full[c % 2], 1)
                if n >= LAG:
                    c, i, b = n - LAG, (n - LAG) // 3, (n - LAG) // 3 % 2
                    take("inner1", 2 + c % 2, c // 2)
                    pe.wait_ge(combw_ready, i + 1)
                    weights_row(2 + c % 2, b, c % 3)

            def outer(stage, chunks, after):
                pe.wait_ge(ld_f2, 16 if stage == "outer1" else 48)
                for first, end in ((0, 4), (4, 5)):
                    for t in range(first, end):
                        take(stage, t % 4, t // 4)
                        for c, rows in chunks:
                            for s in range(2):
                                mm = pe.matmul(slot(t % 4)[0:P, s * BANK:s * BANK + HALF], hT[0:rows, c, t * P:(t + 1) * P],
                                               fw2[0:rows, c, s * HALF:(s + 1) * HALF], start=(c == 0),
                                               stop=(after is None and c == chunks[-1][0]))
                        if after is None:
                            mm.then_inc(full[t % 4], 1)
                    if after is not None:
                        for t in range(first, end):
                            after(t)

            def spectral(t):
                if t == 0:
                    pe.wait_ge(green_in, 16)
                    pe.wait_ge(specw_ready, 1)
                for s in range(2):
                    o = slot(t % 4)[0:P, s * BANK:s * BANK + HALF]
                    pe.matmul(o, combT[:, t * P:(t + 1) * P], b2r[:, s * HALF:(s + 1) * HALF], start=False, stop=False)
                    mm = pe.matmul(o, feats[:, t * P:(t + 1) * P], specw[:, s * HALF:(s + 1) * HALF],
                                   start=False, stop=True)
                mm.then_inc(full[t % 4], 1)

            pe.wait_ge(act_done, 1)
            pe.wait_ge(inner_done, FK)
            def list_rows(q, hot, j0, n):
                for j in range(n):
                    for t in range(T):
                        mm = pe.matmul(slot(q)[:, LIST + 2 * j:LIST + 2 * j + 2], hot[:, t, (j0 + j) * 128:(j0 + j + 1) * 128],
                                       node_of[:, t, :], start=(t == 0), stop=(t == T - 1))
                return mm

            for b in range(2):
                pe.wait_ge(inlist_ready, b + 1)
                take("lists", b, 0)
                list_rows(b, inlist[b], 0, RT).then_inc(full[b], 1)
            outer("outer1", [(c, 128) for c in range(FK)], spectral)

            turn("turn4", xn, lambda: pe.wait_ge(xn_ready, 4 * T))
            def turn_rows(q, rows_of):
                for k in range(K):
                    mm = pe.transpose(slot(q)[:, k * 128:(k + 1) * 128], rows_of[:, k * 128:(k + 1) * 128], ident[:, :])
                mm.then_inc(full[q], 1)

            def take_r(q, n):
                pe.wait_ge(free[q], BEFORE["relations"][q] + n)

            def relation_product(q, hi, lo, b):
                for k in range(K):
                    for part, (a, wt) in enumerate(((hi, whi[b]), (hi, wlo[b]), (lo, whi[b]))):
                        for s in range(2):
                            mm = pe.matmul(slot(q)[:, s * BANK:s * BANK + HALF], a[:, k, :],
                                           wt[:, k, s * HALF:(s + 1) * HALF],
                                           start=(k == 0 and part == 0), stop=(k == K - 1 and part == 2))
                mm.then_inc(full[q], 1)

            def tile_m(r, b, j, turned):
                n = r * MORE + (j - RT) + 1
                job = 1 + turned + r * (1 + 2 * MORE) + 2 * (j - RT)
                pe.wait_ge(inlist_m_ready, n)
                take_r(0, job)
                list_rows(0, inlist_m, 0, 1).then_inc(full[0], 1)
                pe.wait_ge(x_m_ready, n)
                take_r(0, job + 1)
                turn_rows(0, xg_m)
                pe.wait_ge(xlo_m_ready, n)
                take_r(2, r * (1 + MORE) + 1 + (j - RT))
                relation_product(2, xhi_m, xlo_m, b)

            def relation(i, b, listed, more):
                r = i * 2 + b
                if more:
                    if listed:
                        pe.wait_ge(inlist_ready, r + 3)
                    take_r(0, 1 + r * (1 + 2 * MORE))
                    if listed:
                        list_rows(0, inlist[b], 0, RT)
                    pe.wait_ge(x_gathered[1 - b][0], (i + b) * 16 + 16)
                    turn_rows(0, xg[1 - b][0])
                pe.wait_ge(split_lo, r * 2 + 2)
                pe.wait_ge(xlo_ready, r * RT + 1)
                take_r(2, r * (1 + MORE))
                relation_product(2, xhi[b][0], xlo[b][0], b)
                if more:
                    take_r(1, 1 + r)
                    pe.wait_ge(x_gathered[1 - b][1], (i + b) * 16 + 16)
                    turn_rows(1, xg[1 - b][1])
                pe.wait_ge(xlo_ready, r * RT + 2)
                take_r(3, r)
                relation_product(3, xhi[b][1], xlo[b][1], b)

                def skip_m(n):
                    tiles = MORE - n
                    pe.wait_ge(full[0], BEFORE["relations"][0] + 1 + int(more) + r * (1 + 2 * MORE) + 2 * tiles)
                    pe.sem_inc(full[0], 2 * n)
                    pe.wait_ge(full[2], BEFORE["relations"][2] + r * (1 + MORE) + 1 + tiles)
                    pe.sem_inc(full[2], n)

                beyond(pe, r, lambda j: tile_m(r, b, j, int(more)), skip_m)

            for j in range(RT):
                take_r(j, 0)
                pe.wait_ge(x_gathered[0][j], 16)
                turn_rows(j, xg[0][j])
            with pe.Fori(0, REL // 2 - 1) as i:
                for b in range(2):
                    relation(i, b, True, True)
            for b in range(2):
                relation(REL // 2 - 1, b, False, b == 0)

            for q in range(4):
                take("messages", q, 0)

            def scatter(b, start):
                for part in (mhi[b], mlo[b]):
                    for i in range(T):
                        for o, c, m in piece(0, i * D, D):
                            mm = pe.matmul(PS[0:P, c:c + m], hotf[b][:, i * P:(i + 1) * P], part[:, o:o + m],
                                           start=start and part is mhi[b] and c % BANK == 0, stop=False, skip_group_check=True)
                mm.then_inc(msg_used, 1)

            for b in range(2):
                pe.wait_ge(msg_ready, b + 1)
                scatter(b, b == 0)
            with pe.Fori(1, ET // 2) as i:
                for b in range(2):
                    pe.wait_ge(msg_ready, i * 2 + b + 1)
                    scatter(b, False)
            pe.wait_ge(ld_root, 32)
            for i in range(T):
                for o, c, m in piece(0, i * D, D):
                    for k in range(K):
                        pe.matmul(PS[0:P, c:c + m], xT[:, k, i * P:(i + 1) * P], wroot[:, k, o:o + m],
                                  start=False, stop=False, skip_group_check=True)
                    mm = pe.matmul(PS[0:P, c:c + m], ones[0:1, 0:P], rbrow[:, o:o + m],
                                   start=False, stop=True, skip_group_check=True)
            mm.then_inc(full[0], 1)
            pe.wait_ge(full[0], BEFORE["messages"][0] + 1)
            for q in range(1, 4):
                pe.sem_inc(full[q], 1)

            turn("turn5", h1, lambda: pe.wait_ge(h1_ready, 1))
            pe.wait_ge(ld_gcn, 32)
            product("wgcn", wgcn, 5)
            pe.wait_ge(xws_ready, T)
            for i in range(T):
                take("gcn", i % 4, i // 4)
                for t in range(T):
                    for s in range(2):
                        mm = pe.matmul(slot(i % 4)[0:P, s * BANK:s * BANK + HALF], cnt[:, t, i * P:(i + 1) * P],
                                       xws[:, t, s * HALF:(s + 1) * HALF], start=(t == 0), stop=(t == T - 1))
                mm.then_inc(full[i % 4], 1)

            turn("turn6", xn, lambda: pe.wait_ge(xn_ready, 5 * T))
            logits("route2", wr_sb, NE, 6)
            RANKED = NE + 1
            for n in range(FK + RANKED):
                if n < FK:
                    c, b = n, n // 3 % 2
                    pe.wait_ge(ld_f1[b], 64 + 64 * (n // 3 // 2 + 1))
                    take("inner2", 0, c)
                    inner(slot(0), fw1[b], c % 3).then_inc(full[0], 1)
                    take("inner2", 1, c)
                    inner(slot(1), fw3[b], c % 3).then_inc(full[1], 1)
                if n < NE:
                    pe.wait_ge(cols_ready, HEADS + 1 + n + 1)
                    take("inner2", 3, n)
                    spread(3, lambda t: scol[n % 2][:, t:t + 1])
                if n >= RANKED:
                    c = n - RANKED
                    take("inner2", 2, c)
                    pe.wait_ge(combw_ready, 4 + c // 3 + 1)
                    weights_row(2, c // 3 % 2, c % 3)
            pe.wait_ge(ld_f1[0], 64 + 128 + 32)
            for c in range(2):
                take("shared", 0, c)
                inner(slot(0), fw1[0], c, F // 2).then_inc(full[0], 1)
                take("shared", 1, c)
                inner(slot(1), fw3[0], c, F // 2).then_inc(full[1], 1)
            pe.wait_ge(weighted, FK)
            pe.wait_ge(inner_done, 2 * FK + 2)
            outer("outer2", [(c, 128) for c in range(FK)] + [(FK, F // 2), (FK + 1, F // 2)], None)


_WEIGHTS = [
    "L0_gnn_W1",
    "L0_gnn_a_src1",
    "L0_gnn_a_dst1",
    "L0_gnn_b1",
    "L0_gnn_W2",
    "L0_gnn_a_src2",
    "L0_gnn_a_dst2",
    "L0_gnn_b2",
    "L0_ffn_v_w",
    "L0_ffn_v_b",
    "L0_ffn_gate_w",
    "L0_ffn_gate_b",
    "L0_ffn_w1",
    "L0_ffn_b1",
    "L0_ffn_w2",
    "L0_ffn_b2",
    "L0_ffn_out_w",
    "L0_ffn_out_b",
    "L0_ffn_bk_scale",
    "L1_gnn_W_rel",
    "L1_gnn_W_root",
    "L1_gnn_b_rgcn",
    "L1_gnn_W_gcn",
    "L1_gnn_b_gcn",
    "L1_ffn_Wr",
    "L1_ffn_w1",
    "L1_ffn_w3",
    "L1_ffn_w2",
    "L1_ffn_s1",
    "L1_ffn_s3",
    "L1_ffn_s2",
]


def kernel(**inputs):
    import numpy as _np
    import concourse.bacc as _bacc
    from concourse.bass_utils import run_bass_kernel_spmd as _run

    nc = _bacc.Bacc("TRN2", target_bir_lowering=False, num_devices=1)
    arrays, aps = {}, {}
    for name in ["x", "src", "dst", "edge_type_34"] + _WEIGHTS:
        a = _np.ascontiguousarray(inputs[name])
        if name == "L0_ffn_v_b":
            a = a.reshape(1)
        arrays[f"in_{name}"] = a
        aps[name] = nc.dram_tensor(f"in_{name}", a.shape, mybir.dt.from_np(a.dtype), kind="ExternalInput").ap()
    aps["out"] = nc.dram_tensor("out_0", (N, D), mybir.dt.float32, kind="ExternalOutput").ap()
    build(nc, aps["x"], aps["src"], aps["dst"], aps["edge_type_34"], aps)
    r = _run(nc, [arrays], core_ids=[0])
    return r.results[0]["out_0"]
```

```python
import concourse.bass as bass
from concourse import mybir
from contextlib import ExitStack, contextmanager

N, D = 625, 768
P = 125
T = N // P
K = D // 128
EDGES = 10000
EP = 125
ET = EDGES // EP
REL = 34
HEADS, HC = 8, D // 8
NE, F = 8, 192
FF = NE * F
FK = FF // 128
CAP = 196
BC = 25
GT = EDGES // T // 128 + 2
GE = GT * 128
AHEAD = 8
RT = 2
MORE = -(-N // 128) - RT
LIST = 1000
FIRST = REL * RT * 128
FEW = 4
MANY = -(-EDGES * MORE // ((RT + MORE - 1) * 128 + 1))
HALF = D // 2
BANK = 512
EPS = 1e-5

STAGES = [
    ("edges", [1, 1, 1, 1]), ("turn1", [2, 2, 1, 1]), ("mask", [2, 1, 1, 1]), ("ranks", [0, 1, 1, 0]),
    ("w1", [2, 1, 1, 1]), ("lists", [1, 1, 0, 0]), ("heads1", [HEADS] * 4),
    ("turn2", [2, 2, 1, 1]), ("w2", [2, 1, 1, 1]), ("heads2", [3, 1, 1, 3]),
    ("turn3", [2, 2, 1, 1]), ("route1", [1, 1, 1, 0]), ("inner1", [6, 6, 6, 6]),
    ("outer1", [2, 1, 1, 1]),
    ("turn4", [2, 2, 1, 1]), ("relations", [REL] * 4),
    ("messages", [2, 1, 1, 1]), ("turn5", [2, 2, 1, 1]), ("wgcn", [2, 1, 1, 1]), ("gcn", [2, 1, 1, 1]),
    ("turn6", [2, 2, 1, 1]), ("route2", [1, 0, 0, 0]),
    ("places", [0, 0, 0, 1]), ("lists2", [0, 0, 0, NE // 2]), ("ranks2", [0, 0, 0, NE]),
]
SH = 3
ITEMS = [(None, t) for t in range(SH)] + [(e, j) for e in range(NE) for j in range(RT)] + [(None, t) for t in range(SH, T)]
OWN = SH + NE * RT
RING = 3
FIRST2 = NE * RT * 128
MANY2 = 4 * -(-2 * N * MORE // (4 * ((RT + MORE - 1) * 128 + 1)))


def at(i, b, per, more=0):
    return i * (2 * per) + (b * per + more)


BEFORE, _n = {}, [0, 0, 0, 0]
for _name, _jobs in STAGES:
    BEFORE[_name] = list(_n)
    _n = [a + b for a, b in zip(_n, _jobs)]


class Track:

    def __init__(self, eng, own):
        self.eng, self.own, self.n, self.extra = eng, own, 0, None

    def __call__(self, ins):
        ins.then_inc(self.own, 1)
        self.n += 1
        return ins

    def sync(self):
        self.eng.wait_ge(self.own, self.n if self.extra is None else self.n + self.extra)

    def do(self, ins):
        self(ins)
        self.sync()

    @contextmanager
    def turns(self, n, signals):
        start = self.n
        with self.eng.Fori(0, n) as i:
            self.extra = i * signals
            yield i
        assert self.n - start == signals, (self.n - start, signals)
        self.extra = None
        self.n = start + signals * n


def build(nc, x, src, dst, etype, w):
    f32, f32r, bf16 = mybir.dt.float32, mybir.dt.float32r, mybir.dt.bfloat16
    i32, u32, i16 = mybir.dt.int32, mybir.dt.uint32, mybir.dt.int16
    ALU, ACT, AX = mybir.AluOpType, mybir.ActivationFunctionType, mybir.AxisListType

    out = w["out"]
    z_dram = nc.dram_tensor("z_dram", [FIRST + MANY * 128, D], f32).ap()
    inv_dram = nc.dram_tensor("inv_dram", [REL * N, 1], f32).ap()
    zrow_dram = nc.dram_tensor("zrow_dram", [REL * N, 1], u32).ap()
    xn_dram = nc.dram_tensor("xn_dram", [N, D], f32).ap()
    y_dram = nc.dram_tensor("y_dram", [FIRST2 + MANY2 * 128, D], f32).ap()
    edge_dram = nc.dram_tensor("edge_dram", [T * GE, 4], f32).ap()
    v_dram = nc.dram_tensor("v_dram", [N], f32).ap()
    mat_dram = nc.dram_tensor("mat_dram", [BC, 16], f32).ap()
    rho_dram = nc.dram_tensor("rho_dram", [BC, 4], f32).ap()
    green_dram = nc.dram_tensor("green_dram", [2, N], f32).ap()

    ctx = ExitStack()
    with ctx:
        def sb(name, shape, dt=f32, where=ctx):
            return where.enter_context(nc.sbuf_tensor(name, shape, dt))

        def sem(name):
            return ctx.enter_context(nc.semaphore(name))

        x_res = sb("x_res", [P, T, D])
        xn_all = sb("xn", [128, T, D])
        xn = xn_all[0:P, :, :]
        xT = sb("xT", [128, K, N])
        counts = sb("counts", [P, T, N + REL])
        cnt = counts[:, :, 0:N]
        ident = sb("ident", [128, 128])
        ones = sb("ones", [128, 128])
        stats = sb("stats", [P, T, 2, 6])
        mv = sb("mv", [P, T, 2])
        rstd = sb("rstd", [P, T])
        small = sb("small", [P, 12, T, NE])
        rev = sb("rev", [P, NE])
        asg = sb("asg", [P, T, NE])
        comb1 = sb("comb1", [P, T, NE])
        t5 = sb("t5", [P, 8, T])
        dinv = sb("dinv", [P, T])
        evw = sb("evw", [EP, ET])
        dstf = sb("dstf", [EP, ET])
        zidx = sb("zidx", [EP, ET], u32)
        iota_all = sb("iota16", [128, T * 128], i16)
        iota16 = iota_all[0:P, :]
        rec = sb("rec", [EP, ET, 4])
        grec = sb("grec", [128, T * GT, 4])
        grow = sb("grow", [128, T * GT], u32)
        eplace = sb("eplace", [EP, ET], u32)
        in_row = sb("in_row", [EP, T])
        idxb2 = sb("idxb2", [EP, AHEAD], u32)
        recb = sb("recb", [EP, AHEAD, 4])
        crowded = sb("crowded", [1, 1], i32)
        pos = sb("pos", [P, T, REL + 1])
        poscol = sb("poscol", [P, T])
        more_n = sb("more_n", [1, 1], i32)
        more_at = sb("more_at", [1, 2, MANY], i32)
        node_of = sb("node_of", [P, T, 2], bf16)
        inlist = [sb(f"inlist{b}", [P, T, RT * 128], bf16) for b in range(2)]
        xrow = sb("xrow", [128, 2, RT], u32)
        node = sb("node", [128, RT])
        gate_sb = sb("gate_sb", [128, K, NE + 1])
        wr_sb = sb("wr_sb", [128, K, NE])
        gate_b = sb("gate_b", [P, NE])
        before16, ones16 = sb("before16", [P, P], bf16), sb("ones16", [P, P], bf16)
        asg16 = sb("asg16", [P, T, NE], bf16)
        scol = [sb(f"scol{b}", [P, T]) for b in range(2)]
        v_b = sb("v_b", [P, 1])
        PS = ctx.enter_context(nc.psum_tensor("PS", [128, 8 * BANK], f32))

        def slot(q):
            return PS[:, q * 2 * BANK:(q + 1) * 2 * BANK]

        full = [sem(f"slot{q}_full") for q in range(4)]
        free = [sem(f"slot{q}_free") for q in range(4)]
        act_step, dve_step, pool_step = sem("act_step"), sem("dve_step"), sem("pool_step")
        consts_ready = sem("consts_ready")
        ld_edges, ld_x, ld_gate, ld_rows = sem("ld_edges"), sem("ld_x"), sem("ld_gate"), sem("ld_rows")
        ld_w1, ld_w2 = sem("ld_w1"), sem("ld_w2")
        onehots_ready, onehots_used = sem("onehots_ready"), sem("onehots_used")
        cnt_ready, inv_ready, inv_stored = sem("cnt_ready"), sem("inv_ready"), sem("inv_stored")
        cidx_ready, evw_loaded, evw_ready = sem("cidx_ready"), sem("evw_loaded"), sem("evw_ready")
        idx_used = sem("idx_used")
        var_ready, std_ready, xn_ready, xT_ready = sem("var_ready"), sem("std_ready"), sem("xn_ready"), sem("xT_ready")
        h_ready, cols_ready, r_ready = sem("h_ready"), sem("cols_ready"), sem("r_ready")
        exps_ready, probs_ready, agg_taken = sem("exps_ready"), sem("probs_ready"), sem("agg_taken")
        elu_in, elu_exp = sem("elu_in"), sem("elu_exp")
        logits_in, logits_exp = sem("logits_in"), sem("logits_exp")
        deg_ready, deg_sqrt = sem("deg_ready"), sem("deg_sqrt")
        comb_ready, combw_ready = sem("comb_ready"), sem("combw_ready")
        act_done, inner_done = sem("act_done"), sem("inner_done")
        ld_f1, ld_f2 = [sem("ld_f1a"), sem("ld_f1b")], sem("ld_f2")
        ld_small = sem("ld_small")
        spec_ready, spec_out, spec_in = sem("spec_ready"), sem("spec_out"), sem("spec_in")
        specw_ready, layer_done = sem("specw_ready"), sem("layer_done")
        split_hi, split_lo = sem("split_hi"), sem("split_lo")
        raw_loaded = [sem("raw_loaded0"), sem("raw_loaded1")]
        folded, fold_used = sem("folded"), sem("fold_used")
        pres_ready = sem("pres_ready")
        xn_stored, inlist_ready, rows_ready = sem("xn_stored"), sem("inlist_ready"), sem("rows_ready")
        x_gathered = [[sem(f"x_gathered{b}_{j}") for j in range(RT)] for b in range(2)]
        z_stored = [[sem(f"z_stored{b}_{j}") for j in range(RT)] for b in range(2)]
        xhi_ready, xlo_ready = sem("xhi_ready"), sem("xlo_ready")
        zrow_ready, zrow_stored, z_begun, z_filled = sem("zrow_ready"), sem("zrow_stored"), sem("z_begun"), sem("z_filled")
        ld_shared, ld_w13, ld_w2e = sem("ld_shared"), [sem(f"ld_w13_{b}") for b in range(RING)], [sem(f"ld_w2_{b}") for b in range(RING)]
        asg_ready, inlist2_ready, rows2_ready = sem("asg_ready"), sem("inlist2_ready"), sem("rows2_ready")
        turned, x_taken, inner_full, gate_ready, h2_ready = sem("turned"), sem("x_taken"), sem("inner_full"), sem("gate_ready"), sem("h2_ready")
        h_turned, hT_ready, outer_full, outer_taken = sem("h_turned"), sem("hT_ready"), sem("outer_full"), sem("outer_taken")
        y_stored, y_begun, scol_ready, srow_ready, yrow_ready = [sem("y_stored0"), sem("y_stored1")], sem("y_begun"), sem("scol_ready"), sem("srow_ready"), sem("yrow_ready")
        y_complete, y_gathered, tile_done = sem("y_complete"), [sem(f"y_gathered{t}") for t in range(T)], sem("tile_done")
        f_more_ready, f_more_gathered, f_loaded, f_stored, f_freed = sem("f_more_ready"), sem("f_more_gathered"), sem("f_loaded"), sem("f_stored"), sem("f_freed")
        act_more2, dve_more2, pe_more2 = sem("act_more2"), sem("dve_more2"), sem("pe_more2")
        m_gathered, m_stored, m_split_lo = sem("m_gathered"), sem("m_stored"), sem("m_split_lo")
        m_loaded = [sem("m_loaded0"), sem("m_loaded1")]
        act_more, dve_more, pe_more = sem("act_more"), sem("dve_more"), sem("pe_more")
        in_row_ready, eplace_ready, cleared, grec_blank = sem("in_row_ready"), sem("eplace_ready"), sem("cleared"), sem("grec_blank")
        rec_stored, grec_loaded, grow_ready = sem("rec_stored"), sem("grec_loaded"), sem("grow_ready")
        more_ready, rows_loaded = sem("more_ready"), sem("rows_loaded")
        gathered = [sem(f"gathered{b}") for b in range(5)]
        msg_hi, msg_ready, msg_used, hot_ready = sem("msg_hi"), sem("msg_ready"), sem("msg_used"), sem("hot_ready")
        ld_root, ld_gcn = sem("ld_root"), sem("ld_gcn")
        h1_ready, xw_ready, xws_ready = sem("h1_ready"), sem("xw_ready"), sem("xws_ready")
        wa_ready, al_taken = sem("wa_ready"), sem("al_taken")
        earlier_ready = sem("earlier_ready")
        begun = sem("begun")
        out_stored = sem("out_stored")

        g = ExitStack()
        with g:
            negm = sb("negm", [P, T, N], f32, g)
            hx = sb("hx", [P, T, D + HEADS], f32, g)
            gw = [sb(f"gw{b}", [128, K, D], f32, g) for b in range(2)]
            arow = sb("arow", [128, 4, D], f32, g)
            brow = sb("brow", [P, 2, D], f32, g)
            al = sb("al", [P, T, 2, HEADS], f32, g)
            wa1 = sb("wa1", [128, K, 2, HEADS], f32, g)
            wa2 = sb("wa2", [128, K, 2, 1], f32, g)
            hcol = [sb(f"hcol{b}", [P, T, 2], f32, g) for b in range(2)]
            rcol = [sb(f"rcol{b}", [P, T, 3], f32, g) for b in range(2)]
            smax = sb("smax", [P, 4, T], f32, g)
            cidx = sb("cidx", [EP, 2, ET], u32, g)
            idxb = sb("idxb", [EP, 2, AHEAD], u32, g)
            evwb = sb("evwb", [EP, AHEAD], f32, g)
            zidxb = sb("zidxb", [EP, AHEAD], u32, g)
            smore = sb("smore", [1, 2, MANY], f32, g)
            ran = sb("ran", [P, 3, REL], f32, g)
            gcount = sb("gcount", [P, 2, T], f32, g)
            gmax = sb("gmax", [1, 1], f32, g)
            rel_row = sb("rel_row", [P, 3, REL], f32, g)
            with ExitStack() as edges:
                tmp = [sb(f"tmp{b}", [128, D], f32, edges) for b in range(2)]
                iota34 = sb("iota34", [EP, REL], i16, edges)
                eint = sb("eint", [EP, 3, ET], i32, edges)
                ef = sb("ef", [EP, 3, ET], f32, edges)
                hot_s = [sb(f"hot_s{b}", [EP, N], bf16, edges) for b in range(AHEAD)]
                hot_dr = [sb(f"hot_dr{b}", [EP, N + REL], bf16, edges) for b in range(AHEAD)]
                pres = sb("pres", [P, T, REL], f32, edges)
                before = sb("before", [P, P], f32, edges)
                zrow = sb("zrow", [P, T, REL], u32, edges)
                further = sb("further", [P, T, REL], f32, edges)
                inv = sb("inv", [P, T, REL], f32, edges)
            e1 = [sb(f"e1_{b}", [P, T, N], f32, g) for b in range(2)]
            e2 = [sb(f"e2_{b}", [P, T, N], f32, g) for b in range(2)]
        g = ExitStack()
        with g:
            hT = sb("hT", [128, FK + 2, N], f32, g)
            fw1 = [sb(f"fw1_{b}", [128, K, 2 * F], f32, g) for b in range(2)]
            fw3 = [sb(f"fw3_{b}", [128, K, 2 * F], f32, g) for b in range(2)]
            fw2 = sb("fw2", [128, FK + 2, D], f32, g)
            combw = [sb(f"combw{b}", [P, T, 2 * F], f32, g) for b in range(2)]
            b1r = sb("b1r", [FK, 128], f32, g)
            b1T = sb("b1T", [128, FK], f32, g)
            b2r = sb("b2r", [NE, D], f32, g)
            combT = sb("combT", [NE, N], f32, g)
        g = ExitStack()
        with g:
            pad = sb("pad", [128, FK + 2, N], f32, g)
            pad2 = sb("pad2", [128, 2, K, 2 * F], f32, g)
            vch = sb("vch", [BC, BC], f32, g)
            ar = sb("ar", [BC, 2, BC], f32, g)
            ar2 = sb("ar2", [BC, BC, 2, 2], f32, g)
            S = sb("S", [BC, BC + 2, 8], f32, g)
            SW = sb("SW", [BC, 2, 8], f32, g)
            ml = sb("ml", [1, BC, 16], f32, g)
            mo = sb("mo", [1, BC, 2, 12], f32, g)
            rho = sb("rho", [1, BC + 1, 2, 2], f32, g)
            rhoo = sb("rhoo", [1, BC, 4], f32, g)
            mt = sb("mt", [1, 5, 2, 4], f32, g)
            rin = sb("rin", [BC, 2, 2], f32, g)
            nrin = sb("nrin", [BC, 2, 2], f32, g)
            sol = sb("sol", [BC, 2, BC + 1, 2], f32, g)
            dq = sb("dq", [BC, 6, 2, BC, 2], f32, g)
            green = sb("green", [BC, 2, BC], f32, g)
            v_col = sb("v_col", [P, T], f32, g)
        feats, bkrow, specw = hT[0:3, FK, :], fw2[0:3, FK, :], fw2[0:3, FK + 1, :]
        g = ExitStack()
        with g:
            raw = sb("raw", [128, K, D], f32, g)
            whi = [sb(f"whi{b}", [128, K, D], f32r, g) for b in range(2)]
            wlo = [sb(f"wlo{b}", [128, K, D], f32r, g) for b in range(2)]
            xg = [[sb(f"xg{b}_{j}", [128, D], f32, g) for j in range(RT)] for b in range(2)]
            xhi = [[sb(f"xhi{b}_{j}", [128, K, 128], f32r, g) for j in range(RT)] for b in range(2)]
            xlo = [[sb(f"xlo{b}_{j}", [128, K, 128], f32r, g) for j in range(RT)] for b in range(2)]
        zb = [[xn_all[:, 2 * b + j, :] for j in range(RT)] for b in range(2)]
        late = ExitStack()
        with late:
            s13 = sb("s13", [128, K, 2 * F], f32, late)
            s2 = sb("s2", [HC, 2, D], f32, late)
            w13 = [sb("w13_0", [128, K, 2 * F], f32, late)]
            w2e = [sb("w2e_0", [HC, 2, D], f32, late)]
            g = ExitStack()
            wroot = sb("wroot", [128, K, D], f32, g)
            wgcn = sb("wgcn", [128, K, D], f32, g)
            rbrow = sb("rbrow", [1, D], f32, g)
            gbrow = sb("gbrow", [P, D], f32, g)
            hotf = [sb(f"hotf{b}", [128, N], f32r, g) for b in range(2)]
            zg = [sb(f"zg{b}", [128, D], f32, g) for b in range(4)]
            mhi = [sb(f"mhi{b}", [128, D], f32r, g) for b in range(2)]
            mlo = [sb(f"mlo{b}", [128, D], f32r, g) for b in range(2)]
            zib = [sb(f"zib{b}", [EP, 1], u32, g) for b in range(4)]
            h1 = sb("h1", [P, T, D], f32, g)
            hotf += [sb(f"hotf{b}", [128, P], f32r, g) for b in (2, 3)]
            with ExitStack() as first:
                zg += [sb("zg4", [128, D], f32, first)]
                mhi += [sb(f"mhi{b}", [128, D], f32r, first) for b in (2, 3)]
                mlo += [sb(f"mlo{b}", [128, D], f32r, first) for b in (2, 3)]
            xws = sb("xws", [P, T, D], f32, g)
            gtmp = sb("gtmp", [P, 4], f32, g)
            g.close()
            g = late
            w2e += [sb(f"w2e_{b}", [HC, 2, D], f32, g) for b in (1, 2)]
            w13 += [sb(f"w13_{b}", [128, K, 2 * F], f32, g) for b in (1, 2)]
            fx = [sb(f"fx{b}", [128, D], f32, g) for b in range(4)]
            fxT = [sb(f"fxT{b}", [128, K, 128], f32, g) for b in range(2)]
            gate = [sb(f"gate{b}", [128, F], f32, g) for b in range(2)]
            hh = [sb(f"hh{b}", [128, F], f32, g) for b in range(2)]
            hhT = [sb(f"hhT{b}", [HC, 2, 128], f32, g) for b in range(2)]
            yb = [sb(f"yb{b}", [128, D], f32, g) for b in range(2)]
            inlist2 = [sb(f"inlist2_{b}", [P, T, RT * 128], bf16, g) for b in range(2)]
            earlier = sb("earlier", [P, T, N], f32, g)
            compared = sb("compared", [P, T, P], f32, g)
            srow = [sb(f"srow{b}", [P, T, P], f32, g) for b in range(2)]
            place = sb("place", [P, T, NE], f32, g)
            yrow_f = sb("yrow_f", [P, T, NE], f32, g)
            ysel = sb("ysel", [P, T, NE], f32, g)
            yrow = sb("yrow", [P, 2, T], u32, g)
            yw = sb("yw", [P, 2, T], f32, g)
            fn = sb("fn", [P, 4, NE], f32, g)
            frow = sb("frow", [P, 3, NE], f32, g)
            fover = sb("fover", [1, MANY2, NE], f32, g)
            fof = sb("fof", [1, 2, MANY2], f32, g)
            f_at = sb("f_at", [1, 2, MANY2], i32, g)
            f_n = sb("f_n", [1, 1], i32, g)
            xrow2 = sb("xrow2", [128, NE, RT], u32, g)
            yg = [b[0:P, :, :].rearrange("p k f -> p (k f)")[:, i * D:(i + 1) * D] for b in w13[1:] for i in range(3)]
            yg += [b[0:P, :] for b in fx[1:]] + [sb("yg9", [P, D], f32, g)[:, :]]

        def further_tiles(eng, tile, number=more_n, most=MANY):
            total = eng.value_load(number[0:1, 0:1], min_val=0, max_val=most)
            with eng.If(total > 0):
                with eng.Fori(0, total) as m:
                    tile(m)

        psT = lambda q: slot(q)[:, 0:T * 128].rearrange("p (t c) -> p t c", c=128)

        block = ctx.enter_context(nc.Block())

        @block.sync
        def _(sp):
            sp.dma_start(eint[:, 0, :], src.rearrange("(p j) -> p j", j=ET)).then_inc(ld_edges, 16)
            sp.dma_start(eint[:, 1, :], dst.rearrange("(p j) -> p j", j=ET)).then_inc(ld_edges, 16)
            sp.dma_start(eint[:, 2, :], etype.rearrange("(p j) -> p j", j=ET)).then_inc(ld_edges, 16)
            sp.dma_start(x_res[:, :, :], x.rearrange("(t p) d -> p t d", p=P)).then_inc(ld_x, 16)
            sp.dma_start(gw[0][:, :, :], w["L0_gnn_W1"].rearrange("(k p) n -> p k n", p=128)).then_inc(ld_w1, 16)
            for n, name in enumerate(("L0_gnn_a_src1", "L0_gnn_a_dst1", "L0_gnn_a_src2", "L0_gnn_a_dst2")):
                sp.dma_start(arow[:, n, :], w[name].rearrange("h c -> (h c)").partition_broadcast(128)).then_inc(ld_rows, 16)
            for n, name in enumerate(("L0_gnn_b1", "L0_gnn_b2")):
                sp.dma_start(brow[:, n, :], w[name].partition_broadcast(P)).then_inc(ld_rows, 16)
            sp.dma_start(gw[1][:, :, :], w["L0_gnn_W2"].rearrange("(k p) n -> p k n", p=128)).then_inc(ld_w2, 16)
            sp.dma_start(gate_sb[:, :, 0:NE], w["L0_ffn_gate_w"].rearrange("(k p) n -> p k n", p=128)).then_inc(ld_gate, 16)
            sp.dma_start(gate_sb[:, :, NE:NE + 1], w["L0_ffn_v_w"].rearrange("(k p n) -> p k n", p=128, n=1), allow_slow_non_contiguous=True).then_inc(ld_gate, 16)
            sp.dma_start(wr_sb[:, :, :], w["L1_ffn_Wr"].rearrange("(k p) n -> p k n", p=128)).then_inc(ld_gate, 16)
            sp.dma_start(gate_b[:, :], w["L0_ffn_gate_b"].partition_broadcast(P)).then_inc(ld_gate, 16)
            sp.dma_start(v_b[:, :], w["L0_ffn_v_b"].partition_broadcast(P)).then_inc(ld_gate, 16)
            sp.wait_ge(inv_ready, 1)
            sp.dma_start(inv_dram.rearrange("(t p r) o -> p t (r o)", p=P, r=REL), inv[:, :, :]).then_inc(inv_stored, 16)
            sp.wait_ge(cleared, 1)
            sp.dma_start(edge_dram.rearrange("(q p) c -> p q c", p=128), grec[:, :, :]).then_inc(grec_blank, 16)
            sp.dma_start(z_dram[FIRST:FIRST + FEW * 128, :], x[0:FEW * 128, :]).then_inc(z_begun, 16)
            for first in range(0, MANY2 * 128, 4 * 128):
                sp.dma_start(y_dram[FIRST2 + first:FIRST2 + first + 4 * 128, :], x[0:4 * 128, :]).then_inc(y_begun, 16)
            sp.wait_ge(y_begun, 16 * (MANY2 // 4))
            sp.wait_ge(z_begun, 16)
            sp.wait_ge(zrow_ready, 1)
            sp.dma_start(zrow_dram.rearrange("(t p r) o -> p t (r o)", p=P, r=REL), zrow[:, :, :]).then_inc(zrow_stored, 16)
            sp.wait_ge(more_ready, 1)
            sp.wait_ge(grec_blank, 16)
            total = sp.value_load(more_n[0:1, 0:1], min_val=0, max_val=MANY)
            with sp.If(total > FEW):
                for n in range(FEW, MANY, FEW):
                    rows = min(FEW, MANY - n) * 128
                    sp.dma_start(z_dram[FIRST + n * 128:FIRST + n * 128 + rows, :], x[0:rows, :]).then_inc(z_begun, 16)
                sp.wait_ge(z_begun, 16 * -(-MANY // FEW))
                sp.sem_inc(z_filled, 1)
            with sp.Else():
                sp.sem_inc(z_filled, 1)

            sp.wait_ge(inv_stored, 16)
            sp.wait_ge(evw_ready, 1)
            sp.wait_ge(layer_done, 1)
            sp.dma_start(b1r[:, :], w["L0_ffn_b1"].rearrange("e f -> (e f)").rearrange("(c p) -> c p", p=128)).then_inc(ld_small, 16)
            sp.dma_start(b2r[:, :], w["L0_ffn_b2"]).then_inc(ld_small, 16)
            sp.dma_start(specw[0:2], w["L0_ffn_out_w"]).then_inc(ld_small, 16)
            sp.dma_start(specw[2:3], w["L0_ffn_out_b"].rearrange("(a d) -> a d", a=1)).then_inc(ld_small, 16)
            sp.dma_start(bkrow, w["L0_ffn_bk_scale"].partition_broadcast(3)).then_inc(ld_small, 16)
            w1v = w["L0_ffn_w1"].rearrange("e (k p) f -> e p k f", p=128)

            def load_pair(buf, view, i, signal):
                for e in range(2):
                    sp.dma_start(buf[:, :, e * F:(e + 1) * F], view[2 * i + e, :, :, :]).then_inc(signal, 16)

            load_pair(fw1[0], w1v, 0, ld_f1[0])
            load_pair(fw1[1], w1v, 1, ld_f1[1])
            sp.dma_start(fw2[:, 0:FK, :], w["L0_ffn_w2"].rearrange("e f d -> (e f) d").rearrange("(c p) d -> p c d", p=128)).then_inc(ld_f2, 16)
            for i in (2, 3):
                sp.wait_ge(act_done, 1 + 3 * (i - 1))
                load_pair(fw1[i % 2], w1v, i, ld_f1[i % 2])
            sp.wait_ge(layer_done, 2)
            wv = w["L1_gnn_W_rel"].rearrange("r (k p) n -> r p k n", p=128)
            KH = K // 2

            def load_raw(r, first):
                for half in range(2):
                    if not first:
                        sp.wait_ge(split_lo, r * 2 + half - 1)
                    sp.dma_start(raw[:, half * KH:(half + 1) * KH, :],
                                 wv[r, :, half * KH:(half + 1) * KH, :]).then_inc(raw_loaded[half], 16)

            load_raw(0, True)
            sp.wait_ge(xn_ready, 4 * T)
            sp.dma_start(xn_dram.rearrange("(t p) d -> p t d", p=P), xn).then_inc(xn_stored, 16)
            with sp.Fori(1, REL) as r:
                load_raw(r, False)
            sp.wait_ge(split_lo, 2 * REL)
            sp.wait_ge(more_ready, 1)
            sp.sem_inc(m_split_lo, 2)

            def further_weights(m):
                rel = sp.value_load(more_at[0:1, 0, bass.ds(m, 1)], min_val=0, max_val=REL - 1)
                for half in range(2):
                    sp.wait_ge(m_split_lo, m * 2 + half + 1)
                    sp.dma_start(raw[:, half * KH:(half + 1) * KH, :],
                                 wv[bass.ds(rel, 1), :, half * KH:(half + 1) * KH, :].rearrange("r p k n -> p (r k) n")).then_inc(m_loaded[half], 16)

            further_tiles(sp, further_weights)

            sp.wait_ge(msg_used, 6)
            sp.dma_start(wroot[:, :, :], w["L1_gnn_W_root"].rearrange("(k p) n -> p k n", p=128)).then_inc(ld_root, 16)
            sp.dma_start(rbrow[:, :], w["L1_gnn_b_rgcn"].rearrange("(a d) -> a d", a=1)).then_inc(ld_root, 16)
            sp.wait_ge(msg_used, 14)
            sp.dma_start(wgcn[:, :, :], w["L1_gnn_W_gcn"].rearrange("(k p) n -> p k n", p=128)).then_inc(ld_gcn, 16)
            sp.dma_start(gbrow[:, :], w["L1_gnn_b_gcn"].partition_broadcast(P)).then_inc(ld_gcn, 16)

            sp.wait_ge(msg_used, 30)
            for n, name in enumerate(("L1_ffn_s1", "L1_ffn_s3")):
                sp.dma_start(s13[:, :, n * F:(n + 1) * F], w[name].rearrange("(k p) f -> p k f", p=128)).then_inc(ld_shared, 16)
            sp.dma_start(s2[:, :, :], w["L1_ffn_s2"].rearrange("(c p) d -> p c d", c=2)).then_inc(ld_shared, 16)
            v13 = [w[name].rearrange("e (k p) f -> e p k f", p=128) for name in ("L1_ffn_w1", "L1_ffn_w3")]
            v2 = w["L1_ffn_w2"].rearrange("e (c p) d -> e p c d", c=2)

            def load_w13(e, b, signal):
                for n in range(2):
                    sp.dma_start(w13[b][:, :, n * F:(n + 1) * F], v13[n][e]).then_inc(signal, 16)

            load_w13(0, 0, ld_w13[0])
            sp.dma_start(w2e[0][:, :, :], v2[0]).then_inc(ld_w2e[0], 16)
            sp.wait_ge(layer_done, 4)
            for b in range(1, RING):
                load_w13(b, b, ld_w13[b])
                sp.dma_start(w2e[b][:, :, :], v2[b]).then_inc(ld_w2e[b], 16)
            sp.wait_ge(xn_ready, 5 * T)
            sp.dma_start(xn_dram.rearrange("(t p) d -> p t d", p=P), xn).then_inc(xn_stored, 16)
            for e in range(RING, NE):
                sp.wait_ge(inner_full, SH + RT * (e - RING + 1))
                load_w13(e, e % RING, ld_w13[e % RING])
                sp.wait_ge(outer_full, SH + RT * (e - RING + 1))
                sp.dma_start(w2e[e % RING][:, :, :], v2[e]).then_inc(ld_w2e[e % RING], 16)
            sp.wait_ge(outer_full, SH + RT * (NE - RING + 1))
            sp.wait_ge(f_more_ready, 1)
            sp.sem_inc(f_freed, 1)

            def further_weights2(m):
                e = sp.value_load(f_at[0:1, 0, bass.ds(m, 1)], min_val=0, max_val=NE - 1)
                sp.wait_ge(f_freed, m + 1)
                for n in range(2):
                    sp.dma_start(w13[NE % RING][:, :, n * F:(n + 1) * F],
                                 v13[n][bass.ds(e, 1)].rearrange("e p k f -> p (e k) f")).then_inc(f_loaded, 16)
                sp.dma_start(w2e[NE % RING][:, :, :], v2[bass.ds(e, 1)].rearrange("e p c d -> p (e c) d")).then_inc(f_loaded, 16)

            further_tiles(sp, further_weights2, f_n, MANY2)
            for t in range(T):
                sp.wait_ge(tile_done, t + 1)
                sp.dma_start(out[t * P:(t + 1) * P, :], x_res[:, t, :]).then_inc(out_stored, 16)
            sp.wait_ge(out_stored, 16 * T)

        @block.gpsimd
        def _(pool):
            step = Track(pool, pool_step)
            step(pool.iota(iota_all[:, :], [[1, T * 128]], base=0, channel_multiplier=0, allow_small_or_imprecise_dtypes=True))
            step(pool.iota(iota34[:, :], [[1, REL]], base=0, channel_multiplier=0, allow_small_or_imprecise_dtypes=True))
            step(pool.iota(rev[:, :], [[-1, NE]], base=NE, channel_multiplier=0, allow_small_or_imprecise_dtypes=True))
            step(pool.memset(ones[:, :], 1.0))
            step.do(pool.memset(ident[:, :], 0.0))
            step.do(pool.affine_select(out=ident[:, :], in_=ident[:, :], compare_op=ALU.not_equal, fill=1.0,
                                       base=0, pattern=[[-1, 128]], channel_multiplier=1))
            pool.sem_inc(consts_ready, 1)
            step(pool.iota(node_of[:, :, 0], [[0, T]], base=0, channel_multiplier=1, allow_small_or_imprecise_dtypes=True))
            step(pool.iota(node_of[:, :, 1], [[1, T]], base=0, channel_multiplier=0, allow_small_or_imprecise_dtypes=True))
            step(pool.iota(rel_row[:, 0, :], [[RT * 128, REL]], base=0, channel_multiplier=0, allow_small_or_imprecise_dtypes=True))
            step.do(pool.memset(before[:, :], 1.0))
            step.do(pool.affine_select(out=before[:, :], in_=before[:, :], compare_op=ALU.is_gt, fill=0.0,
                                       base=0, pattern=[[1, P]], channel_multiplier=-1))
            step(pool.tensor_copy(before16[:, :], before[:, :]))
            step.do(pool.memset(ones16[:, :], 1.0))
            pool.sem_inc(consts_ready, 1)
            pool.wait_ge(ld_rows, 96)
            pool.sem_inc(fold_used, 2)
            for layer, ready in enumerate((ld_w1, ld_w2)):
                pool.wait_ge(ready, 16)
                with pool.Fori(0, K) as k:
                    for s in range(2):
                        pool.wait_ge(fold_used, k * 2 + s + 2 * K * layer + 1)
                        pool.sem_inc(begun, 1)
                        pool.tensor_tensor(tmp[s][:, :], gw[layer][:, bass.ds(k, 1), :].rearrange("p o n -> p (o n)"),
                                           arow[:, 2 * layer + s, :], ALU.mult).then_inc(folded, 1)
            step.do(pool.memset(grec[:, :, :], 0.0))
            step.do(pool.memset(rec[:, :, 3], 0.0))
            pool.sem_inc(cleared, 1)
            pool.wait_ge(inv_stored, 16)
            pool.wait_ge(zrow_stored, 16)
            pool.wait_ge(cidx_ready, 1)
            with step.turns(ET // AHEAD, 3) as j:
                step.do(pool.tensor_copy(idxb[:, :, :], cidx[:, :, bass.ds(j * AHEAD, AHEAD)]))
                pool.sem_inc(begun, 1)
                for n in range(AHEAD):
                    pool.indirect_dma_start(evwb[:, n:n + 1], None, inv_dram,
                                            bass.IndirectOffsetOnAxis(ap=idxb[:, 0, n:n + 1], axis=0)).then_inc(evw_loaded, 16)
                    pool.indirect_dma_start(zidxb[:, n:n + 1], None, zrow_dram,
                                            bass.IndirectOffsetOnAxis(ap=idxb[:, 1, n:n + 1], axis=0)).then_inc(rows_loaded, 16)
                pool.wait_ge(evw_loaded, j * (16 * AHEAD) + 16 * AHEAD)
                step(pool.tensor_copy(evw[:, bass.ds(j * AHEAD, AHEAD)], evwb[:, :]))
                pool.wait_ge(rows_loaded, j * (16 * AHEAD) + 16 * AHEAD)
                step.do(pool.tensor_copy(zidx[:, bass.ds(j * AHEAD, AHEAD)], zidxb[:, :]))
            pool.sem_inc(evw_ready, 1)
            step(pool.tensor_copy(rec[:, :, 0], zidx[:, :]))
            step.do(pool.tensor_copy(rec[:, :, 1], evw[:, :]))
            pool.wait_ge(grec_blank, 16)
            pool.wait_ge(eplace_ready, 1)
            with step.turns(ET // AHEAD, 2) as j:
                step(pool.tensor_copy(idxb2[:, :], eplace[:, bass.ds(j * AHEAD, AHEAD)]))
                step.do(pool.tensor_copy(recb[:, :, :], rec[:, bass.ds(j * AHEAD, AHEAD), :]))
                pool.sem_inc(begun, 1)
                for n in range(AHEAD):
                    pool.indirect_dma_start(edge_dram, bass.IndirectOffsetOnAxis(ap=idxb2[:, n:n + 1], axis=0), recb[:, n, :], None,
                                            bounds_check=T * GE - 1, oob_is_err=False).then_inc(rec_stored, 16)
                pool.wait_ge(rec_stored, j * (16 * AHEAD) + 16 * AHEAD)
                pool.sem_inc(begun, 1)
            pool.dma_start(grec[:, :, :], edge_dram.rearrange("(q p) c -> p q c", p=128)).then_inc(grec_loaded, 16)
            pool.wait_ge(spec_ready, 1)
            pool.dma_start(v_dram.rearrange("(t p) -> p t", p=P), v_col[:, :], allow_slow_non_contiguous=True).then_inc(spec_out, 16)
            pool.wait_ge(spec_out, 16)
            pool.dma_start(vch[:, :], v_dram.rearrange("(c t) -> c t", t=BC)).then_inc(spec_in, 16)
            pool.wait_ge(spec_ready, 2)
            pool.dma_start(mat_dram, S[:, BC:BC + 2, :].rearrange("p a b -> p (a b)")).then_inc(spec_out, 16)
            pool.wait_ge(spec_out, 32)
            pool.dma_start(ml[:, :, :], mat_dram.rearrange("(a c) m -> a c m", a=1)).then_inc(spec_in, 16)
            pool.wait_ge(spec_ready, 3)
            pool.dma_start(rho_dram.rearrange("(a c) m -> a c m", a=1), rhoo[:, :, :]).then_inc(spec_out, 16)
            pool.wait_ge(spec_out, 48)
            pool.dma_start(rin[:, :, :].rearrange("p a b -> p (a b)"), rho_dram).then_inc(spec_in, 16)
            pool.wait_ge(spec_ready, 4)
            pool.dma_start(green_dram.rearrange("r (c t) -> c r t", t=BC), green[:, :, :]).then_inc(spec_out, 16)
            pool.wait_ge(spec_out, 64)
            pool.dma_start(feats[0:2], green_dram).then_inc(spec_in, 16)

            def gather_x(b, k):
                pool.wait_ge(rows_ready, 2 * k + b + 1)
                pool.sem_inc(begun, 1)
                for j in range(RT):
                    pool.indirect_dma_start(xg[b][j][:, :], None, xn_dram,
                                            bass.IndirectOffsetOnAxis(ap=xrow[:, b, j:j + 1], axis=0)).then_inc(x_gathered[b][j], 16)

            pool.wait_ge(layer_done, 2)
            pool.wait_ge(xn_stored, 16)
            gather_x(0, 0)
            gather_x(1, 0)

            with pool.Fori(1, REL // 2) as i:
                for b in range(2):
                    gather_x(b, i)

            def further_gather(m):
                pool.wait_ge(dve_more, m * 11 + 8)
                pool.sem_inc(begun, 1)
                pool.indirect_dma_start(xg[0][0][:, :], None, xn_dram,
                                        bass.IndirectOffsetOnAxis(ap=xrow[:, 0, 0:1], axis=0)).then_inc(m_gathered, 16)

            pool.wait_ge(more_ready, 1)
            further_tiles(pool, further_gather)

            pool.wait_ge(layer_done, 3)

            def gather_z(z_rows):
                with pool.Fori(0, ET // 4) as j:
                    for b in range(4):
                        pool.wait_ge(idx_used, j * 4 + b + 1)
                        pool.sem_inc(begun, 1)
                        pool.indirect_dma_start(zg[b][0:EP, :], None, z_rows,
                                                bass.IndirectOffsetOnAxis(ap=zib[b][:, :], axis=0)).then_inc(gathered[b], 16)

            total = pool.value_load(more_n[0:1, 0:1], min_val=0, max_val=MANY)

            def gather_groups(z_rows):
                for q in range(T * GT):
                    if q >= 5:
                        pool.wait_ge(msg_ready, q - 4)
                    pool.indirect_dma_start(zg[q % 5][:, :], None, z_rows,
                                            bass.IndirectOffsetOnAxis(ap=grow[:, q:q + 1], axis=0)).then_inc(gathered[q % 5], 16)

            largest = pool.value_load(crowded[0:1, 0:1], min_val=0, max_val=EDGES)
            for gather, rows in ((gather_z, "all"), (gather_groups, "fit")):
                with (pool.If(largest > GE) if rows == "all" else pool.Else()):
                    if rows == "fit":
                        pool.wait_ge(grow_ready, 1)
                    with pool.If(total > FEW):
                        gather(z_dram)
                    with pool.Else():
                        gather(z_dram[0:FIRST + FEW * 128, :])
            pool.wait_ge(layer_done, 4)
            step.do(pool.memset(earlier[:, :, :], 1.0))
            for i in range(T):
                step(pool.affine_select(out=earlier[:, i, :], in_=earlier[:, i, :], compare_op=ALU.is_gt, fill=0.0,
                                        base=i * P, pattern=[[-1, N]], channel_multiplier=1))
            step.sync()
            pool.sem_inc(earlier_ready, 1)
            pool.wait_ge(xn_stored, 32)
            for n in range(NE * RT):
                e, j = ITEMS[SH + n]
                if j == 0:
                    pool.wait_ge(rows2_ready, e + 1)
                if n >= 4:
                    pool.wait_ge(turned, n - 3)
                b = n % 4
                pool.indirect_dma_start(fx[b][:, :], None, xn_dram,
                                        bass.IndirectOffsetOnAxis(ap=xrow2[:, e, j:j + 1], axis=0)).then_inc(x_gathered[b // 2][b % 2], 16)

            def further_gather2(m):
                pool.wait_ge(dve_more2, m * 9 + 8)
                pool.sem_inc(begun, 1)
                pool.indirect_dma_start(fx[0][:, :], None, xn_dram,
                                        bass.IndirectOffsetOnAxis(ap=xrow2[:, 0, 0:1], axis=0)).then_inc(f_more_gathered, 16)

            pool.wait_ge(f_more_ready, 1)
            further_tiles(pool, further_gather2, f_n, MANY2)
            pool.wait_ge(yrow_ready, 1)
            pool.wait_ge(y_complete, 1)
            for n in range(2 * T):
                pool.indirect_dma_start(yg[n], None, y_dram,
                                        bass.IndirectOffsetOnAxis(ap=yrow[:, n % 2, n // 2:n // 2 + 1], axis=0)).then_inc(y_gathered[n // 2], 16)

        @block.scalar
        def _(act):
            step = Track(act, act_step)

            def evict(stage, q, k, dst_ap, src_ap, signal=None):
                act.wait_ge(full[q], BEFORE[stage][q] + k + 1)
                ins = act.activation(dst_ap, src_ap, ACT.Copy)
                step.do(ins)
                act.sem_inc(free[q], 1)
                if signal is not None:
                    act.sem_inc(signal, 1)

            def turn(stage):
                for k in range(K):
                    evict(stage, k % 4, k // 4, xT[:, k, :].rearrange("p (t c) -> p t c", c=P), psT(k % 4)[:, :, 0:P], xT_ready)

            def root(ready, k, ap_out, ap_in):
                act.wait_ge(ready, k)
                step.do(act.activation(ap_out, ap_in, ACT.Sqrt))
                act.sem_inc(std_ready, 1)

            def sides(q):
                return slot(q).rearrange("p (b c) -> p b c", c=BANK)[0:P, :, 0:HALF]

            def product(stage, dst_of, signal):
                for t in range(T):
                    to = dst_of(t)
                    of = sides(t % 4)
                    if stage in ("w1", "w2"):
                        act.wait_ge(al_taken, t + 1 + T * (stage == "w2"))
                    evict(stage, t % 4, t // 4, to, of.rearrange("p b (h c) -> p b h c", c=HC) if stage == "w1" else of, signal)

            for layer, (wa, heads) in enumerate(((wa1, HEADS), (wa2, 1))):
                with act.Fori(0, K) as k:
                    for s in range(2):
                        act.wait_ge(folded, k * 2 + s + 1 + 2 * K * layer)
                        for h in range(heads):
                            o = tmp[s][:, h * (D // heads):(h + 1) * (D // heads)]
                            ins = act.activation(o, o, ACT.Copy, accum_out=wa[:, bass.ds(k, 1), s, h:h + 1].rearrange("p o h -> p (o h)"))
                        ins.then_inc(fold_used, 1)
                if layer == 0:
                    root(var_ready, 1, rstd[:, :], t5[:, 0, :])
            act.wait_ge(fold_used, 4 * K + 2)
            act.sem_inc(wa_ready, 1)
            flat = counts[:, :, :].rearrange("p t n -> p (t n)")
            for q in range(3):
                evict("edges", q, 0, flat[:, q * 2 * BANK:(q + 1) * 2 * BANK], slot(q)[0:P, :])
            act.sem_inc(cnt_ready, 1)
            turn("turn1")
            act.wait_ge(deg_ready, 1)
            step.do(act.activation(dinv[:, :], t5[:, 7, :], ACT.Sqrt))
            act.sem_inc(deg_sqrt, 1)
            hv = hx[:, :, :].rearrange("p t (h c) -> p t h c", c=HC + 1)
            product("w1", lambda t: hv[:, t, :, 0:HC].rearrange("p (b h) c -> p b h c", b=2), h_ready)

            def exps(b, h, k1, k2):
                if not isinstance(h, int) or h >= 2:
                    act.wait_ge(full[3], h + (BEFORE["heads1"][3] - 1))
                act.wait_ge(full[1], k1)
                act.wait_ge(full[2], k2)
                for t in range(T):
                    for q, to, bias in ((1, e1[b], hcol[b][:, t, 0:1]), (2, e2[b], rcol[b][:, t, 0:1])):
                        ins = act.activation(to[:, t, :].rearrange("p (t c) -> p t c", c=P), psT(q)[0:P, :, 0:P],
                                             ACT.Exp, bias=bias)
                        if t == T - 1:
                            step.do(ins)
                            act.sem_inc(free[q], 1)
                    if t < T - 1:
                        ins.then_inc(exps_ready, 1)
                act.sem_inc(exps_ready, 1)

            def exps1(b, h):
                exps(b, h, h + BEFORE["heads1"][1] + 1, h + BEFORE["heads1"][2] + 1)

            for b in range(2):
                exps1(b, b)
            with step.turns(HEADS // 2 - 1, 4) as i:
                for b in range(2):
                    exps1(b, i * 2 + 2 + b)
            act.wait_ge(elu_in, 1)
            for t in range(T):
                step(act.activation(hx[:, t, 0:D], xn[:, t, :], ACT.Exp))
            step.sync()
            act.sem_inc(elu_exp, 1)
            turn("turn2")
            product("w2", lambda t: hx[:, t, 0:D].rearrange("p (b c) -> p b c", b=2), h_ready)
            exps(0, HEADS, BEFORE["heads2"][1] + 1, BEFORE["heads2"][2] + 1)

            def router(n):
                act.wait_ge(logits_in, n)
                step.do(act.activation(small[:, 1, :, :], small[:, 0, :, :], ACT.Exp))
                act.sem_inc(logits_exp, 1)

            root(var_ready, 2, rstd[:, :], t5[:, 0, :])
            turn("turn3")
            router(1)
            act.wait_ge(full[1], BEFORE["route1"][1] + 1)
            step.do(act.activation(combT[:, :].rearrange("p (t c) -> p t c", c=P), psT(1)[0:NE, :, 0:P], ACT.Copy))
            act.sem_inc(free[1], 1)
            act.wait_ge(full[2], BEFORE["route1"][2] + 1)
            step.do(act.activation(b1T[:, :], slot(2)[:, 0:FK], ACT.Copy))
            act.sem_inc(free[2], 1)
            act.sem_inc(act_done, 1)

            def gelus(c, b, k):
                act.wait_ge(full[b], BEFORE["inner1"][b] + 1 + k)
                step.do(act.activation(hT[:, c, :], slot(b)[:, 0:N], ACT.Gelu_apprx_tanh, bias=b1T[:, c:c + 1]))
                act.sem_inc(free[b], 1)
                act.sem_inc(act_done, 1)

            for c in range(FK):
                gelus(c, c % 2, c // 2)

            root(var_ready, 3, rstd[:, :], t5[:, 0, :])
            turn("turn4")
            KH = K // 2

            def w_high(i, b, *halves):
                for half in halves:
                    act.wait_ge(raw_loaded[half], at(i, b, 16, 16))
                    step.do(act.activation(whi[b][:, half * KH:(half + 1) * KH, :],
                                           raw[:, half * KH:(half + 1) * KH, :], ACT.Copy))
                    act.sem_inc(split_hi, 1)

            def columns_of(q):
                return slot(q)[:, 0:K * 128].rearrange("p (k c) -> p k c", k=K)

            def x_high(i, b, j):
                act.wait_ge(full[j], at(i, b, 1, BEFORE["relations"][j] + 1))
                step.do(act.activation(xhi[b][j][:, :, :], columns_of(j), ACT.Copy))
                act.sem_inc(xhi_ready, 1)

            def z_out(i, b, j, first):
                act.wait_ge(full[2 + j], at(i, b, 1, BEFORE["relations"][2 + j] + 1))
                if not first:
                    act.wait_ge(z_stored[b][j], i * 16)
                step.do(act.activation(zb[b][j].rearrange("p (b c) -> p b c", b=2),
                                       slot(2 + j).rearrange("p (b c) -> p b c", c=BANK)[:, :, 0:HALF], ACT.Copy))
                act.sem_inc(free[2 + j], 1)
                act.sem_inc(begun, 1)
                act.dma_start(z_dram[bass.ds(at(i, b, RT * 128, j * 128), 128), :], zb[b][j]).then_inc(z_stored[b][j], 16)

            def relation(i, b, more, first):
                for j in range(RT):
                    if more:
                        x_high(i + b, 1 - b, j)
                        if j == 0:
                            w_high(i + b, 1 - b, 0, 1)
                    z_out(i, b, j, first)

            act.wait_ge(z_filled, 1)
            act.wait_ge(xn_stored, 16)
            w_high(0, 0, 0, 1)
            for j in range(RT):
                x_high(0, 0, j)
            for b in range(2):
                relation(0, b, True, True)
            with act.Fori(1, REL // 2 - 1) as i:
                start = step.n
                A_STEPS = 2 * (2 + 2 * RT)
                step.extra = (i - 1) * A_STEPS
                for b in range(2):
                    relation(i, b, True, False)
                step.extra = None
            assert step.n - start == A_STEPS, step.n - start
            step.n = start + A_STEPS * (REL // 2 - 2)
            for b in range(2):
                relation(REL // 2 - 1, b, b == 0, False)
            for b in range(2):
                for j in range(RT):
                    act.wait_ge(z_stored[b][j], REL // 2 * 16)

            def further_tile(m):
                mine = Track(act, act_more)
                mine.extra = m * 4
                for half in range(2):
                    act.wait_ge(m_loaded[half], m * 16 + 16)
                    mine.do(act.activation(whi[0][:, half * KH:(half + 1) * KH, :],
                                           raw[:, half * KH:(half + 1) * KH, :], ACT.Copy))
                act.wait_ge(pe_more, m * 3 + 2)
                mine.do(act.activation(xhi[0][0][:, :, :], columns_of(0), ACT.Copy))
                act.wait_ge(pe_more, m * 3 + 3)
                act.wait_ge(m_stored, m * 16 + 16)
                mine.do(act.activation(zb[0][0].rearrange("p (b c) -> p b c", b=2),
                                       slot(2).rearrange("p (b c) -> p b c", c=BANK)[:, :, 0:HALF], ACT.Copy))
                assert mine.n == 4
                act.dma_start(z_dram[bass.ds(m * 128 + FIRST, 128), :], zb[0][0]).then_inc(m_stored, 16)
                act.sem_inc(begun, 1)

            act.wait_ge(more_ready, 1)
            act.sem_inc(m_stored, 16)
            further_tiles(act, further_tile)
            total = act.value_load(more_n[0:1, 0:1], min_val=0, max_val=MANY)
            act.wait_ge(m_stored, total * 16 + 16)
            act.sem_inc(layer_done, 1)

            def high(i, b, z):
                act.wait_ge(gathered[z], i * 16 + 16)
                act.wait_ge(hot_ready, i * 4 + z + 1)
                step.do(act.activation(mhi[b][0:EP, :], zg[z][0:EP, :], ACT.Copy, scale=gtmp[:, z:z + 1]))
                act.sem_inc(msg_hi, 1)

            largest = act.value_load(crowded[0:1, 0:1], min_val=0, max_val=EDGES)
            first_step = step.n
            with act.If(largest > GE):
                with step.turns(ET // 4, 4) as i:
                    for z in range(4):
                        high(i, z % 2, z)
            with act.Else():
                for q in range(T * GT):
                    act.wait_ge(gathered[q % 5], 16 * (q // 5 + 1))
                    if q >= 4:
                        act.wait_ge(msg_used, q - 3)
                    act.activation(mhi[q % 4][:, :], zg[q % 5][:, :], ACT.Copy, scale=grec[:, q, 1:2]).then_inc(msg_hi, 1)
                act.sem_inc(act_step, step.n - first_step)

            turn("turn5")
            product("wgcn", lambda t: xws[:, t, :].rearrange("p (b c) -> p b c", b=2), xw_ready)

            root(var_ready, 4, rstd[:, :], t5[:, 0, :])
            turn("turn6")
            router(2)

            def columns2(q):
                return slot(q)[:, 0:K * 128].rearrange("p (k c) -> p k c", k=K)

            def take_x(n):
                act.wait_ge(turned, n - SH + 1)
                step.do(act.activation(fxT[n % 2][:, :, :], columns2(0), ACT.Copy))
                act.sem_inc(x_taken, 1)

            def y_out(n):
                k = n - SH
                act.wait_ge(outer_full, n + 1)
                if k >= 2:
                    act.wait_ge(y_stored[k % 2], 16 * (k // 2))
                step.do(act.activation(yb[k % 2][:, :].rearrange("p (b c) -> p b c", b=2),
                                       slot(2).rearrange("p (b c) -> p b c", c=BANK)[:, :, 0:HALF], ACT.Copy))
                act.sem_inc(outer_taken, 1)
                act.dma_start(y_dram[k * 128:(k + 1) * 128, :], yb[k % 2][:, :]).then_inc(y_stored[k % 2], 16)

            def experts(first, end):
                for n in range(first, end + 1):
                    if SH <= n + 1 < min(end, OWN):
                        take_x(n + 1)
                    if n < end:
                        rows = P if ITEMS[n][0] is None else 128
                        act.wait_ge(inner_full, n + 1)
                        step.do(act.activation(gate[n % 2][0:rows, :], slot(1)[0:rows, 0:F], ACT.Silu))
                        act.sem_inc(gate_ready, 1)
                    if n > first and SH <= n - 1 < OWN:
                        y_out(n - 1)
                    if n < end:
                        act.wait_ge(h_turned, n + 1)
                        step.do(act.activation(hhT[n % 2][:, :, 0:rows],
                                               slot(1)[0:HC, BANK:BANK + 256].rearrange("p (c n) -> p c n", c=2)[:, :, 0:rows], ACT.Copy))
                        act.sem_inc(hT_ready, 1)
                    k = n - NE // 2
                    if n < end and 0 <= k < NE:
                        act.wait_ge(full[3], BEFORE["ranks2"][3] + k + 1)
                        step.do(act.activation(srow[k % 2][:, :, :], psT(3)[0:P, :, 0:P], ACT.Copy))
                        act.sem_inc(free[3], 1)
                        act.sem_inc(srow_ready, 1)

            experts(0, OWN)
            for b in range(2):
                act.wait_ge(y_stored[b], 16 * NE * RT // 2)

            def further_expert(m):
                mine = Track(act, act_more2)
                mine.extra = m * 4
                act.wait_ge(pe_more2, m * 5 + 2)
                mine.do(act.activation(fxT[0][:, :, :], columns2(0), ACT.Copy))
                act.wait_ge(pe_more2, m * 5 + 3)
                mine.do(act.activation(gate[0][:, :], slot(1)[:, 0:F], ACT.Silu))
                act.wait_ge(pe_more2, m * 5 + 4)
                mine.do(act.activation(hhT[0][:, :, :], slot(1)[0:HC, BANK:BANK + 256].rearrange("p (c n) -> p c n", c=2), ACT.Copy))
                act.wait_ge(pe_more2, m * 5 + 5)
                mine.do(act.activation(yb[0][:, :].rearrange("p (b c) -> p b c", b=2),
                                       slot(2).rearrange("p (b c) -> p b c", c=BANK)[:, :, 0:HALF], ACT.Copy))
                act.dma_start(y_dram[bass.ds(m * 128 + FIRST2, 128), :], yb[0][:, :]).then_inc(f_stored, 16)
                act.wait_ge(f_stored, m * 16 + 16)
                act.sem_inc(f_freed, 1)

            act.wait_ge(y_begun, 16 * (MANY2 // 4))
            act.wait_ge(f_more_ready, 1)
            further_tiles(act, further_expert, f_n, MANY2)
            act.sem_inc(y_complete, 1)
            experts(OWN, len(ITEMS))

        @block.vector
        def _(dve):
            step = Track(dve, dve_step)
            do = step.do

            def tt(o, a, b, op):
                return dve.tensor_tensor(o, a, b, op)

            def ts(o, a, s1, s2, op0, op1=None):
                return dve.tensor_scalar(o, a, s1, s2, op0) if op1 is None else dve.tensor_scalar(o, a, s1, s2, op0, op1)

            def free_slot(q):
                dve.sem_inc(free[q], 1)

            def norm(n, source):
                for t in range(T):
                    for s in range(2):
                        step(dve.bn_stats(stats[:, t, s, :], source[:, t, s * HALF:(s + 1) * HALF]))
                step.sync()
                for t in range(T):
                    step(dve.bn_aggr(mv[:, t, :], stats[:, t, :, :].rearrange("p a b -> p (a b)")))
                step.sync()
                do(ts(t5[:, 0, :], mv[:, :, 1], EPS, None, ALU.add))
                dve.sem_inc(var_ready, 1)
                dve.wait_ge(std_ready, n)
                do(dve.reciprocal(rstd[:, :], rstd[:, :]))
                for t in range(T):
                    do(ts(xn[:, t, :], source[:, t, :], mv[:, t, 0:1], rstd[:, t:t + 1], ALU.subtract, ALU.mult))
                    dve.sem_inc(xn_ready, 1)

            dve.wait_ge(ld_edges, 48)
            dve.wait_ge(consts_ready, 1)
            do(dve.tensor_copy(ef[:, :, :], eint[:, :, :]))
            step(dve.tensor_copy(dstf[:, :], ef[:, 1, :]))
            step(dve.scalar_tensor_tensor(cidx[:, 1, :], ef[:, 0, :], float(REL), ef[:, 2, :], ALU.mult, ALU.add))
            do(dve.scalar_tensor_tensor(cidx[:, 0, :], ef[:, 1, :], float(REL), ef[:, 2, :], ALU.mult, ALU.add))
            dve.sem_inc(cidx_ready, 1)

            def onehots(j, b, first):
                if not first:
                    dve.wait_ge(onehots_used, j + b - AHEAD + 1)
                dve.tensor_scalar(hot_s[b][:, :], iota16[:, 0:N], ef[:, 0, bass.ds(j + b, 1)], None, ALU.is_equal)
                dve.tensor_scalar(hot_dr[b][:, 0:N], iota16[:, 0:N], ef[:, 1, bass.ds(j + b, 1)], None, ALU.is_equal)
                dve.tensor_scalar(hot_dr[b][:, N:N + REL], iota34[:, :], ef[:, 2, bass.ds(j + b, 1)], None,
                                  ALU.is_equal).then_inc(onehots_ready, 1)

            for b in range(AHEAD):
                onehots(0, b, True)
            with dve.Fori(1, ET // AHEAD // 2) as i:
                for b in range(AHEAD):
                    onehots(i * AHEAD, b, False)
            dve.wait_ge(ld_x, 16)
            norm(1, x_res)
            with dve.Fori(ET // AHEAD // 2, ET // AHEAD) as i:
                for b in range(AHEAD):
                    onehots(i * AHEAD, b, False)
            scratch = e2[1][:, :, :].rearrange("p t n -> p (t n)")
            in_group, upto_a, upto_b, tmp_g = (scratch[:, n * T * ET:(n + 1) * T * ET].rearrange("p (g j) -> p g j", g=T) for n in range(4))
            for n in range(T):
                do(ts(in_group[:, n, :], dstf[:, :], float(n * P), None, ALU.is_ge))
                do(dve.scalar_tensor_tensor(in_group[:, n, :], dstf[:, :], float((n + 1) * P), in_group[:, n, :], ALU.is_lt, ALU.mult))
            do(dve.tensor_copy(upto_a, in_group))
            n, ga, gb = 1, upto_a, upto_b
            while n < ET:
                step(dve.tensor_copy(gb[:, :, 0:n], ga[:, :, 0:n]))
                do(tt(gb[:, :, n:ET], ga[:, :, n:ET], ga[:, :, 0:ET - n], ALU.add))
                n, ga, gb = 2 * n, gb, ga
            do(dve.tensor_copy(in_row[:, :], ga[:, :, ET - 1]))
            dve.sem_inc(in_row_ready, 1)
            dve.wait_ge(full[3], BEFORE["edges"][3] + 1)
            flat = counts[:, :, :].rearrange("p t n -> p (t n)")
            rest = T * (N + REL) - 6 * BANK
            do(dve.tensor_copy(flat[:, 6 * BANK:T * (N + REL)], slot(3)[0:P, 0:rest]))
            dve.sem_inc(cnt_ready, 1)
            step(ts(inv[:, :, :].rearrange("p t r -> p (t r)"), slot(3)[0:P, rest:rest + T * REL], 1.0, None, ALU.max))
            step.sync()
            free_slot(3)
            dve.wait_ge(cnt_ready, 2)
            do(ts(pres[:, :, :], counts[:, :, N:N + REL], 1.0, None, ALU.min))
            dve.sem_inc(pres_ready, 1)
            do(dve.reciprocal(inv[:, :, :], inv[:, :, :]))
            dve.sem_inc(inv_ready, 1)
            for t in range(T):
                dve.wait_ge(full[t % 4], BEFORE["mask"][t % 4] + t // 4 + 1)
                if t == 0:
                    do(ts(t5[:, 7, :], slot(0)[0:P, 700:700 + T], 1.0, None, ALU.add))
                    dve.sem_inc(deg_ready, 1)
                    do(ts(t5[:, 6, :], t5[:, 7, :], 1.0, -2e30, ALU.is_gt, ALU.mult))
                    do(ts(t5[:, 6, :], t5[:, 6, :], 1e30, None, ALU.add))
                do(ts(negm[:, t, :].rearrange("p (t c) -> p t c", c=P), psT(t % 4)[0:P, :, 0:P], 0.0, t5[:, 6, t:t + 1],
                      ALU.is_equal, ALU.mult))
                free_slot(t % 4)
            dve.wait_ge(full[1], BEFORE["ranks"][1] + 1)
            do(dve.memset(pos[:, :, REL:REL + 1], 0.0))
            do(dve.scalar_tensor_tensor(pos[:, :, 0:REL], slot(1)[0:P, 0:T * REL].rearrange("p (t r) -> p t r", t=T), 1.0,
                                        pres[:, :, :], ALU.add, ALU.mult))
            step(ts(pos[:, :, :], pos[:, :, :], -1.0, None, ALU.add))
            do(dve.tensor_copy(ran[:, 0, :], slot(1)[0:P, BANK:BANK + REL]))
            free_slot(1)
            do(ts(ran[:, 2, :], ran[:, 0, :], float(RT * 128), None, ALU.is_gt))
            for j in range(RT + 1, RT + MORE):
                do(dve.scalar_tensor_tensor(ran[:, 2, :], ran[:, 0, :], float(j * 128), ran[:, 2, :], ALU.is_gt, ALU.add))
            do(dve.tensor_copy(ran[:, 0, :], ran[:, 2, :]))
            n, a, b = 1, 0, 1
            while n < REL:
                step(dve.tensor_copy(ran[:, b, 0:n], ran[:, a, 0:n]))
                do(tt(ran[:, b, n:REL], ran[:, a, n:REL], ran[:, a, 0:REL - n], ALU.add))
                n, a, b = 2 * n, b, a
            upto = a
            do(tt(rel_row[:, 2, :], ran[:, upto, :], ran[:, 2, :], ALU.subtract))
            dve.wait_ge(consts_ready, 2)
            do(dve.scalar_tensor_tensor(rel_row[:, 1, :], rel_row[:, 2, :], 128.0, rel_row[:, 0, :], ALU.mult, ALU.subtract))
            do(ts(rel_row[:, 1, :], rel_row[:, 1, :], float(FIRST - RT * 128), None, ALU.add))
            do(ts(further[:, :, :], pos[:, :, 0:REL], float(RT * 128), None, ALU.is_ge))
            do(tt(further[:, :, :], further[:, :, :], rel_row[:, 1, :].unsqueeze(1).broadcast_to([P, T, REL]), ALU.mult))
            do(tt(further[:, :, :], further[:, :, :], rel_row[:, 0, :].unsqueeze(1).broadcast_to([P, T, REL]), ALU.add))
            do(tt(further[:, :, :], further[:, :, :], pos[:, :, 0:REL], ALU.add))
            do(ts(zrow[:, :, :], further[:, :, :], 0.0, None, ALU.max))
            dve.sem_inc(zrow_ready, 1)
            dve.wait_ge(full[2], BEFORE["ranks"][2] + 1)
            do(dve.tensor_copy(gcount[:, :, :], slot(2)[0:P, 0:2 * BANK].rearrange("p (b c) -> p b c", c=BANK)[:, :, 0:T]))
            free_slot(2)
            do(dve.tensor_reduce(gmax[:, :], gcount[0:1, 1, :], AX.X, ALU.max))
            do(dve.tensor_copy(crowded[:, :], gmax[:, :]))
            do(tt(ga, ga, in_group, ALU.subtract))
            do(tt(ga, ga, gcount[:, 0, :].unsqueeze(2).broadcast_to([P, T, ET]), ALU.add))
            do(ts(tmp_g, ga, float(GE), 1e6, ALU.is_ge, ALU.mult))
            do(tt(ga, ga, tmp_g, ALU.add))
            for n in range(1, T):
                do(ts(ga[:, n, :], ga[:, n, :], float(n * GE), None, ALU.add))
            do(tt(ga, ga, in_group, ALU.mult))
            do(dve.tensor_reduce(tmp_g[:, 0, :], ga.rearrange("p g j -> p j g"), AX.X, ALU.add))
            do(dve.tensor_copy(eplace[:, :], tmp_g[:, 0, :]))
            do(dve.tensor_copy(rec[:, :, 2], dstf[:, :]))
            for n in range(1, T):
                do(dve.scalar_tensor_tensor(rec[:, :, 2], in_group[:, n, :], float(-n * P), rec[:, :, 2], ALU.mult, ALU.add))
            dve.sem_inc(eplace_ready, 1)
            def in_list(r, b):
                do(dve.tensor_copy(poscol[:, :], pos[:, :, bass.ds(r, 1)].rearrange("p t o -> p (t o)")))
                for t in range(T):
                    step(dve.tensor_scalar(inlist[b][:, t, :], iota16[:, 0:RT * 128], poscol[:, t:t + 1], None, ALU.is_equal))
                step.sync()
                dve.sem_inc(inlist_ready, 1)

            def rows(q, b):
                L = slot(q)[:, LIST:LIST + 2 * RT].rearrange("p (j c) -> p j c", c=2)
                do(dve.tensor_copy(node[:, :], L[:, :, 0]))
                do(dve.scalar_tensor_tensor(xrow[:, b, :], L[:, :, 1], float(P), node[:, :], ALU.mult, ALU.add))
                dve.sem_inc(rows_ready, 1)

            over = e2[1][0:1, :, :].rearrange("p t n -> p (t n)")[:, 0:MANY * REL].rearrange("p (m r) -> p m r", r=REL)
            of = smore[:, :, :]
            by_tile = lambda a: a.unsqueeze(1).broadcast_to([1, MANY, REL])
            do(tt(over, by_tile(ran[0:1, upto, :]), iota16[0:1, 0:MANY].unsqueeze(2).broadcast_to([1, MANY, REL]), ALU.is_le))
            do(dve.tensor_reduce(of[:, 0, :], over, AX.X, ALU.add))
            do(tt(over, over, by_tile(ran[0:1, 2, :]), ALU.mult))
            do(dve.tensor_reduce(of[:, 1, :], over, AX.X, ALU.add))
            step(ts(more_at[:, 0, :], of[:, 0, :], float(REL - 1), None, ALU.min))
            do(tt(of[:, 1, :], iota16[0:1, 0:MANY], of[:, 1, :], ALU.subtract))
            do(ts(of[:, 1, :], of[:, 1, :], float(RT), float(RT + MORE - 1), ALU.add, ALU.min))
            step(dve.tensor_copy(more_at[:, 1, :], of[:, 1, :]))
            do(dve.tensor_copy(more_n[:, :], ran[0:1, upto, REL - 1:REL]))
            dve.sem_inc(more_ready, 1)
            dve.wait_ge(consts_ready, 2)
            for b in range(2):
                in_list(b, b)
            dve.wait_ge(deg_sqrt, 1)
            do(dve.reciprocal(dinv[:, :], dinv[:, :]))

            hv = hx[:, :, :].rearrange("p t (h c) -> p t h c", c=HC + 1)
            do(dve.memset(hv[:, :, :, HC:HC + 1], 1.0))
            for t in range(T):
                dve.wait_ge(full[t % 4], BEFORE["w1"][t % 4] + t // 4 + 1)
                do(dve.tensor_copy(al[:, t, :, :].rearrange("p s h -> p (s h)"),
                                   slot(t % 4)[0:P, BANK + HALF:BANK + HALF + 2 * HEADS]))
                dve.sem_inc(al_taken, 1)

            for b in range(2):
                dve.wait_ge(full[b], BEFORE["lists"][b] + 1)
                rows(b, b)
                free_slot(b)
            def columns(b, h):
                do(dve.tensor_copy(hcol[b][:, :, :], al[:, :, :, bass.ds(h, 1)].rearrange("p t s o -> p t (s o)")))
                do(ts(rcol[b][:, :, 0], hcol[b][:, :, 0], 0.2, None, ALU.mult))
                dve.sem_inc(cols_ready, 1)

            def maxima(b, k):
                dve.wait_ge(full[0], k)
                dve.sem_inc(begun, 1)
                for i in range(T):
                    step(dve.tensor_tensor_reduce(e1[b][:, i, :].rearrange("p (t c) -> p t c", c=P),
                                                  negm[:, i, :].rearrange("p (t c) -> p t c", c=P), psT(0)[0:P, :, 0:P],
                                                  1.0, -3e38, ALU.add, ALU.max, smax[:, 0, i:i + 1]))
                step.sync()
                free_slot(0)
                do(tt(smax[:, 1, :], smax[:, 0, :], hcol[b][:, :, 1], ALU.add))
                do(dve.scalar_tensor_tensor(smax[:, 2, :], smax[:, 1, :], 0.2, smax[:, 1, :], ALU.mult, ALU.max))
                step(tt(rcol[b][:, :, 1], hcol[b][:, :, 1], smax[:, 2, :], ALU.subtract))
                do(dve.scalar_tensor_tensor(rcol[b][:, :, 2], hcol[b][:, :, 1], 0.2, smax[:, 2, :], ALU.mult, ALU.subtract))
                dve.sem_inc(r_ready, 1)

            def weigh(b, h):
                for t in range(T):
                    if isinstance(h, int) and h == HEADS:
                        dve.wait_ge(exps_ready, h * T + t + 1)
                    do(tt(e2[b][:, t, :], e1[b][:, t, :], e2[b][:, t, :], ALU.max))
                    do(dve.scalar_tensor_tensor(e2[b][:, t, :], e2[b][:, t, :], 1.0, cnt[:, t, :], ALU.min, ALU.mult))
                dve.sem_inc(probs_ready, 1)

            def head_sums(h, k):
                dve.wait_ge(full[3], k)
                o = slot(3)[0:P, 0:T * (HC + 1)].rearrange("p (t c) -> p t c", c=HC + 1)
                do(ts(smax[:, 3, :], o[:, :, HC], 1e-16, None, ALU.add))
                do(dve.reciprocal(smax[:, 3, :], smax[:, 3, :]))
                do(tt(xn[:, :, bass.ds(h * HC, HC)], o[:, :, 0:HC], smax[:, 3, :].unsqueeze(2).broadcast_to([P, T, HC]), ALU.mult))
                free_slot(3)
                dve.sem_inc(agg_taken, 1)

            def head(b, h, more):
                dve.wait_ge(exps_ready, h * T + T)
                if more:
                    columns(b, h + 2)
                weigh(b, h)
                if not (isinstance(h, int) and h == 0):
                    head_sums(h - 1, h + BEFORE["heads1"][3])
                if more:
                    maxima(b, h + 2 + BEFORE["heads1"][0] + 1)

            HEAD_STEPS = 2 + 2 * T + T + 4 + 3
            dve.wait_ge(xT_ready, K)
            dve.wait_ge(inv_stored, 16)
            dve.wait_ge(zrow_stored, 16)
            for b in range(2):
                columns(b, b)
                maxima(b, b + BEFORE["heads1"][0] + 1)
            for b in range(2):
                head(b, b, True)
            with step.turns(HEADS // 2 - 2, 2 * HEAD_STEPS) as i:
                for b in range(2):
                    head(b, i * 2 + 2 + b, True)
            for b in range(2):
                head(b, HEADS - 2 + b, False)
            head_sums(HEADS - 1, HEADS + BEFORE["heads1"][3])

            for t in range(T):
                do(tt(xn[:, t, :], xn[:, t, :], brow[:, 0, :], ALU.add))
            dve.sem_inc(elu_in, 1)
            dve.wait_ge(elu_exp, 1)
            for t in range(T):
                do(ts(hx[:, t, 0:D], hx[:, t, 0:D], 1.0, -1.0, ALU.min, ALU.add))
                do(dve.scalar_tensor_tensor(xn[:, t, :], xn[:, t, :], 0.0, hx[:, t, 0:D], ALU.max, ALU.add))
                dve.sem_inc(xn_ready, 1)
            do(dve.memset(hx[:, :, D:D + 1], 1.0))
            for t in range(T):
                dve.wait_ge(full[t % 4], BEFORE["w2"][t % 4] + t // 4 + 1)
                do(dve.tensor_copy(al[:, t, :, 0:1].rearrange("p s h -> p (s h)"),
                                   slot(t % 4)[0:P, BANK + HALF:BANK + HALF + 2]))
                dve.sem_inc(al_taken, 1)

            def agg2():
                for i in range(T):
                    q = (3, 0)[i % 2]
                    base = BEFORE["heads2"][q] + (1 if q == 0 else 0)
                    dve.wait_ge(full[q], base + i // 2 + 1)
                    do(ts(smax[:, 1, 0:1], slot(q)[0:P, BANK + HALF:BANK + HALF + 1], 1e-16, None, ALU.add))
                    do(dve.reciprocal(smax[:, 1, 0:1], smax[:, 1, 0:1]))
                    do(dve.scalar_tensor_tensor(xn[:, i, :].rearrange("p (b c) -> p b c", b=2),
                                                slot(q).rearrange("p (b c) -> p b c", c=BANK)[0:P, :, 0:HALF],
                                                smax[:, 1, 0:1],
                                                x_res[:, i, :].rearrange("p (b c) -> p b c", b=2), ALU.mult, ALU.add))
                    free_slot(q)
                    do(tt(x_res[:, i, :], xn[:, i, :], brow[:, 1, :], ALU.add))

            columns(0, 0)
            maxima(0, BEFORE["heads2"][0] + 1)
            weigh(0, HEADS)
            agg2()
            dve.wait_ge(evw_ready, 1)
            dve.sem_inc(layer_done, 1)

            norm(2, x_res)

            def route(n, stage, bias):
                dve.wait_ge(full[0], BEFORE[stage][0] + 1)
                lg = slot(0)[0:P, 0:T * 16].rearrange("p (t c) -> p t c", c=16)
                L, E1, pr, k1, oh1, p2, oh2 = (small[:, i, :, :] for i in range(7))
                wide = lambda a: a.unsqueeze(2).broadcast_to([P, T, NE])
                if bias:
                    do(tt(pr, lg[:, :, 0:NE], gate_b[:, :].unsqueeze(1).broadcast_to([P, T, NE]), ALU.add))
                    do(ts(v_col[:, :], lg[:, :, NE], v_b[:, 0:1], -3.0, ALU.add, ALU.max))
                    do(ts(v_col[:, :], v_col[:, :], 3.0, -2.0, ALU.min, ALU.add))
                    dve.sem_inc(spec_ready, 1)
                else:
                    do(dve.tensor_copy(pr, lg[:, :, 0:NE]))
                free_slot(0)
                do(dve.tensor_reduce(t5[:, 1, :], pr, AX.X, ALU.max))
                do(tt(L, pr, wide(t5[:, 1, :]), ALU.subtract))
                dve.sem_inc(logits_in, 1)
                dve.wait_ge(logits_exp, n)
                do(dve.tensor_reduce(t5[:, 1, :], E1, AX.X, ALU.add))
                do(dve.reciprocal(t5[:, 1, :], t5[:, 1, :]))
                do(tt(pr, E1, wide(t5[:, 1, :]), ALU.mult))
                for m, source, hot in ((2, pr, oh1), (3, p2, oh2)):
                    do(dve.tensor_reduce(t5[:, m, :], source, AX.X, ALU.max))
                    do(tt(k1, source, wide(t5[:, m, :]), ALU.is_equal))
                    do(tt(k1, k1, rev[:, :].unsqueeze(1).broadcast_to([P, T, NE]), ALU.mult))
                    do(dve.tensor_reduce(t5[:, 4, :], k1, AX.X, ALU.max))
                    do(tt(hot, k1, wide(t5[:, 4, :]), ALU.is_equal))
                    if m == 2:
                        do(dve.scalar_tensor_tensor(p2, hot, -2.0, pr, ALU.mult, ALU.add))
                do(tt(t5[:, 4, :], t5[:, 2, :], t5[:, 3, :], ALU.add))
                if not bias:
                    do(ts(t5[:, 4, :], t5[:, 4, :], 1e-9, None, ALU.max))
                do(dve.reciprocal(t5[:, 4, :], t5[:, 4, :]))
                do(tt(asg[:, :, :], oh1, oh2, ALU.add))
                do(tt(comb1[:, :, :], pr, asg[:, :, :], ALU.mult))
                do(tt(comb1[:, :, :], comb1[:, :, :], wide(t5[:, 4, :]), ALU.mult))

            dve.wait_ge(ld_gate, 80)
            route(1, "route1", True)
            dve.sem_inc(comb_ready, 1)

            def widen(i, b):
                do(dve.tensor_copy(combw[b][:, :, :].rearrange("p t (e f) -> p t e f", e=2),
                                   comb1[:, :, 2 * i:2 * i + 2].unsqueeze(3).broadcast_to([P, T, 2, F])))
                dve.sem_inc(combw_ready, 1)

            def spectral_steps():
                dve.wait_ge(spec_in, 16)
                step(dve.tensor_copy(ar[:, 0, :], vch[:, :]))
                do(dve.tensor_copy(ar[:, 1, :], vch[:, ::-1]))
                step(ts(ar2[:, :, :, 0], ar[:, :, :].rearrange("p d t -> p t d"), -1.0, None, ALU.mult))
                step(dve.tensor_copy(ar2[:, :, :, 1], ar[:, :, :].rearrange("p d t -> p t d")))
                do(dve.memset(S[:, 0:2, :], 0.0))
                S5 = S[:, :, :].rearrange("p t (d k c) -> p t d k c", d=2, k=2)
                step(dve.memset(S5[:, 0, :, 1, 0:1], 1.0))
                do(dve.memset(S5[:, 1, :, 0, 0:1], 1.0))
                SW4 = SW[:, :, :].rearrange("p a (d k c) -> p a d k c", d=2, k=2)
                for t in range(BC):
                    step(tt(SW[:, 0, :], S[:, t + 1, :], S[:, t, :], ALU.add))
                    do(tt(SW4[:, 1, :, :, :], S5[:, t + 1, :, :, ::-1],
                          ar2[:, t, :, :].unsqueeze(2).broadcast_to([BC, 2, 2, 2]), ALU.mult))
                    do(tt(S[:, t + 2, :], SW[:, 0, :], SW[:, 1, :], ALU.add))
                    yield
                dve.sem_inc(spec_ready, 1)
                dve.wait_ge(spec_in, 32)
                m6 = ml[:, :, :].rearrange("o c (m d k r) -> o c m d k r", m=2, d=2, k=2)
                mo6 = mo[:, :, :, :].rearrange("o c d (k m r) -> o c d k m r", k=3, m=2)
                for d in range(2):
                    s = slice(None, None, -1) if d else slice(None)
                    for m in range(2):
                        step(dve.tensor_copy(mo6[:, :, d, 0, m, :], m6[:, s, m, d, 0, :]))
                        step(dve.tensor_copy(mo6[:, :, d, 1, m, :], m6[:, s, m, d, 1, :]))
                        step(ts(mo6[:, :, d, 2, m, 0], m6[:, s, m, d, 1, 1], -1.0, None, ALU.mult))
                        step(dve.tensor_copy(mo6[:, :, d, 2, m, 1], m6[:, s, m, d, 1, 0]))
                do(dve.memset(rho[:, 0:1, :, :], 0.0))
                for c in range(BC - 1):
                    cur = rho[:, c, :, :]
                    M4 = lambda k: mo[:, c, :, 4 * k:4 * k + 4]
                    step(tt(mt[:, 0, :, :], M4(1), cur[:, :, 0:1].broadcast_to([1, 2, 4]), ALU.mult))
                    do(tt(mt[:, 1, :, :], M4(2), cur[:, :, 1:2].broadcast_to([1, 2, 4]), ALU.mult))
                    do(tt(mt[:, 0, :, :], mt[:, 0, :, :], M4(0), ALU.add))
                    do(tt(mt[:, 0, :, :], mt[:, 0, :, :], mt[:, 1, :, :], ALU.add))
                    num, den = mt[:, 0, :, 0:2], mt[:, 0, :, 2:4]
                    nd = mt[:, 0, :, :].rearrange("o d (m r) -> o d m r", m=2)
                    step(tt(mt[:, 2, :, :].rearrange("o d (m r) -> o d m r", m=2), nd,
                            den.unsqueeze(2).broadcast_to([1, 2, 2, 2]), ALU.mult))
                    do(tt(mt[:, 3, :, 0:2], num, den[:, :, ::-1], ALU.mult))
                    step(dve.tensor_reduce(mt[:, 4, :, 0:3:2], mt[:, 2, :, :].rearrange("o d (m r) -> o d m r", m=2), AX.X, ALU.add))
                    do(tt(mt[:, 4, :, 1:2], mt[:, 3, :, 1:2], mt[:, 3, :, 0:1], ALU.subtract))
                    do(dve.reciprocal(mt[:, 4, :, 3:4], mt[:, 4, :, 2:3]))
                    do(tt(rho[:, c + 1, :, :], mt[:, 4, :, 0:2], mt[:, 4, :, 3:4].broadcast_to([1, 2, 2]), ALU.mult))
                    yield
                step(dve.tensor_copy(rhoo[:, :, 0:2], rho[:, 0:BC, 0, :]))
                do(dve.tensor_copy(rhoo[:, :, 2:4], rho[:, 0:BC, 1, :][:, ::-1, :]))
                dve.sem_inc(spec_ready, 1)
                dve.wait_ge(spec_in, 48)
                do(ts(nrin[:, :, :], rin[:, :, :], -1.0, None, ALU.mult))
                for d in range(2):
                    al_, be = S5[:, 1:, d, 0, :], S5[:, 1:, d, 1, :]
                    do(dve.scalar_tensor_tensor(sol[:, d, :, :], be, rin[:, d, 0:1], al_, ALU.mult, ALU.add))
                    step(dve.scalar_tensor_tensor(sol[:, d, :, 0], be[:, :, 1], nrin[:, d, 1:2], sol[:, d, :, 0], ALU.mult, ALU.add))
                    do(dve.scalar_tensor_tensor(sol[:, d, :, 1], be[:, :, 0], rin[:, d, 1:2], sol[:, d, :, 1], ALU.mult, ALU.add))
                for d in range(2):
                    X, Y = sol[:, d, 1:, :], sol[:, d, 0:BC, :]
                    q = lambda i: dq[:, i, d, :, :]
                    step(tt(q(0), X, Y, ALU.mult))
                    step(tt(q(1), X, Y[:, :, ::-1], ALU.mult))
                    do(tt(q(2), Y, Y, ALU.mult))
                    step(tt(q(3)[:, :, 0], q(1)[:, :, 1], q(1)[:, :, 0], ALU.subtract))
                    step(dve.scalar_tensor_tensor(q(3)[:, :, 1], q(0)[:, :, 0], -1.0, q(0)[:, :, 1], ALU.mult, ALU.subtract))
                    do(dve.tensor_reduce(q(4)[:, :, 0], q(2), AX.X, ALU.add))
                    do(dve.reciprocal(q(4)[:, :, 1], q(4)[:, :, 0]))
                    do(tt(q(5), q(3), q(4)[:, :, 1:2].broadcast_to([BC, BC, 2]), ALU.mult))
                do(tt(dq[:, 0, 0, :, :], dq[:, 5, 0, :, :], dq[:, 5, 1, ::-1, :], ALU.add))
                step(tt(dq[:, 0, 0, :, 0], dq[:, 0, 0, :, 0], ar[:, 0, :], ALU.subtract))
                do(ts(dq[:, 0, 0, :, 1], dq[:, 0, 0, :, 1], 1.0, None, ALU.add))
                do(tt(dq[:, 1, 0, :, :], dq[:, 0, 0, :, :], dq[:, 0, 0, :, :], ALU.mult))
                do(dve.tensor_reduce(dq[:, 2, 0, :, 0], dq[:, 1, 0, :, :], AX.X, ALU.add))
                do(dve.reciprocal(dq[:, 2, 0, :, 1], dq[:, 2, 0, :, 0]))
                step(tt(green[:, 0, :], dq[:, 0, 0, :, 0], dq[:, 2, 0, :, 1], ALU.mult))
                do(dve.scalar_tensor_tensor(green[:, 1, :], dq[:, 0, 0, :, 1], -1.0, dq[:, 2, 0, :, 1], ALU.mult, ALU.mult))
                do(ts(green[:, :, :], green[:, :, :], 10.0, -10.0, ALU.min, ALU.max))
                do(dve.memset(feats, 1.0))
                dve.sem_inc(spec_ready, 1)
                dve.wait_ge(ld_small, 80)
                do(tt(specw, specw, bkrow, ALU.mult))
                dve.sem_inc(specw_ready, 1)


            spectral = spectral_steps()
            widen(0, 0)
            widen(1, 1)
            for c in range(FK):
                dve.wait_ge(act_done, c + 2)
                dve.wait_ge(full[2 + c % 2], BEFORE["inner1"][2 + c % 2] + c // 2 + 1)
                do(tt(hT[:, c, :], hT[:, c, :], slot(2 + c % 2)[:, 0:N], ALU.mult))
                free_slot(2 + c % 2)
                dve.sem_inc(inner_done, 1)
                if c % 3 == 2 and c // 3 + 2 < NE // 2:
                    widen(c // 3 + 2, c // 3 % 2)
                for _ in range(3):
                    next(spectral, None)
            for _ in spectral:
                pass

            def add_result(stage):
                for t in range(T):
                    q = t % 4
                    dve.wait_ge(full[q], BEFORE[stage][q] + t // 4 + 1)
                    xr = x_res[:, t, :].rearrange("p (b c) -> p b c", b=2)
                    do(tt(xr, slot(q).rearrange("p (b c) -> p b c", c=BANK)[0:P, :, 0:HALF], xr, ALU.add))
                    free_slot(q)

            add_result("outer1")
            dve.sem_inc(layer_done, 1)

            norm(3, x_res)
            KH = K // 2

            def w_low(i, b, *halves):
                for half in halves:
                    dve.wait_ge(split_hi, at(i, b, 2, half + 1))
                    s = slice(half * KH, (half + 1) * KH)
                    do(tt(wlo[b][:, s, :], raw[:, s, :], whi[b][:, s, :].bitcast(f32), ALU.subtract))
                    dve.sem_inc(split_lo, 1)

            def columns_of(q):
                return slot(q)[:, 0:K * 128].rearrange("p (k c) -> p k c", k=K)

            def x_low(i, b, j):
                dve.wait_ge(xhi_ready, at(i, b, RT, j + 1))
                do(tt(xlo[b][j][:, :, :], columns_of(j), xhi[b][j][:, :, :].bitcast(f32), ALU.subtract))
                dve.sem_inc(xlo_ready, 1)

            def relation(i, b, listed, more):
                if more:
                    x_low(i + b, 1 - b, 0)
                if listed:
                    rows(0, b)
                if more:
                    free_slot(0)
                    w_low(i + b, 1 - b, 0, 1)
                if listed:
                    in_list(i * 2 + b + 3, 1 - b)
                if more:
                    x_low(i + b, 1 - b, 1)
                    free_slot(1)

            in_list(2, 0)
            w_low(0, 0, 0, 1)
            for j in range(RT):
                x_low(0, 0, j)
                free_slot(j)
            for b in range(2):
                relation(0, b, True, True)
            with dve.Fori(1, REL // 2 - 1) as i:
                start = step.n
                V_STEPS = 2 * (6 + 2 + 2 + 2)
                step.extra = (i - 1) * V_STEPS
                for b in range(2):
                    relation(i, b, True, True)
                step.extra = None
            assert step.n - start == V_STEPS, step.n - start
            step.n = start + V_STEPS * (REL // 2 - 2)
            for b in range(2):
                relation(REL // 2 - 1, b, False, b == 0)

            def further_tile(m):
                mine = Track(dve, dve_more)
                mine.extra = m * F_STEPS
                rel = dve.value_load(more_at[0:1, 0, bass.ds(m, 1)], min_val=0, max_val=REL - 1)
                tile = dve.value_load(more_at[0:1, 1, bass.ds(m, 1)], min_val=RT, max_val=RT + MORE - 1)
                mine.do(dve.tensor_copy(poscol[:, :], pos[:, :, bass.ds(rel, 1)].rearrange("p t o -> p (t o)")))
                for t in range(T):
                    mine(dve.tensor_scalar(inlist[0][:, t, 0:128], iota16[:, bass.ds(tile * 128, 128)], poscol[:, t:t + 1], None,
                                           ALU.is_equal))
                mine.sync()
                dve.wait_ge(pe_more, m * 3 + 1)
                mine.do(dve.tensor_copy(node[:, 0:1], slot(0)[:, LIST:LIST + 1]))
                mine.do(dve.scalar_tensor_tensor(xrow[:, 0, 0:1], slot(0)[:, LIST + 1:LIST + 2], float(P), node[:, 0:1],
                                                 ALU.mult, ALU.add))
                for half in range(2):
                    dve.wait_ge(act_more, m * 4 + half + 1)
                    s = slice(half * KH, (half + 1) * KH)
                    mine.do(tt(wlo[0][:, s, :], raw[:, s, :], whi[0][:, s, :].bitcast(f32), ALU.subtract))
                    dve.sem_inc(m_split_lo, 1)
                dve.wait_ge(act_more, m * 4 + 3)
                mine.do(tt(xlo[0][0][:, :, :], columns_of(0), xhi[0][0][:, :, :].bitcast(f32), ALU.subtract))
                assert mine.n == F_STEPS

            F_STEPS = 1 + T + 2 + 2 + 1
            further_tiles(dve, further_tile)

            dve.wait_ge(layer_done, 3)

            def message(j, z, first, more=True):
                b = z % 2
                if not first:
                    dve.wait_ge(msg_used, j + z - 1)
                step(dve.tensor_copy(gtmp[:, z:z + 1], evw[:, bass.ds(j + z, 1)]))
                do(dve.tensor_scalar(hotf[b][0:EP, :], iota16[:, 0:N], dstf[:, bass.ds(j + z, 1)], None, ALU.is_equal))
                dve.sem_inc(hot_ready, 1)
                dve.wait_ge(msg_hi, j + z + 1)
                do(dve.scalar_tensor_tensor(mlo[b][0:EP, :], zg[z][0:EP, :], gtmp[:, z:z + 1], mhi[b][0:EP, :].bitcast(f32),
                                            ALU.mult, ALU.subtract))
                dve.sem_inc(msg_ready, 1)
                if more:
                    do(dve.tensor_copy(zib[z][:, :], zidx[:, bass.ds(j + z + 4, 1)]))
                    dve.sem_inc(idx_used, 1)

            dve.wait_ge(grec_loaded, 16)
            do(dve.tensor_copy(grow[:, :], grec[:, :, 0]))
            dve.sem_inc(grow_ready, 1)
            largest = dve.value_load(crowded[0:1, 0:1], min_val=0, max_val=EDGES)
            first_step = step.n
            with dve.If(largest > GE):
                for z in range(4):
                    step(dve.tensor_copy(zib[z][:, :], zidx[:, z:z + 1]))
                step.sync()
                dve.sem_inc(idx_used, 4)
                for z in range(4):
                    message(0, z, z < 2)
                with step.turns(ET // 4 - 2, 16) as i:
                    for z in range(4):
                        message(i * 4 + 4, z, False)
                for z in range(4):
                    message(ET - 4, z, False, False)
                for q in range(4):
                    dve.wait_ge(full[q], BEFORE["messages"][q] + 1)
                do(dve.tensor_copy(h1[:, :, :], PS[0:P, 0:T * D].rearrange("p (t d) -> p t d", d=D)))
                for q in range(4):
                    free_slot(q)
                free_slot(0)
            with dve.Else():
                last_step, step.n = step.n, first_step

                def h1_out(n):
                    q = n % 4
                    dve.wait_ge(full[q], BEFORE["messages"][q] + n // 4 + 1)
                    do(dve.tensor_copy(h1[:, n, :].rearrange("p (b c) -> p b c", b=2),
                                       slot(q).rearrange("p (b c) -> p b c", c=BANK)[0:P, :, 0:HALF]))
                    free_slot(q)

                for q in range(T * GT):
                    if q >= 4:
                        dve.wait_ge(msg_used, q - 3)
                    dve.tensor_scalar(hotf[q % 4][:, 0:P], iota_all[:, 0:P], grec[:, q, 2:3], None, ALU.is_equal)
                    dve.wait_ge(msg_hi, q + 1)
                    dve.scalar_tensor_tensor(mlo[q % 4][:, :], zg[q % 5][:, :], grec[:, q, 1:2], mhi[q % 4][:, :].bitcast(f32),
                                             ALU.mult, ALU.subtract).then_inc(msg_ready, 1)
                    if q % GT == 10 and q > GT:
                        h1_out(q // GT - 1)
                h1_out(T - 1)
                dve.sem_inc(dve_step, last_step - step.n)
                step.n = last_step
            dve.sem_inc(h1_ready, 1)
            for t in range(T):
                do(tt(cnt[:, t, t * P:(t + 1) * P], cnt[:, t, t * P:(t + 1) * P], ident[0:P, 0:P], ALU.add))
                dve.wait_ge(xw_ready, t + 1)
                do(ts(xws[:, t, :], xws[:, t, :], dinv[:, t:t + 1], None, ALU.mult))
                dve.sem_inc(xws_ready, 1)
            dve.wait_ge(ld_gcn, 32)
            for t in range(T):
                q = t % 4
                dve.wait_ge(full[q], BEFORE["gcn"][q] + t // 4 + 1)
                xr = x_res[:, t, :].rearrange("p (b c) -> p b c", b=2)
                do(dve.scalar_tensor_tensor(xr, slot(q).rearrange("p (b c) -> p b c", c=BANK)[0:P, :, 0:HALF],
                                            dinv[:, t:t + 1], xr, ALU.mult, ALU.add))
                free_slot(q)
                do(tt(x_res[:, t, :], x_res[:, t, :], gbrow[:, :], ALU.add))
            dve.sem_inc(layer_done, 1)

            norm(4, x_res)
            route(2, "route2", False)
            do(dve.tensor_copy(asg16[:, :, :], asg[:, :, :]))
            dve.sem_inc(asg_ready, 1)
            score = small[:, 7, :, :]
            do(dve.scalar_tensor_tensor(score, asg[:, :, :], -1.0, comb1[:, :, :], ALU.add, ALU.add))
            dve.wait_ge(full[3], BEFORE["places"][3] + 1)
            do(dve.scalar_tensor_tensor(place[:, :, :], slot(3)[0:P, 0:T * NE].rearrange("p (t e) -> p t e", e=NE), 1.0,
                                        asg[:, :, :], ALU.add, ALU.mult))
            do(ts(place[:, :, :], place[:, :, :], -1.0, None, ALU.add))
            do(dve.tensor_copy(fn[:, 0, :], slot(3)[0:P, BANK:BANK + NE]))
            free_slot(3)

            def in_list2(e):
                for t in range(T):
                    step(dve.tensor_scalar(inlist2[e % 2][:, t, :], iota16[:, 0:RT * 128], place[:, t, e:e + 1], None, ALU.is_equal))
                step.sync()
                dve.sem_inc(inlist2_ready, 1)

            def rows2(e):
                dve.wait_ge(full[3], BEFORE["lists2"][3] + e // 2 + 1)
                L = slot(3)[:, e % 2 * 2 * RT:(e % 2 + 1) * 2 * RT].rearrange("p (j c) -> p j c", c=2)
                do(dve.tensor_copy(node[:, :], L[:, :, 0]))
                do(dve.scalar_tensor_tensor(xrow2[:, e, :], L[:, :, 1], float(P), node[:, :], ALU.mult, ALU.add))
                if e % 2 == 1:
                    free_slot(3)
                dve.sem_inc(rows2_ready, 1)

            def further_tables():
                do(ts(fn[:, 1, :], fn[:, 0, :], float(RT * 128), None, ALU.is_gt))
                for j in range(RT + 1, RT + MORE):
                    do(dve.scalar_tensor_tensor(fn[:, 1, :], fn[:, 0, :], float(j * 128), fn[:, 1, :], ALU.is_gt, ALU.add))
                do(dve.tensor_copy(fn[:, 2, :], fn[:, 1, :]))
                n, a, b = 1, 2, 3
                while n < NE:
                    step(dve.tensor_copy(fn[:, b, 0:n], fn[:, a, 0:n]))
                    do(tt(fn[:, b, n:NE], fn[:, a, n:NE], fn[:, a, 0:NE - n], ALU.add))
                    n, a, b = 2 * n, b, a
                by_tile = lambda v: v.unsqueeze(1).broadcast_to([1, MANY2, NE])
                do(tt(fover[:, :, :], by_tile(fn[0:1, a, :]), iota16[0:1, 0:MANY2].unsqueeze(2).broadcast_to([1, MANY2, NE]), ALU.is_le))
                do(dve.tensor_reduce(fof[:, 0, :], fover[:, :, :], AX.X, ALU.add))
                do(tt(fover[:, :, :], fover[:, :, :], by_tile(fn[0:1, 1, :]), ALU.mult))
                do(dve.tensor_reduce(fof[:, 1, :], fover[:, :, :], AX.X, ALU.add))
                step(ts(f_at[:, 0, :], fof[:, 0, :], float(NE - 1), None, ALU.min))
                do(tt(fof[:, 1, :], iota16[0:1, 0:MANY2], fof[:, 1, :], ALU.subtract))
                do(ts(fof[:, 1, :], fof[:, 1, :], float(RT), float(RT + MORE - 1), ALU.add, ALU.min))
                step(dve.tensor_copy(f_at[:, 1, :], fof[:, 1, :]))
                do(dve.tensor_copy(f_n[:, :], fn[0:1, a, NE - 1:NE]))
                dve.sem_inc(f_more_ready, 1)
                do(tt(frow[:, 1, :], fn[:, a, :], fn[:, 1, :], ALU.subtract))
                do(ts(frow[:, 0, :], rev[:, :], float(-RT * 128), float(NE * RT * 128), ALU.mult, ALU.add))
                do(dve.scalar_tensor_tensor(frow[:, 1, :], frow[:, 1, :], 128.0, frow[:, 0, :], ALU.mult, ALU.subtract))
                do(ts(frow[:, 1, :], frow[:, 1, :], float(FIRST2 - RT * 128), None, ALU.add))
                do(ts(yrow_f[:, :, :], place[:, :, :], float(RT * 128), None, ALU.is_ge))
                do(tt(yrow_f[:, :, :], yrow_f[:, :, :], frow[:, 1, :].unsqueeze(1).broadcast_to([P, T, NE]), ALU.mult))
                do(tt(yrow_f[:, :, :], yrow_f[:, :, :], frow[:, 0, :].unsqueeze(1).broadcast_to([P, T, NE]), ALU.add))
                do(tt(yrow_f[:, :, :], yrow_f[:, :, :], place[:, :, :], ALU.add))
                for c, hot in enumerate((4, 6)):
                    do(tt(ysel[:, :, :], yrow_f[:, :, :], small[:, hot, :, :], ALU.mult))
                    do(dve.tensor_reduce(yw[:, c, :], ysel[:, :, :], AX.X, ALU.add))
                do(dve.tensor_copy(yrow[:, :, :], yw[:, :, :]))
                dve.sem_inc(yrow_ready, 1)

            def rank(e):
                dve.wait_ge(srow_ready, e + 1)
                row = srow[e % 2][:, :, :]
                for i in range(T):
                    own = scol[e % 2][:, i:i + 1]
                    do(dve.tensor_scalar(compared[:, :, :], row, own, None, ALU.is_gt, ALU.add, accum_out=small[:, 8, i, e:e + 1]))
                    do(dve.scalar_tensor_tensor(compared[:, :, :], row, own, earlier[:, i, :].rearrange("p (t c) -> p t c", c=P),
                                                ALU.is_equal, ALU.mult, accum_out=small[:, 9, i, e:e + 1]))

            def column2(e):
                do(dve.tensor_copy(scol[e % 2][:, :], score[:, :, e]))
                dve.sem_inc(scol_ready, 1)

            dve.wait_ge(earlier_ready, 1)

            def experts(first, end):
                for n in range(first, end + 1):
                    if n < NE // 2:
                        in_list2(2 * n)
                        in_list2(2 * n + 1)
                    if n < end:
                        rows = P if ITEMS[n][0] is None else 128
                        dve.wait_ge(gate_ready, n + 1)
                        do(tt(hh[n % 2][0:rows, :], gate[n % 2][0:rows, :], slot(1)[0:rows, F:2 * F], ALU.mult))
                        dve.sem_inc(h2_ready, 1)
                    if n < NE // 2:
                        rows2(2 * n)
                        rows2(2 * n + 1)
                    if n > first and ITEMS[n - 1][0] is None:
                        dve.wait_ge(outer_full, n)
                        t = ITEMS[n - 1][1]
                        xr = x_res[:, t, :].rearrange("p (b c) -> p b c", b=2)
                        do(tt(xr, slot(2).rearrange("p (b c) -> p b c", c=BANK)[0:P, :, 0:HALF], xr, ALU.add))
                        dve.sem_inc(outer_taken, 1)
                    if n == NE // 2 - 1:
                        for k in range(2):
                            column2(k)
                    if n == NE // 2:
                        further_tables()
                    k = n - NE // 2 - 1
                    if 0 <= k < NE:
                        rank(k)
                        if k + 2 < NE:
                            column2(k + 2)

            experts(0, OWN)
            do(tt(small[:, 8, :, :], small[:, 8, :, :], small[:, 9, :, :], ALU.add))
            do(ts(small[:, 8, :, :], small[:, 8, :, :], float(CAP), None, ALU.is_lt))
            do(tt(comb1[:, :, :], comb1[:, :, :], small[:, 8, :, :], ALU.mult))
            for c, hot in enumerate((4, 6)):
                do(tt(ysel[:, :, :], comb1[:, :, :], small[:, hot, :, :], ALU.mult))
                do(dve.tensor_reduce(yw[:, c, :], ysel[:, :, :], AX.X, ALU.add))

            def further_expert(m):
                mine = Track(dve, dve_more2)
                mine.extra = m * G_STEPS
                e = dve.value_load(f_at[0:1, 0, bass.ds(m, 1)], min_val=0, max_val=NE - 1)
                tile = dve.value_load(f_at[0:1, 1, bass.ds(m, 1)], min_val=RT, max_val=RT + MORE - 1)
                mine.do(dve.tensor_copy(poscol[:, :], place[:, :, bass.ds(e, 1)].rearrange("p t o -> p (t o)")))
                for t in range(T):
                    mine(dve.tensor_scalar(inlist2[0][:, t, 0:128], iota16[:, bass.ds(tile * 128, 128)], poscol[:, t:t + 1], None,
                                           ALU.is_equal))
                mine.sync()
                dve.wait_ge(pe_more2, m * 5 + 1)
                mine.do(dve.tensor_copy(node[:, 0:1], slot(3)[:, 0:1]))
                mine.do(dve.scalar_tensor_tensor(xrow2[:, 0, 0:1], slot(3)[:, 1:2], float(P), node[:, 0:1], ALU.mult, ALU.add))
                dve.wait_ge(act_more2, m * 4 + 2)
                mine.do(tt(hh[0][:, :], gate[0][:, :], slot(1)[:, F:2 * F], ALU.mult))
                assert mine.n == G_STEPS

            G_STEPS = 1 + T + 2 + 1
            further_tiles(dve, further_expert, f_n, MANY2)
            experts(OWN, len(ITEMS))
            for t in range(T):
                dve.wait_ge(y_gathered[t], 32)
                for c in range(2):
                    do(dve.scalar_tensor_tensor(x_res[:, t, :], yg[2 * t + c], yw[:, c, t:t + 1], x_res[:, t, :], ALU.mult, ALU.add))
                dve.sem_inc(tile_done, 1)

        @block.tensor
        def _(pe):
            def take(stage, q, k):
                n = k + BEFORE[stage][q]
                if not isinstance(n, int) or n > 0:
                    pe.wait_ge(free[q], n)

            def piece(o, c0, n):
                while n:
                    m = min(n, BANK - c0 % BANK)
                    yield o, c0, m
                    c0, o, n = c0 + m, o + m, n - m

            pe.wait_ge(consts_ready, 1)

            def count(b, start):
                for i in range(T):
                    for o, c, m in piece(0, i * (N + REL), N + REL):
                        pe.matmul(PS[0:P, c:c + m], hot_s[b][:, i * P:(i + 1) * P], hot_dr[b][:, o:o + m],
                                  start=start and c % BANK == 0, stop=False, skip_group_check=True)
                for i in range(T):
                    c = T * (N + REL) + i * REL
                    last = pe.matmul(PS[0:P, c:c + REL], hot_dr[b][:, i * P:(i + 1) * P], hot_dr[b][:, N:N + REL],
                                     start=False, stop=False, skip_group_check=True)
                return last

            for b in range(AHEAD):
                pe.wait_ge(onehots_ready, b + 1)
                count(b, b == 0).then_inc(onehots_used, 1)
            with pe.Fori(1, ET // AHEAD) as i:
                for b in range(AHEAD):
                    pe.wait_ge(onehots_ready, i * AHEAD + b + 1)
                    count(b, False).then_inc(onehots_used, 1)
            pe.wait_ge(onehots_used, ET)
            for q in range(4):
                pe.sem_inc(full[q], 1)

            def turn(stage, source, ready):
                ready()
                for k in range(K):
                    take(stage, k % 4, k // 4)
                    for t in range(T):
                        mm = pe.transpose(psT(k % 4)[:, t, 0:P], source[:, t, k * 128:(k + 1) * 128], ident[0:P, 0:P])
                    mm.then_inc(full[k % 4], 1)

            def product(stage, weights, turns_done, extra=None):
                pe.wait_ge(xT_ready, turns_done * K)
                for t in range(T):
                    take(stage, t % 4, t // 4)
                    for k in range(K):
                        for s in range(2):
                            mm = pe.matmul(slot(t % 4)[0:P, s * BANK:s * BANK + HALF], xT[:, k, t * P:(t + 1) * P],
                                           weights[:, k, s * HALF:(s + 1) * HALF], start=(k == 0), stop=(k == K - 1))
                    if extra is not None:
                        n = extra.shape[2] * extra.shape[3]
                        for k in range(K):
                            mm = pe.matmul(slot(t % 4)[0:P, BANK + HALF:BANK + HALF + n], xT[:, k, t * P:(t + 1) * P],
                                           extra[:, k, :, :].rearrange("p s h -> p (s h)"), start=(k == 0), stop=(k == K - 1))
                    mm.then_inc(full[t % 4], 1)

            def spread(q, column):
                for t in range(T):
                    mm = pe.matmul(psT(q)[0:P, t, 0:P], column(t).broadcast_to([P, P]), ident[0:P, 0:P],
                                   start=True, stop=True)
                mm.then_inc(full[q], 1)

            turn("turn1", xn, lambda: pe.wait_ge(xn_ready, T))

            pe.wait_ge(cnt_ready, 2)
            for i in range(T):
                take("mask", i % 4, i // 4)
                for t in range(T):
                    mm = pe.transpose(psT(i % 4)[0:P, t, 0:P], cnt[:, t, i * P:(i + 1) * P], ident[0:P, 0:P])
                if i == 0:
                    for j in range(T):
                        for t in range(T):
                            mm = pe.matmul(slot(0)[0:P, 700 + j:701 + j], cnt[:, t, j * P:(j + 1) * P], ones[0:P, 0:1],
                                           start=(t == 0), stop=(t == T - 1))
                mm.then_inc(full[i % 4], 1)
            pe.wait_ge(pres_ready, 1)
            pe.wait_ge(consts_ready, 2)
            take("ranks", 1, 0)
            for i in range(T):
                for t in range(i + 1):
                    pe.matmul(slot(1)[0:P, i * REL:(i + 1) * REL], before[:, :] if t == i else ones[0:P, 0:P], pres[:, t, :],
                              start=(t == 0), stop=(t == i))
            pe.wait_ge(in_row_ready, 1)
            take("ranks", 2, 0)
            pe.matmul(slot(2)[0:P, 0:T], before[:, :], in_row[:, :], start=True, stop=True)
            pe.matmul(slot(2)[0:P, BANK:BANK + T], ones[0:P, 0:P], in_row[:, :], start=True, stop=True).then_inc(full[2], 1)
            for t in range(T):
                mm = pe.matmul(slot(1)[0:P, BANK:BANK + REL], ones[0:P, 0:P], pres[:, t, :], start=(t == 0), stop=(t == T - 1))
            mm.then_inc(full[1], 1)

            pe.wait_ge(ld_w1, 16)
            pe.wait_ge(wa_ready, 1)
            product("w1", gw[0], 1, wa1)

            def list_rows(q, hot, j0, n):
                for j in range(n):
                    for t in range(T):
                        mm = pe.matmul(slot(q)[:, LIST + 2 * j:LIST + 2 * j + 2], hot[:, t, (j0 + j) * 128:(j0 + j + 1) * 128],
                                       node_of[:, t, :], start=(t == 0), stop=(t == T - 1))
                return mm

            for b in range(2):
                pe.wait_ge(inlist_ready, b + 1)
                take("lists", b, 0)
                list_rows(b, inlist[b], 0, RT).then_inc(full[b], 1)
            def source_row(stage, b, h, k):
                pe.wait_ge(cols_ready, h + 1)
                take(stage, 0, k)
                spread(0, lambda t: hcol[b][:, t, 0:1])

            def target_rows(stage, b, h, k):
                pe.wait_ge(r_ready, h + 1)
                for q in (1, 2):
                    take(stage, q, k)
                    spread(q, lambda t: rcol[b][:, t, q:q + 1])

            def head_product(b, h):
                take("heads1", 3, h)
                pe.wait_ge(probs_ready, h + 1)
                for i in range(T):
                    for t in range(T):
                        mm = pe.matmul(slot(3)[0:P, i * (HC + 1):(i + 1) * (HC + 1)], e2[b][:, t, i * P:(i + 1) * P],
                                       hx[:, t, bass.ds(h * (HC + 1), HC + 1)], start=(t == 0), stop=(t == T - 1))
                mm.then_inc(full[3], 1)

            for b in range(2):
                source_row("heads1", b, b, b)
                target_rows("heads1", b, b, b)
            with pe.Fori(0, HEADS // 2 - 1) as i:
                for b in range(2):
                    source_row("heads1", b, i * 2 + 2 + b, i * 2 + 2 + b)
                    head_product(b, i * 2 + b)
                    target_rows("heads1", b, i * 2 + 2 + b, i * 2 + 2 + b)
            for b in range(2):
                head_product(b, HEADS - 2 + b)

            turn("turn2", xn, lambda: pe.wait_ge(xn_ready, 2 * T))
            pe.wait_ge(ld_w2, 16)
            product("w2", gw[1], 2, wa2)
            source_row("heads2", 0, HEADS, 0)
            target_rows("heads2", 0, HEADS, 0)
            pe.wait_ge(probs_ready, HEADS + 1)
            for i in range(T):
                q = (3, 0)[i % 2]
                take("heads2", q, i // 2 + (1 if q == 0 else 0))
                for t in range(T):
                    for s in range(2):
                        n = HALF + s
                        mm = pe.matmul(slot(q)[0:P, s * BANK:s * BANK + n], e2[0][:, t, i * P:(i + 1) * P],
                                       hx[:, t, s * HALF:s * HALF + n], start=(t == 0), stop=(t == T - 1))
                mm.then_inc(full[q], 1)

            turn("turn3", xn, lambda: pe.wait_ge(xn_ready, 3 * T))

            def logits(stage, weights, n, turns_done):
                pe.wait_ge(xT_ready, turns_done * K)
                take(stage, 0, 0)
                for t in range(T):
                    for k in range(K):
                        mm = pe.matmul(slot(0)[0:P, 16 * t:16 * t + n], xT[:, k, t * P:(t + 1) * P], weights[:, k, :],
                                       start=(k == 0), stop=(k == K - 1))
                mm.then_inc(full[0], 1)

            pe.wait_ge(ld_gate, 80)
            logits("route1", gate_sb, NE + 1, 3)
            pe.wait_ge(comb_ready, 1)
            take("route1", 1, 0)
            for t in range(T):
                mm = pe.transpose(psT(1)[0:NE, t, 0:P], comb1[:, t, :], ident[0:P, 0:P])
            mm.then_inc(full[1], 1)
            pe.wait_ge(ld_small, 80)
            take("route1", 2, 0)
            pe.transpose(slot(2)[:, 0:FK], b1r[:, :], ident[0:FK, 0:FK]).then_inc(full[2], 1)

            def inner(dst_ps, weights, c, rows=128):
                for k in range(K):
                    for o, n in ((0, BANK), (BANK, N - BANK)):
                        mm = pe.matmul(dst_ps[0:rows, o:o + n], weights[:, k, c * rows:(c + 1) * rows],
                                       xT[:, k, o:o + n], start=(k == 0), stop=(k == K - 1))
                return mm

            def weights_row(q, b, c):
                for t in range(T):
                    for o, p0, n in piece(0, t * P, P):
                        mm = pe.matmul(slot(q)[:, p0:p0 + n], combw[b][:, t, c * 128:(c + 1) * 128],
                                       ident[0:P, o:o + n], start=True, stop=True)
                mm.then_inc(full[q], 1)

            LAG = 1
            for n in range(FK + LAG):
                if n < FK:
                    c, i, b = n, n // 3, n // 3 % 2
                    pe.wait_ge(ld_f1[b], 32 * (i // 2 + 1))
                    take("inner1", c % 2, c // 2)
                    inner(slot(c % 2), fw1[b], c % 3).then_inc(full[c % 2], 1)
                if n >= LAG:
                    c, i, b = n - LAG, (n - LAG) // 3, (n - LAG) // 3 % 2
                    take("inner1", 2 + c % 2, c // 2)
                    pe.wait_ge(combw_ready, i + 1)
                    weights_row(2 + c % 2, b, c % 3)

            def outer(stage, chunks, after):
                pe.wait_ge(ld_f2, 16 if stage == "outer1" else 48)
                for first, end in ((0, 4), (4, 5)):
                    for t in range(first, end):
                        take(stage, t % 4, t // 4)
                        for c, rows in chunks:
                            for s in range(2):
                                mm = pe.matmul(slot(t % 4)[0:P, s * BANK:s * BANK + HALF], hT[0:rows, c, t * P:(t + 1) * P],
                                               fw2[0:rows, c, s * HALF:(s + 1) * HALF], start=(c == 0),
                                               stop=(after is None and c == chunks[-1][0]))
                        if after is None:
                            mm.then_inc(full[t % 4], 1)
                    if after is not None:
                        for t in range(first, end):
                            after(t)

            def spectral(t):
                if t == 0:
                    pe.wait_ge(spec_in, 64)
                    pe.wait_ge(specw_ready, 1)
                for s in range(2):
                    o = slot(t % 4)[0:P, s * BANK:s * BANK + HALF]
                    pe.matmul(o, combT[:, t * P:(t + 1) * P], b2r[:, s * HALF:(s + 1) * HALF], start=False, stop=False)
                    mm = pe.matmul(o, feats[:, t * P:(t + 1) * P], specw[:, s * HALF:(s + 1) * HALF],
                                   start=False, stop=True)
                mm.then_inc(full[t % 4], 1)

            pe.wait_ge(act_done, 1)
            pe.wait_ge(inner_done, FK)
            outer("outer1", [(c, 128) for c in range(FK)], spectral)

            turn("turn4", xn, lambda: pe.wait_ge(xn_ready, 4 * T))
            def turn_rows(q, rows_of, done):
                for k in range(K):
                    mm = pe.transpose(slot(q)[:, k * 128:(k + 1) * 128], rows_of[:, k * 128:(k + 1) * 128], ident[:, :])
                mm.then_inc(done, 1)

            def take_r(q, i, b):
                pe.wait_ge(free[q], at(i, b, 1, BEFORE["relations"][q]))

            def relation_product(q, hi, lo, b, done):
                for k in range(K):
                    for part, (a, wt) in enumerate(((hi, whi[b]), (hi, wlo[b]), (lo, whi[b]))):
                        for s in range(2):
                            mm = pe.matmul(slot(q)[:, s * BANK:s * BANK + HALF], a[:, k, :],
                                           wt[:, k, s * HALF:(s + 1) * HALF],
                                           start=(k == 0 and part == 0), stop=(k == K - 1 and part == 2))
                mm.then_inc(done, 1)

            def relation(i, b, listed, more):
                if more:
                    if listed:
                        pe.wait_ge(inlist_ready, at(i, b, 1, 3))
                    take_r(0, i, b + 1)
                    if listed:
                        list_rows(0, inlist[b], 0, RT)
                    pe.wait_ge(x_gathered[1 - b][0], at(i, b, 8, 16) if b == 0 else at(i, b, 8, 24))
                    turn_rows(0, xg[1 - b][0], full[0])
                pe.wait_ge(split_lo, at(i, b, 2, 2))
                pe.wait_ge(xlo_ready, at(i, b, RT, 1))
                take_r(2, i, b)
                relation_product(2, xhi[b][0], xlo[b][0], b, full[2])
                if more:
                    take_r(1, i, b + 1)
                    pe.wait_ge(x_gathered[1 - b][1], at(i, b, 8, 16) if b == 0 else at(i, b, 8, 24))
                    turn_rows(1, xg[1 - b][1], full[1])
                pe.wait_ge(xlo_ready, at(i, b, RT, 2))
                take_r(3, i, b)
                relation_product(3, xhi[b][1], xlo[b][1], b, full[3])

            for j in range(RT):
                take_r(j, 0, 0)
                pe.wait_ge(x_gathered[0][j], 16)
                turn_rows(j, xg[0][j], full[j])
            with pe.Fori(0, REL // 2 - 1) as i:
                for b in range(2):
                    relation(i, b, True, True)
            for b in range(2):
                relation(REL // 2 - 1, b, False, b == 0)

            def further_tile(m):
                pe.wait_ge(dve_more, m * 11 + 6)
                list_rows(0, inlist[0], 0, 1).then_inc(pe_more, 1)
                pe.wait_ge(m_gathered, m * 16 + 16)
                turn_rows(0, xg[0][0], pe_more)
                pe.wait_ge(m_split_lo, m * 2 + 4)
                pe.wait_ge(dve_more, m * 11 + 11)
                relation_product(2, xhi[0][0], xlo[0][0], 0, pe_more)
                pe.wait_ge(act_more, m * 4 + 4)
                pe.sem_inc(begun, 1)

            for q in range(4):
                take("messages", q, 0)
            further_tiles(pe, further_tile)

            for q in range(4):
                take("messages", q, 0)

            def scatter(b, start):
                for part in (mhi[b], mlo[b]):
                    for i in range(T):
                        for o, c, m in piece(0, i * D, D):
                            mm = pe.matmul(PS[0:P, c:c + m], hotf[b][0:EP, i * P:(i + 1) * P], part[0:EP, o:o + m],
                                           start=start and part is mhi[b] and c % BANK == 0, stop=False, skip_group_check=True)
                mm.then_inc(msg_used, 1)

            largest = pe.value_load(crowded[0:1, 0:1], min_val=0, max_val=EDGES)
            with pe.If(largest > GE):
                for b in range(2):
                    pe.wait_ge(msg_ready, b + 1)
                    scatter(b, b == 0)
                with pe.Fori(1, ET // 2) as i:
                    for b in range(2):
                        pe.wait_ge(msg_ready, i * 2 + b + 1)
                        scatter(b, False)
                pe.wait_ge(ld_root, 32)
                for i in range(T):
                    for o, c, m in piece(0, i * D, D):
                        for k in range(K):
                            pe.matmul(PS[0:P, c:c + m], xT[:, k, i * P:(i + 1) * P], wroot[:, k, o:o + m],
                                      start=False, stop=False, skip_group_check=True)
                        mm = pe.matmul(PS[0:P, c:c + m], ones[0:1, 0:P], rbrow[:, o:o + m],
                                       start=False, stop=True, skip_group_check=True)
                mm.then_inc(full[0], 1)
                pe.wait_ge(full[0], BEFORE["messages"][0] + 1)
                for q in range(1, 4):
                    pe.sem_inc(full[q], 1)
                pe.sem_inc(full[0], 1)
            with pe.Else():
                for n in range(T):
                    take("messages", n % 4, n // 4)
                    for q in range(n * GT, (n + 1) * GT):
                        pe.wait_ge(msg_ready, q + 1)
                        for high, part in ((True, mhi[q % 4]), (False, mlo[q % 4])):
                            for s in range(2):
                                mm = pe.matmul(slot(n % 4)[0:P, s * BANK:s * BANK + HALF], hotf[q % 4][:, 0:P],
                                               part[:, s * HALF:(s + 1) * HALF],
                                               start=q == n * GT and high,
                                               stop=q == (n + 1) * GT - 1 and not high, skip_group_check=True)
                        mm.then_inc(msg_used, 1)
                        k = q - (n + 1) * GT + K + 2
                        if n == 0 and k == 0:
                            pe.wait_ge(ld_root, 32)
                        if 0 <= k <= K:
                            for s in range(2):
                                a, r = (xT[:, k, n * P:(n + 1) * P], wroot[:, k, s * HALF:(s + 1) * HALF]) if k < K else \
                                    (ones[0:1, 0:P], rbrow[:, s * HALF:(s + 1) * HALF])
                                mm = pe.matmul(slot(n % 4)[0:P, s * BANK:s * BANK + HALF], a, r, start=False, stop=False,
                                               skip_group_check=True)
                    pe.wait_ge(msg_used, (n + 1) * GT)
                    pe.sem_inc(full[n % 4], 1)

            turn("turn5", h1, lambda: pe.wait_ge(h1_ready, 1))
            pe.wait_ge(ld_gcn, 32)
            product("wgcn", wgcn, 5)
            pe.wait_ge(xws_ready, T)
            for i in range(T):
                take("gcn", i % 4, i // 4)
                for t in range(T):
                    for s in range(2):
                        mm = pe.matmul(slot(i % 4)[0:P, s * BANK:s * BANK + HALF], cnt[:, t, i * P:(i + 1) * P],
                                       xws[:, t, s * HALF:(s + 1) * HALF], start=(t == 0), stop=(t == T - 1))
                mm.then_inc(full[i % 4], 1)

            turn("turn6", xn, lambda: pe.wait_ge(xn_ready, 5 * T))
            logits("route2", wr_sb, NE, 6)
            for q in range(4):
                pe.wait_ge(free[q], BEFORE["places"][q])

            def turn_x(rows_of, done):
                for k in range(K):
                    mm = pe.transpose(slot(0)[:, k * 128:(k + 1) * 128], rows_of[:, k * 128:(k + 1) * 128], ident[:, :])
                mm.then_inc(done, 1)

            def inner_product(xt, weights, rows, done):
                for k in range(K):
                    mm = pe.matmul(slot(1)[0:rows, 0:2 * F], xt(k), weights[:, k, :], start=(k == 0), stop=(k == K - 1))
                mm.then_inc(done, 1)

            def turn_h(h, rows, done):
                for c in range(2):
                    mm = pe.transpose(slot(1)[0:HC, BANK + c * 128:BANK + c * 128 + rows], h[0:rows, c * HC:(c + 1) * HC], ident[0:rows, 0:rows])
                mm.then_inc(done, 1)

            def outer_product(ht, weights, rows, done):
                for c in range(2):
                    for s in range(2):
                        mm = pe.matmul(slot(2)[0:rows, s * BANK:s * BANK + HALF], ht[:, c, 0:rows], weights[:, c, s * HALF:(s + 1) * HALF],
                                       start=(c == 0), stop=(c == 1))
                mm.then_inc(done, 1)

            def places():
                pe.wait_ge(asg_ready, 1)
                for i in range(T):
                    for t in range(i + 1):
                        pe.matmul(slot(3)[0:P, i * NE:(i + 1) * NE], before16[:, :] if t == i else ones16[:, :], asg16[:, t, :],
                                  start=(t == 0), stop=(t == i))
                for t in range(T):
                    mm = pe.matmul(slot(3)[0:P, BANK:BANK + NE], ones16[:, :], asg16[:, t, :], start=(t == 0), stop=(t == T - 1))
                mm.then_inc(full[3], 1)

            def list2(e):
                pe.wait_ge(inlist2_ready, e + 1)
                if e % 2 == 0:
                    take("lists2", 3, e // 2)
                for j in range(RT):
                    c = 2 * (e % 2 * RT + j)
                    for t in range(T):
                        mm = pe.matmul(slot(3)[:, c:c + 2], inlist2[e % 2][:, t, j * 128:(j + 1) * 128], node_of[:, t, :],
                                       start=(t == 0), stop=(t == T - 1))
                if e % 2 == 1:
                    mm.then_inc(full[3], 1)

            pe.wait_ge(ld_shared, 48)
            def experts(first, end):
                for n in range(first, end + 1):
                    if SH <= n + 1 < min(end, OWN):
                        k = n + 1 - SH
                        pe.wait_ge(x_gathered[k % 4 // 2][k % 2], 16 * (REL // 2 + k // 4 + 1))
                        if k > 0:
                            pe.wait_ge(x_taken, k)
                        turn_x(fx[k % 4], turned)
                    if n < end:
                        e, j = ITEMS[n]
                        rows = P if e is None else 128
                        if n > 0:
                            pe.wait_ge(h2_ready, n)
                        if e is None:
                            inner_product(lambda k: xT[:, k, j * P:(j + 1) * P], s13, P, inner_full)
                            if n == 0:
                                places()
                        else:
                            pe.wait_ge(ld_w13[e % RING], 32 * (e // RING + 1))
                            pe.wait_ge(x_taken, n - SH + 1)
                            inner_product(lambda k: fxT[n % 2][:, k, :], w13[e % RING], 128, inner_full)
                    if n > first:
                        last = ITEMS[n - 1][0]
                        pe.wait_ge(hT_ready, n)
                        if n > 1:
                            pe.wait_ge(outer_taken, n - 1)
                        if last is None:
                            outer_product(hhT[(n - 1) % 2], s2, P, outer_full)
                        else:
                            pe.wait_ge(ld_w2e[last % RING], 16 * (last // RING + 1))
                            outer_product(hhT[(n - 1) % 2], w2e[last % RING], 128, outer_full)
                    if n < end:
                        pe.wait_ge(h2_ready, n + 1)
                        turn_h(hh[n % 2], rows, h_turned)
                    if n < NE // 2:
                        list2(2 * n)
                        list2(2 * n + 1)
                    k = n - NE // 2
                    if n < end and 0 <= k < NE:
                        pe.wait_ge(scol_ready, k + 1)
                        take("ranks2", 3, k)
                        spread(3, lambda t: scol[k % 2][:, t:t + 1])

            experts(0, OWN)
            pe.wait_ge(outer_taken, OWN)
            pe.wait_ge(free[3], BEFORE["ranks2"][3] + NE)
            pe.wait_ge(f_more_ready, 1)

            def further_expert(m):
                pe.wait_ge(dve_more2, m * 9 + 6)
                for t in range(T):
                    mm = pe.matmul(slot(3)[:, 0:2], inlist2[0][:, t, 0:128], node_of[:, t, :], start=(t == 0), stop=(t == T - 1))
                mm.then_inc(pe_more2, 1)
                pe.wait_ge(f_more_gathered, m * 16 + 16)
                turn_x(fx[0], pe_more2)
                pe.wait_ge(act_more2, m * 4 + 1)
                pe.wait_ge(f_loaded, m * 48 + 48)
                inner_product(lambda k: fxT[0][:, k, :], w13[NE % RING], 128, pe_more2)
                pe.wait_ge(dve_more2, m * 9 + 9)
                turn_h(hh[0], 128, pe_more2)
                pe.wait_ge(act_more2, m * 4 + 3)
                outer_product(hhT[0], w2e[NE % RING], 128, pe_more2)
                pe.wait_ge(act_more2, m * 4 + 4)
                pe.sem_inc(begun, 1)

            further_tiles(pe, further_expert, f_n, MANY2)
            experts(OWN, len(ITEMS))


_WEIGHTS = [
    "L0_gnn_W1",
    "L0_gnn_a_src1",
    "L0_gnn_a_dst1",
    "L0_gnn_b1",
    "L0_gnn_W2",
    "L0_gnn_a_src2",
    "L0_gnn_a_dst2",
    "L0_gnn_b2",
    "L0_ffn_v_w",
    "L0_ffn_v_b",
    "L0_ffn_gate_w",
    "L0_ffn_gate_b",
    "L0_ffn_w1",
    "L0_ffn_b1",
    "L0_ffn_w2",
    "L0_ffn_b2",
    "L0_ffn_out_w",
    "L0_ffn_out_b",
    "L0_ffn_bk_scale",
    "L1_gnn_W_rel",
    "L1_gnn_W_root",
    "L1_gnn_b_rgcn",
    "L1_gnn_W_gcn",
    "L1_gnn_b_gcn",
    "L1_ffn_Wr",
    "L1_ffn_w1",
    "L1_ffn_w3",
    "L1_ffn_w2",
    "L1_ffn_s1",
    "L1_ffn_s3",
    "L1_ffn_s2",
]


def kernel(**inputs):
    import numpy as _np
    import concourse.bacc as _bacc
    from concourse.bass_utils import run_bass_kernel_spmd as _run

    nc = _bacc.Bacc("TRN2", target_bir_lowering=False, num_devices=1)
    arrays, aps = {}, {}
    for name in ["x", "src", "dst", "edge_type_34"] + _WEIGHTS:
        a = _np.ascontiguousarray(inputs[name])
        if name == "L0_ffn_v_b":
            a = a.reshape(1)
        arrays[f"in_{name}"] = a
        aps[name] = nc.dram_tensor(f"in_{name}", a.shape, mybir.dt.from_np(a.dtype), kind="ExternalInput").ap()
    aps["out"] = nc.dram_tensor("out_0", (N, D), mybir.dt.float32, kind="ExternalOutput").ap()
    build(nc, aps["x"], aps["src"], aps["dst"], aps["edge_type_34"], aps)
    r = _run(nc, [arrays], core_ids=[0])
    return r.results[0]["out_0"]
```
